# Optimizing a Trainium2 kernel written in Bass

```python
import numpy as np
import jax
import jax.numpy as jnp

def _softmax(x, axis=-1):
    return jax.nn.softmax(x, axis=axis)

def _gelu(x):
    return jax.nn.gelu(x, approximate=True)

def _silu(x):
    return jax.nn.silu(x)

def _sigmoid(x):
    return jax.nn.sigmoid(x)

def _layernorm(x, axis=-1, eps=1e-05):
    m = jnp.mean(x, axis=axis, keepdims=True)
    v = jnp.var(x, axis=axis, keepdims=True)
    return (x - m) / jnp.sqrt(v + eps)

def _scatter_add(tgt, idx, src, axis=0):
    return tgt.at[idx].add(src)

def _segment_sum(src, seg, n):
    return jax.ops.segment_sum(src, seg, n)
kernel_name = 'mk_macaron_d2_jaxref_r8_36fe85'

def setup_inputs(seed: int=0):
    np.random.seed(seed)
    _w = jnp.asarray

    def _L0_attn_setup():
        import jax, jax.numpy as jnp
        import numpy as np
        H = 8
        SPARSITY = 0.1
        key = jax.random.key(seed)
        ks = jax.random.split(key, 16)
        B, S, D = (2, 256, 128)
        g2 = H * H
        std = 0.02
        inp = {'x': jax.random.normal(ks[0], (B, S, D), dtype=jnp.float32), 'Wq': jax.random.normal(ks[1], (D, D)) * std, 'bq': jnp.zeros((D,)), 'Wk': jax.random.normal(ks[2], (D, D)) * std, 'bk': jnp.zeros((D,)), 'Wv': jax.random.normal(ks[3], (D, D)) * std, 'bv': jnp.zeros((D,)), 'Wo': jax.random.normal(ks[4], (D, D)) * std, 'bo': jnp.zeros((D,)), 'Wd': jax.random.normal(ks[5], (g2, g2)) * std, 'bd': jnp.zeros((g2,)), 'Wg': jax.random.normal(ks[6], (g2, D)) * std, 'bg': jnp.zeros((g2,)), 'Wgp': jax.random.normal(ks[7], (D, g2)) * std, 'bgp': jnp.zeros((D,))}
        return inp
    _L0_attn_in = _L0_attn_setup()

    def _L0_ffn_setup():
        import jax, jax.numpy as jnp
        import numpy as np
        ALPHA = 1.702
        LIMIT = 9.0
        TOP_K = 2

        def swiglu(x):
            g, v = (x[..., 0::2], x[..., 1::2])
            g = jnp.clip(g, None, LIMIT)
            v = jnp.clip(v, -LIMIT, LIMIT)
            return g * jax.nn.sigmoid(ALPHA * g) * (v + 1)
        key = jax.random.key(seed)
        ks = jax.random.split(key, 6)
        B, L, D = (2, 256, 128)
        E, F = (8, 256)
        s_gate = 1.0 / np.sqrt(D)
        s1 = 1.0 / np.sqrt(D)
        s2 = 1.0 / np.sqrt(F)
        return {'x': jax.random.normal(ks[0], (B, L, D), dtype=jnp.float32), 'gate_w': jax.random.normal(ks[1], (D, E), dtype=jnp.float32) * s_gate, 'dense_1_w': jax.random.normal(ks[2], (E, 2 * F, D), dtype=jnp.float32) * s1, 'dense_1_b': jnp.zeros((E, 2 * F), dtype=jnp.float32), 'dense_2_w': jax.random.normal(ks[3], (E, D, F), dtype=jnp.float32) * s2, 'dense_2_b': jnp.zeros((E, D), dtype=jnp.float32)}
    _L0_ffn_in = _L0_ffn_setup()

    def _L1_attn_setup():
        import jax, jax.numpy as jnp
        import numpy as np
        D_MODEL = 128
        N_HEADS = 16
        D_KEYS = 64
        D_LLM = 128
        LN_EPS = 1e-12
        key = jax.random.key(seed)
        ks = jax.random.split(key, 14)
        B, L, S = (2, 256, 256)
        AH = N_HEADS * D_KEYS
        w = 0.02
        return {'target_embedding': jax.random.normal(ks[0], (B, L, D_MODEL), jnp.float32), 'source_embedding': jax.random.normal(ks[1], (S, D_LLM), jnp.float32), 'value_embedding': jax.random.normal(ks[2], (S, D_LLM), jnp.float32), 'Wq': jax.random.normal(ks[3], (D_MODEL, AH), jnp.float32) * w, 'bq': jnp.zeros((AH,), jnp.float32), 'Wk': jax.random.normal(ks[4], (D_LLM, AH), jnp.float32) * w, 'bk': jnp.zeros((AH,), jnp.float32), 'Wv': jax.random.normal(ks[5], (D_LLM, AH), jnp.float32) * w, 'bv': jnp.zeros((AH,), jnp.float32), 'Wo': jax.random.normal(ks[6], (AH, D_MODEL), jnp.float32) * w, 'bo': jnp.zeros((D_MODEL,), jnp.float32), 'ln_g': jnp.ones((D_MODEL,), jnp.float32), 'ln_b': jnp.zeros((D_MODEL,), jnp.float32)}
    _L1_attn_in = _L1_attn_setup()

    def _L1_ffn_setup():
        import jax, jax.numpy as jnp
        import numpy as np
        B, S, D, H, E, K = (4, 128, 128, 256, 8, 2)
        key = jax.random.key(seed)
        ks = jax.random.split(key, 5)
        s = 0.02
        return {'x': jax.random.normal(ks[0], (B, S, D), jnp.float32), 'W1': jax.random.normal(ks[1], (E, H, D), jnp.float32) * s, 'b1': jnp.zeros((E, H), jnp.float32), 'W2': jax.random.normal(ks[2], (E, D, H), jnp.float32) * s, 'b2': jnp.zeros((E, D), jnp.float32), 'Wg': jax.random.normal(ks[3], (E, D), jnp.float32) * s, 'bg': jnp.zeros((E,), jnp.float32)}
    _L1_ffn_in = _L1_ffn_setup()
    _d = {'L0_attn_x': _L0_attn_in['x'], 'L0_attn_Wq': _L0_attn_in['Wq'], 'L0_attn_bq': _L0_attn_in['bq'], 'L0_attn_Wk': _L0_attn_in['Wk'], 'L0_attn_bk': _L0_attn_in['bk'], 'L0_attn_Wv': _L0_attn_in['Wv'], 'L0_attn_bv': _L0_attn_in['bv'], 'L0_attn_Wo': _L0_attn_in['Wo'], 'L0_attn_bo': _L0_attn_in['bo'], 'L0_attn_Wd': _L0_attn_in['Wd'], 'L0_attn_bd': _L0_attn_in['bd'], 'L0_attn_Wg': _L0_attn_in['Wg'], 'L0_attn_bg': _L0_attn_in['bg'], 'L0_attn_Wgp': _L0_attn_in['Wgp'], 'L0_attn_bgp': _L0_attn_in['bgp'], 'L0_ffn_gate_w': _L0_ffn_in['gate_w'], 'L0_ffn_dense_1_w': _L0_ffn_in['dense_1_w'], 'L0_ffn_dense_1_b': _L0_ffn_in['dense_1_b'], 'L0_ffn_dense_2_w': _L0_ffn_in['dense_2_w'], 'L0_ffn_dense_2_b': _L0_ffn_in['dense_2_b'], 'L1_attn_source_embedding': _L1_attn_in['source_embedding'], 'L1_attn_value_embedding': _L1_attn_in['value_embedding'], 'L1_attn_Wq': _L1_attn_in['Wq'], 'L1_attn_bq': _L1_attn_in['bq'], 'L1_attn_Wk': _L1_attn_in['Wk'], 'L1_attn_bk': _L1_attn_in['bk'], 'L1_attn_Wv': _L1_attn_in['Wv'], 'L1_attn_bv': _L1_attn_in['bv'], 'L1_attn_Wo': _L1_attn_in['Wo'], 'L1_attn_bo': _L1_attn_in['bo'], 'L1_attn_ln_g': _L1_attn_in['ln_g'], 'L1_attn_ln_b': _L1_attn_in['ln_b'], 'L1_ffn_W1': _L1_ffn_in['W1'], 'L1_ffn_b1': _L1_ffn_in['b1'], 'L1_ffn_W2': _L1_ffn_in['W2'], 'L1_ffn_b2': _L1_ffn_in['b2'], 'L1_ffn_Wg': _L1_ffn_in['Wg'], 'L1_ffn_bg': _L1_ffn_in['bg']}
    _x0 = _d['L0_attn_x']
    _d['L0_attn_x'] = jax.random.normal(jax.random.fold_in(jax.random.key(seed), 1), (8, 256, 128), dtype=_x0.dtype)
    del _x0
    return _d

def reference(L0_attn_x, L0_attn_Wq, L0_attn_bq, L0_attn_Wk, L0_attn_bk, L0_attn_Wv, L0_attn_bv, L0_attn_Wo, L0_attn_bo, L0_attn_Wd, L0_attn_bd, L0_attn_Wg, L0_attn_bg, L0_attn_Wgp, L0_attn_bgp, L0_ffn_gate_w, L0_ffn_dense_1_w, L0_ffn_dense_1_b, L0_ffn_dense_2_w, L0_ffn_dense_2_b, L1_attn_source_embedding, L1_attn_value_embedding, L1_attn_Wq, L1_attn_bq, L1_attn_Wk, L1_attn_bk, L1_attn_Wv, L1_attn_bv, L1_attn_Wo, L1_attn_bo, L1_attn_ln_g, L1_attn_ln_b, L1_ffn_W1, L1_ffn_b1, L1_ffn_W2, L1_ffn_b2, L1_ffn_Wg, L1_ffn_bg):

    def _L0_attn_ref(x, Wq, bq, Wk, bk, Wv, bv, Wo, bo, Wd, bd, Wg, bg, Wgp, bgp):
        import jax, jax.numpy as jnp
        import numpy as np
        H = 8
        SPARSITY = 0.1
        B, S, D = x.shape
        Dh = D // H
        scale = Dh ** (-0.5)
        k = max(int(S * SPARSITY), 1)

        def heads(W, b):
            return (x @ W.T + b).reshape(B, S, H, Dh).transpose(0, 2, 1, 3)
        Q, K, V = (heads(Wq, bq), heads(Wk, bk), heads(Wv, bv))
        scores = jnp.einsum('bhqd,bhkd->bhqk', Q, K) * scale
        thr = jax.lax.top_k(scores, k)[0][..., k - 1:k]
        masked = jnp.where(scores >= thr, scores, -jnp.inf)
        probs = jax.nn.softmax(masked, axis=-1)
        attn = jnp.einsum('bhqk,bhkd->bhqd', probs, V)
        attn = attn.transpose(0, 2, 1, 3).reshape(B, S, D)
        g2 = H * H
        distilled = (attn.reshape(-1, g2) @ Wd.T + bd).reshape(B, S, D)
        gate = jax.nn.sigmoid(x.mean(axis=1) @ Wg.T + bg)
        gate = (gate @ Wgp.T + bgp)[:, None, :]
        mixed = gate * distilled + (1.0 - gate) * attn
        return mixed @ Wo.T + bo

    def _L0_ffn_ref(x, gate_w, dense_1_w, dense_1_b, dense_2_w, dense_2_b):
        import jax, jax.numpy as jnp
        import numpy as np
        ALPHA = 1.702
        LIMIT = 9.0
        TOP_K = 2

        def swiglu(x):
            g, v = (x[..., 0::2], x[..., 1::2])
            g = jnp.clip(g, None, LIMIT)
            v = jnp.clip(v, -LIMIT, LIMIT)
            return g * jax.nn.sigmoid(ALPHA * g) * (v + 1)
        B, L, D = x.shape
        xf = x.reshape(B * L, D)
        gate = xf @ gate_w
        weights, sel = jax.lax.top_k(gate, k=TOP_K)
        weights = jax.nn.softmax(weights, axis=-1)
        h = jnp.einsum('ecd,td->tec', dense_1_w, xf) + dense_1_b[None]
        h = swiglu(h)
        y = jnp.einsum('edf,tef->ted', dense_2_w, h) + dense_2_b[None]
        y_sel = jnp.take_along_axis(y, sel[:, :, None], axis=1)
        out = jnp.einsum('tkd,tk->td', y_sel, weights)
        return out.reshape(B, L, D)

    def _L1_attn_ref(target_embedding, source_embedding, value_embedding, Wq, bq, Wk, bk, Wv, bv, Wo, bo, ln_g, ln_b):
        import jax, jax.numpy as jnp
        import numpy as np
        D_MODEL = 128
        N_HEADS = 16
        D_KEYS = 64
        D_LLM = 128
        LN_EPS = 1e-12
        B, L, _ = target_embedding.shape
        S = source_embedding.shape[0]
        H, E = (N_HEADS, D_KEYS)
        q = (target_embedding @ Wq + bq).reshape(B, L, H, E)
        k = (source_embedding @ Wk + bk).reshape(S, H, E)
        v = (value_embedding @ Wv + bv).reshape(S, H, E)
        eq = jax.nn.elu(q)
        ek = jax.nn.elu(k)
        qn = eq / jnp.linalg.norm(eq, axis=-1, keepdims=True)
        kn = ek / jnp.linalg.norm(ek, axis=-1, keepdims=True)
        scores = jnp.einsum('blhe,she->bhls', qn, kn)
        scale = 1.0 / np.sqrt(E).astype(np.float32)
        A = jax.nn.softmax(scale * scores, axis=-1)
        ctx = jnp.einsum('bhls,she->blhe', A, v).reshape(B, L, H * E)
        h = ctx @ Wo + bo
        x = h + target_embedding
        mu = jnp.mean(x, axis=-1, keepdims=True)
        var = jnp.mean(jnp.square(x - mu), axis=-1, keepdims=True)
        return (x - mu) / jnp.sqrt(var + LN_EPS) * ln_g + ln_b

    def _L1_ffn_ref(x, W1, b1, W2, b2, Wg, bg):
        import jax, jax.numpy as jnp
        import numpy as np
        B, S, D, H, E, K = (4, 128, 128, 256, 8, 2)
        b, s, d = x.shape
        xt = x.reshape(-1, d)
        gate_logits = xt @ Wg.T + bg
        w, idx = jax.lax.top_k(gate_logits, K)
        w = jax.nn.softmax(w, axis=1)
        h = jax.nn.relu(jnp.einsum('td,ehd->eth', xt, W1) + b1[:, None, :])
        y = jnp.einsum('eth,eoh->eto', h, W2) + b2[:, None, :]
        comb = (jax.nn.one_hot(idx, E, dtype=xt.dtype) * w[..., None]).sum(axis=1)
        out = jnp.einsum('eto,te->to', y, comb)
        return out.reshape(b, s, d)
    x = L0_attn_x
    x = x + 0.5 * _L0_ffn_ref(_layernorm(x, axis=-1), L0_ffn_gate_w, L0_ffn_dense_1_w, L0_ffn_dense_1_b, L0_ffn_dense_2_w, L0_ffn_dense_2_b)
    x = x + _L0_attn_ref(_layernorm(x, axis=-1), L0_attn_Wq, L0_attn_bq, L0_attn_Wk, L0_attn_bk, L0_attn_Wv, L0_attn_bv, L0_attn_Wo, L0_attn_bo, L0_attn_Wd, L0_attn_bd, L0_attn_Wg, L0_attn_bg, L0_attn_Wgp, L0_attn_bgp)
    x = x + 0.5 * _L0_ffn_ref(_layernorm(x, axis=-1), L0_ffn_gate_w, L0_ffn_dense_1_w, L0_ffn_dense_1_b, L0_ffn_dense_2_w, L0_ffn_dense_2_b)
    x = x + 0.5 * _L1_ffn_ref(_layernorm(x, axis=-1), L1_ffn_W1, L1_ffn_b1, L1_ffn_W2, L1_ffn_b2, L1_ffn_Wg, L1_ffn_bg)
    x = x + _L1_attn_ref(_layernorm(x, axis=-1), L1_attn_source_embedding, L1_attn_value_embedding, L1_attn_Wq, L1_attn_bq, L1_attn_Wk, L1_attn_bk, L1_attn_Wv, L1_attn_bv, L1_attn_Wo, L1_attn_bo, L1_attn_ln_g, L1_attn_ln_b)
    x = x + 0.5 * _L1_ffn_ref(_layernorm(x, axis=-1), L1_ffn_W1, L1_ffn_b1, L1_ffn_W2, L1_ffn_b2, L1_ffn_Wg, L1_ffn_bg)
    return x

_drawn_inputs = setup_inputs


def setup_inputs(seed=0):
    import zlib

    import numpy as np

    out = dict(_drawn_inputs(seed))
    spreads = {'L0_attn_bq': (0.0, 0.385),
     'L0_attn_bk': (0.0, 2.0),
     'L0_attn_bv': (0.0, 0.1),
     'L0_attn_bo': (0.0, 0.1),
     'L0_attn_bd': (0.0, 0.8),
     'L0_attn_bg': (0.0, 0.8),
     'L0_attn_bgp': (0.0, 0.609),
     'L0_ffn_dense_1_b': (0.0, 0.1),
     'L0_ffn_dense_2_b': (0.0, 0.1),
     'L1_attn_bq': (0.0, 2.0),
     'L1_attn_bk': (0.0, 2.0),
     'L1_attn_bv': (0.0, 0.277),
     'L1_attn_bo': (0.0, 0.1),
     'L1_attn_ln_g': (1.0, 0.2),
     'L1_attn_ln_b': (0.0, 0.1),
     'L1_ffn_b1': (0.0, 0.8),
     'L1_ffn_b2': (0.0, 0.1),
     'L1_ffn_bg': (0.0, 0.1)}
    factors = {'L0_attn_Wd': 8.0,
     'L0_attn_Wg': 34.277,
     'L0_attn_Wgp': 5.929,
     'L1_attn_source_embedding': 64.0,
     'L1_attn_value_embedding': 8.0,
     'L1_attn_Wq': 64.0,
     'L1_attn_Wk': 64.0,
     'L1_attn_Wv': 8.0,
     'L1_ffn_W1': 2.848}
    for name, (base, spread) in spreads.items():
        noise = np.random.default_rng([zlib.crc32(name.encode()), seed]).standard_normal(out[name].shape)
        drawn = base * np.exp(spread * noise) if base else spread * noise
        out[name] = jnp.asarray(drawn.astype(out[name].dtype))
    for name, factor in factors.items():
        out[name] = (out[name] * factor).astype(out[name].dtype)
    return out
```

```python
from contextlib import ExitStack

import numpy as np
import concourse.bass as bass
from concourse import mybir

P = 128
F32 = mybir.dt.float32
BF16 = mybir.dt.bfloat16
U32 = mybir.dt.uint32
ALU = mybir.AluOpType
ACT = mybir.ActivationFunctionType

B, S, D = 8, 256, 128
T = B * S
NT = T // P
CT = 4
CN = CT * P
NC = NT // CT
E = 8
PARTS = 3
ALPHA, LIMIT = 1.702, 9.0
LN_EPS, LN_EPS2 = 1e-5, 1e-12
H0, DH0 = 8, 16
TOPK = max(int(S * 0.1), 1)
ROUNDS = -(-TOPK // 8)
H1, DH1 = 16, 64
FB = H1 // 2


def fields(*sizes):
    at, out = 0, {}
    for name, n in sizes:
        out[name] = (at, at + n)
        at += n
    return out, at


PK0, N0 = fields(("ident", P), ("iota", 2 * CT * E), ("m0_gw", E), ("m0_b1", 4 * E), ("m0_gb", 1), ("m0_b2", D))
PK1, N1 = fields(("m0_w1", 4 * E * P), ("m0_w2", 2 * E * D))
PK2, N2 = fields(("a0_wq", 2 * P), ("a0_wk", 2 * P), ("a0_wv", D), ("a0_wd", D), ("a0_wo", D), ("a0_wg", 64),
                 ("a0_wgp", D), ("a0_bq", 2), ("a0_bk", 2), ("a0_bv", D), ("a0_bd", 1), ("a0_bg", 1),
                 ("a0_bgp", 1), ("a0_bo", D), ("ones", P))
PK3, N3 = fields(("m1_gw", E), ("m1_b1", 2 * E), ("m1_gb", 1), ("m1_b2", D), ("m1_w1", 2 * E * P), ("m1_w2", 2 * E * D))
PK4, N4 = fields(("a1_wq", 1024), ("a1_wk", 1024), ("a1_wv", 1024), ("a1_wo", 1024), ("a1_bq", FB), ("a1_bk", FB),
                 ("a1_src", S), ("a1_val", S), ("a1_bv", 1024), ("a1_g", D), ("a1_b", D), ("a1_bo", CN),
                 ("a1_blk", 2))
PKB, NB = fields(("identb", P), ("sel", E * P), ("blkT", FB // 2 * P))


class Chain:

    def __init__(self, eng, sem, base, met):
        self.eng, self.sem, self.base, self.n, self.met = eng, sem, base, 0, met

    def __call__(self, ins):
        self.n += 1
        ins.then_inc(self.sem, 1)
        alone(self.eng, self.sem, self.base + self.n, self.met)


def wait(eng, ev, n):
    if not isinstance(n, int) or n > 0:
        eng.wait_ge(ev, n + 1)


def alone(eng, ev, n, met):
    if isinstance(n, int):
        wait(eng, ev, n)
    else:
        value = eng.to_reg(n + 1)
        eng.wait_ge(met, 1)
        eng.wait_ge(ev, value)


def build(nc, packed, packed_b, x_in, out):
    ctx = ExitStack()
    with ctx:
        def sb(name, cols, dt=F32, rows=P):
            return ctx.enter_context(nc.sbuf_tensor(name, [rows, cols], dt))

        def sem(name):
            return ctx.enter_context(nc.semaphore(name))

        counted = []

        def events(stage, names):
            made = {n: sem(f"{stage}_{n}") for n in names}
            counted.extend(made.values())
            return made

        bank = [ctx.enter_context(nc.psum_tensor(f"bank{i}", [P, CN], F32)) for i in range(8)]
        pk = [sb(f"pk{i}", n) for i, n in enumerate((N0, N1, N2, N3, N4))]
        pkb = sb("pkb", NB, BF16)
        where = {}
        for t, f in zip(pk, (PK0, PK1, PK2, PK3, PK4)):
            where.update({k: (t, a, b) for k, (a, b) in f.items()})
        where.update({k: (pkb, a, b) for k, (a, b) in PKB.items()})

        def cst(name, a=0, b=None, rows=slice(0, P)):
            t, lo, hi = where[name]
            return t[rows, lo + a:hi if b is None else lo + b]

        x = sb("x", T)
        xnT = sb("xnT", T)
        xn = sb("xn", CN)
        stats = sb("stats", CT * 6)
        mv = sb("mv", CT * 2)
        rstd = sb("rstd", 2 * CT)
        mhalf = sb("mhalf", CN)
        combT = sb("combT", T, BF16, PARTS * E)
        lgT = sb("lgT", CN, F32, E)
        small = {n: sb(n, c) for n, c in dict(lg=CT * E, mx=CT * 8, dif=CT, th=CT, idf=2 * CT, pw=2 * CT,
                                              eq=2 * CT * E, comb=CT * E, rest=CT * E).items()}
        midx = sb("midx", CT * 8, U32)
        comb3 = sb("comb3", CT * PARTS * E, BF16)
        sg = sb("sg", 2 * CN)
        vb = sb("vb", 2 * CN)
        s2b = sb("s2b", 2 * CN)
        hb = sb("hb", 4 * CN)
        yT = sb("yT", CN)

        s_ld = [sem(f"s_ld{i}") for i in range(6)]
        s_x0 = [sem(f"s_x0{i}") for i in range(2)]
        s_const = sem("s_const")
        s_setup = sem("s_setup")
        counted.append(s_setup)
        s_out = sem("s_out")

        class Moe:

            def __init__(self, kind, x_ready, sems, before):
                self.x_ready = x_ready
                self.base = before * NC
                self.k = "m0" if kind == "swiglu" else "m1"
                self.glu = kind == "swiglu"
                self.hbanks = 2 if self.glu else 4
                self.lag = 2
                self.ev = sems
                self.hbuf = sems["hb"] if self.glu else sems["s2"]

            PREP_LINKS = 12

            def dve_norm(self, e, c):
                g = self.base + c
                self.x_ready(e, c)
                for t in range(CT):
                    i = e.bn_stats(stats[:, 6 * t:6 * t + 6], x[:, bass.ds(c * CN + t * P, P)])
                i.then_inc(self.ev["st"], 1)
                alone(e, self.ev["st"], g + 1, s_const)
                for t in range(CT):
                    i = e.bn_aggr(mv[:, 2 * t:2 * t + 2], stats[:, 6 * t:6 * t + 6])
                i.then_inc(self.ev["mv"], 1)

            def pool_rstd(self, e, c):
                g = self.base + c
                alone(e, self.ev["mv"], g + 1, s_const)
                e.tensor_scalar(rstd[:, CT:2 * CT], mv[:, 1:2 * CT:2], LN_EPS, None, ALU.add).then_inc(self.ev["ve"], 1)
                wait(e, self.ev["ve"], g + 1)
                e.tensor_tensor(rstd[:, 0:CT], rstd[:, CT:2 * CT], mhalf[:, 0:CT], ALU.pow).then_inc(self.ev["rstd"], 1)

            def dve_xn(self, e, c):
                g = self.base + c
                wait(e, self.ev["rstd"], g + 1)
                wait(e, self.ev["T"], g)
                for t in range(CT):
                    i = e.tensor_scalar(xn[:, t * P:t * P + P], x[:, bass.ds(c * CN + t * P, P)],
                                        mv[:, 2 * t:2 * t + 1], rstd[:, t:t + 1], ALU.subtract, ALU.mult)
                i.then_inc(self.ev["xn"], 1)

            def pe_T(self, e, c):
                g = self.base + c
                wait(e, self.ev["xn"], g + 1)
                for t in range(CT):
                    i = e.transpose(bank[0][:, t * P:t * P + P], xn[:, t * P:t * P + P], cst("ident"))
                i.then_inc(self.ev["T"], 1)

            def act_xnT(self, e, c):
                g = self.base + c
                wait(e, self.ev["T"], g + 1)
                e.activation(xnT[:, bass.ds(c * CN, CN)], bank[0][:, :], ACT.Copy).then_inc(self.ev["xnT"], 1)

            def pe_LT(self, e, c):
                g = self.base + c
                wait(e, self.ev["xnT"], g + 1)
                e.matmul(bank[0][0:E, :], cst(self.k + "_gw"), xnT[:, bass.ds(c * CN, CN)],
                         start=True, stop=True).then_inc(self.ev["LT"], 1)

            def act_lgT(self, e, c):
                g = self.base + c
                wait(e, self.ev["LT"], g + 1)
                bias = cst(self.k + "_gb", rows=slice(0, E))
                e.activation(lgT[:, :], bank[0][0:E, :], ACT.Identity, bias=bias).then_inc(self.ev["lgT"], 1)

            def pe_LG(self, e, c):
                g = self.base + c
                alone(e, self.ev["lgT"], g + 1, s_const)
                for t in range(CT):
                    i = e.transpose(bank[0][:, t * E:t * E + E], lgT[:, t * P:t * P + P],
                                    cst("ident", 0, E, slice(0, E)))
                i.then_inc(self.ev["LG"], 1)

            def dve_top2(self, e, c):
                g = self.base + c
                m = small
                ch = self.ch = Chain(e, self.ev["dv"], g * self.PREP_LINKS, s_const)
                wait(e, self.ev["LG"], g + 1)
                ch(e.tensor_copy(m["lg"][:, :], bank[0][:, 0:CT * E]))
                for t in range(CT):
                    i = e.max(m["mx"][:, 8 * t:8 * t + 8], m["lg"][:, E * t:E * t + E])
                ch(i)
                mx = m["mx"][:, :].rearrange("p (t k) -> p t k", k=8)
                e.tensor_tensor(m["dif"][:, :], mx[:, :, 0], mx[:, :, 1], ALU.subtract).then_inc(self.ev["dif"], 1)
                for t in range(CT):
                    i = e.max_index(midx[:, 8 * t:8 * t + 8], m["mx"][:, 8 * t:8 * t + 8], m["lg"][:, E * t:E * t + E])
                ch(i)

            def act_th(self, e, c):
                g = self.base + c
                wait(e, self.ev["dif"], g + 1)
                e.activation(small["th"][:, :], small["dif"][:, :], ACT.Tanh, scale=0.5).then_inc(self.ev["th"], 1)

            def dve_comb(self, e, c):
                g = self.base + c
                m, ch = small, self.ch
                ids = midx[:, :].rearrange("p (t k) -> p t k", k=8)
                for k in range(2):
                    i = e.tensor_copy(m["idf"][:, k * CT:k * CT + CT], ids[:, :, k])
                ch(i)
                wait(e, self.ev["th"], g + 1)
                e.tensor_scalar(m["pw"][:, 0:CT], m["th"][:, :], 0.5, 0.5, ALU.mult, ALU.add)
                e.tensor_scalar(m["pw"][:, CT:2 * CT], m["th"][:, :], -0.5, 0.5, ALU.mult, ALU.add)

                def bc(a):
                    return a.unsqueeze(2).to_broadcast([P, 2 * CT, E])

                def wide(a):
                    return a.rearrange("p (k e) -> p k e", e=E)
                ch(e.tensor_tensor(wide(m["eq"][:, :]), wide(cst("iota")), bc(m["idf"][:, :]), ALU.is_equal))
                ch(e.tensor_tensor(wide(m["eq"][:, :]), wide(m["eq"][:, :]), bc(m["pw"][:, :]), ALU.mult))
                ch(e.tensor_tensor(m["comb"][:, :], m["eq"][:, 0:CT * E], m["eq"][:, CT * E:], ALU.add))
                part = comb3[:, :].rearrange("p (t k e) -> p t k e", k=PARTS, e=E)
                f = m["comb"][:, :].rearrange("p (t e) -> p t e", e=E)
                r = m["rest"][:, :].rearrange("p (t e) -> p t e", e=E)
                wait(e, self.ev["CT"], g)
                ch(e.tensor_copy(part[:, :, 0, :], f))
                ch(e.tensor_tensor(r, f, part[:, :, 0, :], ALU.subtract))
                ch(e.tensor_copy(part[:, :, 1, :], r))
                ch(e.tensor_tensor(r, r, part[:, :, 1, :], ALU.subtract))
                ch(e.tensor_copy(part[:, :, 2, :], r))
                e.sem_inc(self.ev["c3"], 1)
                assert ch.n == self.PREP_LINKS, ch.n

            def pe_CT(self, e, c):
                g = self.base + c
                wait(e, self.ev["c3"], g + 1)
                to = bank[0][:, :].bitcast(BF16)
                for t in range(CT):
                    i = e.transpose(to[0:PARTS * E, t * P:t * P + P], comb3[:, t * PARTS * E:(t + 1) * PARTS * E],
                                    cst("identb"))
                i.then_inc(self.ev["CT"], 1)

            def act_cT(self, e, c):
                g = self.base + c
                wait(e, self.ev["CT"], g + 1)
                e.activation(combT[:, bass.ds(c * CN, CN)], bank[0][:, :].bitcast(BF16)[0:PARTS * E, 0:CN],
                             ACT.Copy).then_inc(self.ev["cT"], 1)

            HOOKS = dict(
                dve={1: dve_norm, 2: dve_xn, 8: dve_top2, 10: dve_comb},
                pool={0: pool_rstd},
                pe={3: pe_T, 5: pe_LT, 7: pe_LG, 12: pe_CT},
                act={3: act_xnT, 5: act_lgT, 9: act_th, 12: act_cT})

            def hooks(self, which, e, u, c, nxt):
                if nxt is not None and u in self.HOOKS[which]:
                    self.HOOKS[which][u](self, e, nxt)

            def units(self):
                return [(u, u // 2, u % 2) for u in range(2 * E)]

            def pe_chunk(self, e, c, nxt):
                g = self.base + c
                U, NB_ = g * 2 * E, self.hbanks
                xc = xnT[:, bass.ds(c * CN, CN)]
                wait(e, self.ev["cT"], g + 1)
                wait(e, self.ev["ye"], g)

                def second(u):
                    wait(e, self.hbuf, U + u + 1)
                    e.matmul(bank[1][:, :], cst(self.k + "_w2", u * D, u * D + D), hb[:, (u % 4) * CN:(u % 4 + 1) * CN],
                             start=False, stop=u == 2 * E - 1).then_inc(self.ev["y"], 1)

                for u, x_, j in self.units():
                    wait(e, self.ev["s2"] if self.glu else self.ev["sg"], U + max(u - NB_ + 1, 0))
                    if self.glu:
                        for s in range(2):
                            w = (u * 2 + s) * P
                            i = e.matmul(bank[4 + 2 * s + u % 2][:, :], cst("m0_w1", w, w + P), xc, start=True, stop=True)
                    else:
                        i = e.matmul(bank[4 + u % 4][:, :], cst("m1_w1", u * P, u * P + P), xc, start=True, stop=True)
                    i.then_inc(self.ev["h"], 1)
                    if j == 0:
                        alone(e, self.ev["s2"], U + max(u - 2, 0), s_const)
                        e.matmul(bank[2 + x_ % 2][:, :], cst("sel", x_ * P, x_ * P + P, slice(0, PARTS * E)),
                                 combT[:, bass.ds(c * CN, CN)], start=True, stop=True).then_inc(self.ev["cb"], 1)
                    if u == 0:
                        for k in range(PARTS):
                            e.matmul(bank[1][:, :], b2p[self.k][:, k * D:k * D + D], combT[:, bass.ds(c * CN, CN)],
                                     start=k == 0, stop=False)
                    if u >= self.lag:
                        second(u - self.lag)
                    self.hooks("pe", e, u, c, nxt)
                for u in range(2 * E - self.lag, 2 * E):
                    second(u)
                wait(e, self.ev["ye"], g + 1)
                for t in range(CT):
                    i = e.transpose(bank[0][:, t * P:t * P + P], yT[:, t * P:t * P + P], cst("ident"))
                i.then_inc(self.ev["yt"], 1)

            def act_chunk(self, e, c, nxt):
                g = self.base + c
                U = g * 2 * E
                for u, x_, j in self.units():
                    wait(e, self.ev["h"], U + u + 1)
                    wait(e, self.ev["s2"], U + max(u - 1, 0))
                    o = sg[:, (u % 2) * CN:(u % 2 + 1) * CN]
                    if self.glu:
                        e.activation(o, bank[4 + u % 2][:, :], ACT.Silu, bias=b1s[:, u:u + 1], scale=ALPHA).then_inc(self.ev["sg"], 1)
                    else:
                        e.activation(o, bank[4 + u % 4][:, :], ACT.Relu, bias=cst("m1_b1", u, u + 1)).then_inc(self.ev["sg"], 1)
                    self.hooks("act", e, u, c, nxt)
                wait(e, self.ev["y"], U + 2 * E)
                wait(e, self.ev["yt"], g)
                e.activation(yT[:, :], bank[1][:, :], ACT.Copy).then_inc(self.ev["ye"], 1)

            def dve_chunk(self, e, c, nxt):
                g = self.base + c
                U = g * 2 * E

                def last(u):
                    wait(e, self.ev["s2"], U + u + 1)
                    wait(e, self.ev["y"], U + max(u - 3, 0))
                    e.scalar_tensor_tensor(out=hb[:, (u % 4) * CN:(u % 4 + 1) * CN], in0=vb[:, (u % 2) * CN:(u % 2 + 1) * CN],
                                           scalar=1.0 - LIMIT, in1=s2b[:, (u % 2) * CN:(u % 2 + 1) * CN],
                                           op0=ALU.max, op1=ALU.mult).then_inc(self.hbuf, 1)

                for u, x_, j in self.units():
                    self.hooks("dve", e, u, c, nxt)
                    q = slice((u % 2) * CN, (u % 2 + 1) * CN)
                    if self.glu:
                        wait(e, self.hbuf, U + max(u - 1, 0))
                        wait(e, self.ev["h"], U + u + 1)
                        e.tensor_scalar(vb[:, q], bank[6 + u % 2][:, :], b1v[:, u:u + 1], LIMIT + 1.0, ALU.add, ALU.min)
                    wait(e, self.ev["sg"], U + u + 1)
                    if j == 0:
                        wait(e, self.ev["cb"], g * E + x_ + 1)
                    cb = bank[2 + x_ % 2][:, :]
                    if self.glu:
                        e.scalar_tensor_tensor(out=s2b[:, q], in0=sg[:, q], scalar=SILU_MAX, in1=cb,
                                               op0=ALU.min, op1=ALU.mult).then_inc(self.ev["s2"], 1)
                        if u:
                            last(u - 1)
                    else:
                        wait(e, self.ev["y"], U + max(u - 3, 0))
                        e.tensor_tensor(hb[:, (u % 4) * CN:(u % 4 + 1) * CN], sg[:, q], cb, ALU.mult).then_inc(self.ev["s2"], 1)
                if self.glu:
                    last(2 * E - 1)
                wait(e, self.ev["yt"], g + 1)
                e.scalar_tensor_tensor(out=x[:, bass.ds(c * CN, CN)], in0=bank[0][:, :],
                                       scalar=0.5 / ALPHA if self.glu else 0.5, in1=x[:, bass.ds(c * CN, CN)],
                                       op0=ALU.mult, op1=ALU.add).then_inc(self.ev["x"], 1)

            def pool_chunk(self, e, c, nxt):
                self.hooks("pool", e, 0, c, nxt)

            def run(self, which, e):
                for u in sorted(self.HOOKS[which]):
                    self.HOOKS[which][u](self, e, 0)
                chunk = dict(pe=self.pe_chunk, act=self.act_chunk, dve=self.dve_chunk, pool=self.pool_chunk)[which]
                with e.Fori(0, NC - 1) as c:
                    chunk(e, c, c + 1)
                chunk(e, NC - 1, None)


        class Sparse:
            PAIRS = H0 // 2
            STEPS = 2 * PAIRS
            TK = 2 * (2 * ROUNDS - 1)
            SCALE = DH0 ** -0.5

            def __init__(self, name, x_ready):
                self.x_ready = x_ready
                self.ev = events(name, ("st", "mv", "ve", "rstd", "xn", "T", "xT", "q", "qe", "k", "ke", "V", "Ve", "th", "gs", "gp",
                          "gate", "S", "c", "tk", "nm", "e", "mk", "p", "PT", "pT", "PV", "den", "nrm", "aT", "aTe",
                          "ds", "mi", "mx", "o", "x"))

            def dve_norm(self, e, b, p):
                self.x_ready(e, b, p)
                for t in range(2):
                    i = e.bn_stats(stats[:, 6 * t:6 * t + 6], x[:, bass.ds(b * S + t * P, P)])
                i.then_inc(self.ev["st"], 1)
                alone(e, self.ev["st"], b + 1, s_const)
                for t in range(2):
                    i = e.bn_aggr(mv[:, 2 * t:2 * t + 2], stats[:, 6 * t:6 * t + 6])
                i.then_inc(self.ev["mv"], 1)

            def pool_rstd(self, e, b, p):
                alone(e, self.ev["mv"], b + 1, s_const)
                e.tensor_scalar(rstd[:, CT:CT + 2], mv[:, 1:4:2], LN_EPS, None, ALU.add).then_inc(self.ev["ve"], 1)
                wait(e, self.ev["ve"], b + 1)
                e.tensor_tensor(rstd[:, 0:2], rstd[:, CT:CT + 2], mhalf[:, 0:2], ALU.pow).then_inc(self.ev["rstd"], 1)

            def dve_xn(self, e, b, p):
                wait(e, self.ev["rstd"], b + 1)
                wait(e, self.ev["T"], b)
                for t in range(2):
                    i = e.tensor_scalar(xn[:, t * P:t * P + P], x[:, bass.ds(b * S + t * P, P)],
                                        mv[:, 2 * t:2 * t + 1], rstd[:, t:t + 1], ALU.subtract, ALU.mult)
                i.then_inc(self.ev["xn"], 1)

            def pe_T(self, e, b, p):
                wait(e, self.ev["xn"], b + 1)
                wait(e, self.ev["gate"], b)
                for t in range(2):
                    i = e.transpose(bank[0][:, t * P:t * P + P], xn[:, t * P:t * P + P], cst("ident"))
                i.then_inc(self.ev["T"], 1)

            def act_xT(self, e, b, p):
                wait(e, self.ev["T"], b + 1)
                e.activation(axT[:, :], bank[0][:, 0:S], ACT.Copy, accum_out=xsum[:, :]).then_inc(self.ev["xT"], 1)

            def pe_q(self, e, b, p):
                wait(e, self.ev["xT"], b + 1)
                for n in range(2):
                    i = e.matmul(bank[0][:, n * S:n * S + S], cst("a0_wq", n * P, n * P + P), axT[:, :], start=True, stop=True)
                i.then_inc(self.ev["q"], 1)

            def act_qe(self, e, b, p):
                wait(e, self.ev["q"], b + 1)
                for n in range(2):
                    i = e.activation(qT[p][:, n * S:n * S + S], bank[0][:, n * S:n * S + S], ACT.Identity,
                                     bias=cst("a0_bq", n, n + 1))
                i.then_inc(self.ev["qe"], 1)

            def pe_k(self, e, b, p):
                wait(e, self.ev["qe"], b + 1)
                for n in range(2):
                    i = e.matmul(bank[0][:, n * S:n * S + S], cst("a0_wk", n * P, n * P + P), axT[:, :], start=True, stop=True)
                i.then_inc(self.ev["k"], 1)

            def act_ke(self, e, b, p):
                wait(e, self.ev["k"], b + 1)
                for n in range(2):
                    i = e.activation(kT[p][:, n * S:n * S + S], bank[0][:, n * S:n * S + S], ACT.Identity,
                                     bias=cst("a0_bk", n, n + 1))
                i.then_inc(self.ev["ke"], 1)

            def pe_V(self, e, b, p):
                alone(e, self.ev["ke"], b + 1, s_const)
                for t in range(2):
                    e.matmul(bank[0][:, t * P:t * P + P], axT[:, t * P:t * P + P], cst("a0_wv"), start=True, stop=True)
                e.matmul(bank[0][0:64, S:S + 1], cst("a0_wg"), xsum[:, :], start=True, stop=True).then_inc(self.ev["V"], 1)

            def act_th(self, e, b, p):
                wait(e, self.ev["V"], b + 1)
                e.activation(gsm[:, 0:1], bank[0][0:64, S:S + 1], ACT.Tanh, bias=bgh[:, :], scale=0.5 / S).then_inc(self.ev["th"], 1)

            def dve_Ve(self, e, b, p):
                wait(e, self.ev["th"], b + 1)
                wait(e, self.ev["PV"], b * self.STEPS - self.STEPS if not isinstance(b, int) else max(b - 1, 0) * self.STEPS)
                for t in range(2):
                    e.tensor_tensor(V0[p][:, :].rearrange("p (t h d) -> p t h d", t=2, h=H0)[:, t, :, 0:DH0],
                                    bank[0][:, t * P:t * P + P].rearrange("p (h d) -> p h d", h=H0),
                                    cst("a0_bv").rearrange("p (h d) -> p h d", h=H0), ALU.add)
                e.tensor_scalar(gsm[:, 1:2], gsm[:, 0:1], 0.5, 0.5, ALU.mult, ALU.add).then_inc(self.ev["Ve"], 1)

            def pe_gp(self, e, b, p):
                alone(e, self.ev["Ve"], b + 1, s_const)
                e.matmul(bank[0][:, 0:1], cst("a0_wgp", rows=slice(0, 64)), gsm[:, 1:2], start=True, stop=True).then_inc(self.ev["gp"], 1)

            def dve_gate(self, e, b, p):
                wait(e, self.ev["gp"], b + 1)
                g = gate[p]
                e.tensor_scalar(g[:, 0:1], bank[0][:, 0:1], cst("a0_bgp"), None, ALU.add).then_inc(self.ev["gs"], 1)
                wait(e, self.ev["gs"], b + 1)
                e.tensor_scalar(g[:, 1:2], g[:, 0:1], -1.0, 1.0, ALU.mult, ALU.add).then_inc(self.ev["gate"], 1)

            def pe_S(self, e, A, a):
                p, m = a // self.STEPS % 2, a % self.PAIRS
                if a % self.STEPS == 0:
                    wait(e, self.ev["ke"], self.batch(A, a) + 1)
                if not (isinstance(A, int) and A < 2):
                    wait(e, self.ev["c"], A - 1)
                qt = a // self.PAIRS % 2
                for n in range(2):
                    r = slice(32 * m, 32 * m + DH0)
                    i = e.matmul(bank[4 + a % 2][:, n * S:n * S + S], qT[p][r, n * S + qt * P:n * S + qt * P + P],
                                 kT[p][r, n * S:n * S + S], start=True, stop=True)
                i.then_inc(self.ev["S"], 1)

            def act_c(self, e, A, a):
                wait(e, self.ev["S"], A + 1)
                if not (isinstance(A, int) and A < 4):
                    wait(e, self.ev["p"], A - 3)
                e.activation(sS[:, (a % 4) * 2 * S:(a % 4 + 1) * 2 * S], bank[4 + a % 2][:, :], ACT.Copy).then_inc(self.ev["c"], 1)

            def dve_topk(self, e, A, a):
                wait(e, self.ev["c"], A + 1)
                if not (isinstance(A, int) and A < 2):
                    wait(e, self.ev["p"], A - 1)
                ops = []
                for r in range(ROUNDS):
                    for n in range(2):
                        src = sS[:, (a % 4) * 2 * S + n * S:(a % 4) * 2 * S + n * S + S]
                        w = wk[:, n * S:n * S + S]
                        m8 = m8s[:, ((a % 2) * 2 + n) * 8 * ROUNDS + 8 * r:((a % 2) * 2 + n) * 8 * ROUNDS + 8 * r + 8]
                        ops.append(lambda m8=m8, s_=w if r else src: e.max(m8, s_))
                    if r < ROUNDS - 1:
                        for n in range(2):
                            src = sS[:, (a % 4) * 2 * S + n * S:(a % 4) * 2 * S + n * S + S]
                            w = wk[:, n * S:n * S + S]
                            m8 = m8s[:, ((a % 2) * 2 + n) * 8 * ROUNDS + 8 * r:((a % 2) * 2 + n) * 8 * ROUNDS + 8 * r + 8]
                            ops.append(lambda m8=m8, w=w, s_=w if r else src: e.match_replace(w, m8, s_, -3.0e38))
                for n, op in enumerate(ops):
                    if n >= 2:
                        alone(e, self.ev["tk"], A * self.TK + n - 1, s_const)
                    elif not (isinstance(A, int) and A == 0):
                        alone(e, self.ev["tk"], A * self.TK, s_const)
                    op().then_inc(self.ev["tk"], 1)

            def pool_sel(self, e, A, a):
                m = m8s[:, (a % 2) * 16 * ROUNDS:(a % 2 + 1) * 16 * ROUNDS].rearrange("p (n k) -> p n k", n=2)
                alone(e, self.ev["tk"], A * self.TK + 2, s_const)
                if not (isinstance(A, int) and A < 2):
                    alone(e, self.ev["e"], A - 1, s_const)
                e.tensor_scalar(negm[:, (a % 2) * 2:(a % 2) * 2 + 2], m[:, :, 0], -self.SCALE, None, ALU.mult).then_inc(self.ev["nm"], 1)
                alone(e, self.ev["tk"], A * self.TK + self.TK, s_const)
                alone(e, self.ev["p"], A, s_const)
                for n in range(2):
                    i = e.tensor_scalar(msk[:, n * S:n * S + S], sS[:, (a % 4) * 2 * S + n * S:(a % 4) * 2 * S + n * S + S],
                                        m[:, n, TOPK - 1:TOPK], None, ALU.is_ge)
                i.then_inc(self.ev["mk"], 1)
                wait(e, self.ev["mk"], A + 1)
                wait(e, self.ev["e"], A + 1)
                if not (isinstance(A, int) and A < 2):
                    wait(e, self.ev["PT"], A - 1)
                q = slice((a % 2) * 2 * S, (a % 2 + 1) * 2 * S)
                e.tensor_tensor(pS[:, q], msk[:, :], eS[:, q], ALU.mult).then_inc(self.ev["p"], 1)

            def act_e(self, e, A, a):
                wait(e, self.ev["nm"], A + 1)
                if not (isinstance(A, int) and A < 2):
                    wait(e, self.ev["p"], A - 1)
                for n in range(2):
                    i = e.activation(eS[:, ((a % 2) * 2 + n) * S:((a % 2) * 2 + n + 1) * S],
                                     sS[:, (a % 4) * 2 * S + n * S:(a % 4) * 2 * S + n * S + S], ACT.Exp,
                                     bias=negm[:, (a % 2) * 2 + n:(a % 2) * 2 + n + 1], scale=self.SCALE)
                i.then_inc(self.ev["e"], 1)

            def pe_PT(self, e, A, a):
                wait(e, self.ev["p"], A + 1)
                if not (isinstance(A, int) and A < 2):
                    wait(e, self.ev["pT"], A - 1)
                for n in range(4):
                    i = e.transpose(bank[6 + a % 2][:, n * P:n * P + P], pS[:, (a % 2) * 2 * S + n * P:(a % 2) * 2 * S + n * P + P],
                                    cst("ident"))
                i.then_inc(self.ev["PT"], 1)

            def act_pT(self, e, A, a):
                wait(e, self.ev["PT"], A + 1)
                if not (isinstance(A, int) and A < 2):
                    wait(e, self.ev["PV"], A - 1)
                e.activation(pT[:, (a % 2) * 2 * S:(a % 2 + 1) * 2 * S], bank[6 + a % 2][:, :], ACT.Copy).then_inc(self.ev["pT"], 1)

            def pe_PV(self, e, A, a):
                p, g, m = a // self.STEPS % 2, a // self.PAIRS % 2, a % self.PAIRS
                W = DH0 + 1
                if m == 0:
                    if a % self.STEPS == 0:
                        wait(e, self.ev["Ve"], self.batch(A, a) + 1)
                    if not (isinstance(A, int) and A < 2 * self.PAIRS):
                        wait(e, self.ev["nrm"], self.batch(A, a) * 2 + g - 1)
                wait(e, self.ev["pT"], A + 1)
                for n in range(2):
                    h = m + self.PAIRS * n
                    for t in range(2):
                        i = e.matmul(bank[2 + g][:, h * W:h * W + W], pT[:, ((a % 2) * 4 + n * 2 + t) * P:((a % 2) * 4 + n * 2 + t + 1) * P],
                                     V0[p][:, (t * H0 + h) * W:(t * H0 + h + 1) * W], start=t == 0, stop=t == 1)
                i.then_inc(self.ev["PV"], 1)

            def dve_nrm(self, e, b, g):
                W = DH0 + 1
                o = bank[2 + g][:, 0:H0 * W].rearrange("p (h d) -> p h d", h=H0)
                wait(e, self.ev["PV"], b * self.STEPS + (g + 1) * self.PAIRS)
                if not (isinstance(b, int) and b == 0):
                    wait(e, self.ev["aT"], b)
                e.reciprocal(rden[:, :], o[:, :, DH0]).then_inc(self.ev["den"], 1)
                wait(e, self.ev["den"], 2 * b + g + 1)
                e.tensor_tensor(attn[:, g * P:g * P + P].rearrange("p (h d) -> p h d", h=H0), o[:, :, 0:DH0],
                                rden[:, :].unsqueeze(2).to_broadcast([P, H0, DH0]), ALU.mult).then_inc(self.ev["nrm"], 1)

            def pe_aT(self, e, b, p):
                wait(e, self.ev["nrm"], 2 * b + 2)
                wait(e, self.ev["x"], b)
                for t in range(2):
                    i = e.transpose(bank[1][:, t * P:t * P + P], attn[:, t * P:t * P + P], cst("ident"))
                i.then_inc(self.ev["aT"], 1)

            def act_aT(self, e, b, p):
                wait(e, self.ev["aT"], b + 1)
                e.activation(aT[:, :], bank[1][:, 0:S], ACT.Copy).then_inc(self.ev["aTe"], 1)

            def pe_ds(self, e, b, p):
                wait(e, self.ev["aTe"], b + 1)
                e.matmul(bank[1][:, 0:S], cst("a0_wd"), aT[:, :], start=True, stop=True).then_inc(self.ev["ds"], 1)

            def dve_mix(self, e, b, p):
                wait(e, self.ev["ds"], b + 1)
                wait(e, self.ev["o"], b)
                e.tensor_scalar(mixt[:, :], bank[1][:, 0:S], cst("a0_bd"), gate[p][:, 0:1], ALU.add, ALU.mult).then_inc(self.ev["mi"], 1)
                wait(e, self.ev["mi"], b + 1)
                e.scalar_tensor_tensor(out=mix[:, :], in0=aT[:, :], scalar=gate[p][:, 1:2], in1=mixt[:, :],
                                       op0=ALU.mult, op1=ALU.add).then_inc(self.ev["mx"], 1)

            def pe_o(self, e, b, p):
                wait(e, self.ev["mx"], b + 1)
                for t in range(2):
                    e.matmul(bank[1][:, t * P:t * P + P], mix[:, t * P:t * P + P], cst("a0_wo"), start=True, stop=False)
                    i = e.matmul(bank[1][:, t * P:t * P + P], cst("ones", rows=slice(0, 1)), cst("a0_bo", rows=slice(0, 1)),
                                 start=False, stop=True)
                i.then_inc(self.ev["o"], 1)

            def dve_x(self, e, b, p):
                wait(e, self.ev["o"], b + 1)
                xb = x[:, bass.ds(b * S, S)]
                e.tensor_tensor(xb, bank[1][:, 0:S], xb, ALU.add).then_inc(self.ev["x"], 1)

            def batch(self, A, a):
                return A // self.STEPS if isinstance(A, int) else self.b_of(A, a)

            TASKS = dict(
                dve=((0, dve_norm, 1), (1, dve_xn, 1), (5, dve_Ve, 1), (6, dve_gate, 1), (4, dve_mix, -1), (5, dve_x, -1)),
                pool=((0, pool_rstd, 1),),
                pe=((1, pe_T, 1), (2, pe_q, 1), (3, pe_k, 1), (4, pe_V, 1), (5, pe_gp, 1),
                    (2, pe_aT, -1), (3, pe_ds, -1), (4, pe_o, -1)),
                act=((1, act_xT, 1), (2, act_qe, 1), (3, act_ke, 1), (4, act_th, 1), (2, act_aT, -1)))

            def tasks(self, which, e, b, a, first, final):
                r, p = a % self.STEPS, a // self.STEPS % 2
                for at, task, to in self.TASKS[which]:
                    if at == r and not (to > 0 and final) and not (to < 0 and first):
                        task(self, e, b + to, (p + 1) % 2)

            def step(self, which, e, b, a, first=False, final=False):
                r = a % self.STEPS
                A = b * self.STEPS + r
                self.b_of = lambda A_, a_: b + (a_ // self.STEPS - a // self.STEPS)

                def at(n):
                    if first and r + n < 0 or final and r + n >= self.STEPS:
                        return None
                    return A + n, a + n
                def call(f, n):
                    if at(n) is not None:
                        f(e, *at(n))
                if which == "pe":
                    call(self.pe_S, 2)
                    call(self.pe_PT, -1)
                    call(self.pe_PV, -2)
                elif which == "act":
                    call(self.act_e, 0)
                    call(self.act_c, 2)
                    call(self.act_pT, -1)
                elif which == "pool":
                    self.tasks(which, e, b, a, first, final)
                    call(self.pool_sel, 0)
                else:
                    if r == 2 and not first:
                        self.dve_nrm(e, b - 1, 1)
                    if r == 6:
                        self.dve_nrm(e, b, 0)
                    self.tasks(which, e, b, a, first, final)
                    call(self.dve_topk, 0)
                if which in ("pe", "act"):
                    self.tasks(which, e, b, a, first, final)

            def run(self, which, e):
                for _, task, to in sorted(self.TASKS[which], key=lambda t: t[0]):
                    if to > 0:
                        task(self, e, 0, 0)
                for A in range(2):
                    if which == "pe":
                        self.pe_S(e, A, A)
                    if which == "act":
                        self.act_c(e, A, A)
                N_ = self.STEPS
                for r in range(N_):
                    self.step(which, e, 0, r, first=True)
                with e.Fori(0, (B - 2) // 2) as i:
                    for a in range(N_, 3 * N_):
                        self.step(which, e, 2 * i + a // N_, a)
                for r in range(N_):
                    self.step(which, e, B - 1, N_ + r, final=True)
                if which == "pe":
                    A = B * N_
                    self.pe_PT(e, A - 1, 2 * N_ - 1)
                    for n in (2, 1):
                        self.pe_PV(e, A - n, 2 * N_ - n)
                    self.pe_aT(e, B - 1, 1), self.pe_ds(e, B - 1, 1), self.pe_o(e, B - 1, 1)
                elif which == "act":
                    self.act_pT(e, B * N_ - 1, 2 * N_ - 1)
                    self.act_aT(e, B - 1, 1)
                elif which == "dve":
                    self.dve_nrm(e, B - 1, 1), self.dve_mix(e, B - 1, 1), self.dve_x(e, B - 1, 1)

        class Unit:
            def __init__(self, c, g):
                self.c, self.g = c, g
                if c is None:
                    self.n, self.w, self.N, self.src, self.to = g, "k", S, cst("a1_src"), kn
                else:
                    self.n, self.w, self.N = 2 * c + 2 + g, "q", CN
                    self.src, self.to = xnT[:, bass.ds(c * CN, CN)], qn

        def each_block(task, first):
            return [(first + f, task, f) for f in range(FB // 2)]

        def last_step(task):
            return [(6 if f == 0 else 7, task, f) for f in range(FB // 2)]

        class Cross:
            G = FB // 2
            base = 0

            def __init__(self, name, x_ready):
                self.x_ready = x_ready
                self.ev = events(name, ("st", "mv", "ve", "rstd", "xn", "T", "xT", "q", "rr", "mn", "ex", "eq", "sq", "ss", "sse", "ri", "sp", "rT",
                          "rp", "rb", "qn", "S", "e", "PV", "den", "nrm", "cT", "cTe", "O", "z", "z2", "st2", "mv2", "ve2",
                          "rstd2", "x", "V", "Ve", "keep"))

            def dve_norm(self, e, c):
                self.x_ready(e, c)
                for t in range(CT):
                    i = e.bn_stats(stats[:, 6 * t:6 * t + 6], x[:, bass.ds(c * CN + t * P, P)])
                i.then_inc(self.ev["st"], 1)
                alone(e, self.ev["st"], c + 1, s_const)
                for t in range(CT):
                    i = e.bn_aggr(mv[:, 2 * t:2 * t + 2], stats[:, 6 * t:6 * t + 6])
                i.then_inc(self.ev["mv"], 1)

            def pool_rstd(self, e, c):
                alone(e, self.ev["mv"], c + 1, s_const)
                e.tensor_scalar(rstd[:, CT:2 * CT], mv[:, 1:2 * CT:2], LN_EPS, None, ALU.add).then_inc(self.ev["ve"], 1)
                wait(e, self.ev["ve"], c + 1)
                e.tensor_tensor(rstd[:, 0:CT], rstd[:, CT:2 * CT], mhalf[:, 0:CT], ALU.pow).then_inc(self.ev["rstd"], 1)

            def dve_xn(self, e, c):
                wait(e, self.ev["rstd"], c + 1)
                wait(e, self.ev["T"], c)
                wait(e, self.ev["keep"], c)
                for t in range(CT):
                    i = e.tensor_scalar(xn[:, t * P:t * P + P], x[:, bass.ds(c * CN + t * P, P)],
                                        mv[:, 2 * t:2 * t + 1], rstd[:, t:t + 1], ALU.subtract, ALU.mult)
                i.then_inc(self.ev["xn"], 1)

            def pe_T(self, e, c):
                wait(e, self.ev["xn"], c + 1)
                wait(e, self.ev["mn"], self.G * 2 * (c + 1))
                for t in range(CT):
                    i = e.transpose(bank[0][:, t * P:t * P + P], xn[:, t * P:t * P + P], cst("ident"))
                i.then_inc(self.ev["T"], 1)

            def act_xT(self, e, c):
                wait(e, self.ev["T"], c + 1)
                e.activation(xnT[:, bass.ds(c * CN, CN)], bank[0][:, :], ACT.Copy).then_inc(self.ev["xT"], 1)

            def to(self, u, f):
                f += self.G * u.g
                return u.to[:, f * u.N:f * u.N + u.N]

            def pe_q(self, e, u, f):
                if u.w == "q" and u.g == 0 and f == 0:
                    wait(e, self.ev["xT"], u.c + 1)
                wait(e, self.ev["mn"], self.G * u.n + f)
                if f == 0:
                    wait(e, self.ev["qn"], self.G * u.n)
                f += self.G * u.g
                e.matmul(bank[0][:, 0:u.N], cst("a1_w" + u.w, f * P, f * P + P), u.src, start=True, stop=True).then_inc(self.ev["q"], 1)

            def act_relu(self, e, u, f):
                F = f + self.G * u.g
                wait(e, self.ev["q"], self.G * u.n + f + 1)
                wait(e, self.ev["eq"], self.G * u.n + max(f - 1, 0))
                e.activation(rrb[:, (f % 2) * CN:(f % 2) * CN + u.N], bank[0][:, 0:u.N], ACT.Relu,
                             bias=cst("a1_b" + u.w, F, F + 1)).then_inc(self.ev["rr"], 1)

            def dve_min(self, e, u, f):
                F = f + self.G * u.g
                wait(e, self.ev["rr"], self.G * u.n + f + 1)
                wait(e, self.ev["eq"], self.G * u.n + max(f - 1, 0))
                e.tensor_scalar(exb[:, (f % 2) * CN:(f % 2) * CN + u.N], bank[0][:, 0:u.N], cst("a1_b" + u.w, F, F + 1),
                                0.0, ALU.add, ALU.min).then_inc(self.ev["mn"], 1)

            def act_ex(self, e, u, f):
                wait(e, self.ev["mn"], self.G * u.n + f + 1)
                b = slice((f % 2) * CN, (f % 2) * CN + u.N)
                e.activation(exb[:, b], exb[:, b], ACT.Exp).then_inc(self.ev["ex"], 1)

            def dve_elu(self, e, u, f):
                b = slice((f % 2) * CN, (f % 2) * CN + u.N)
                if u.w == "q" and f == 0:
                    v = 2 * H1 * u.c - H1 + H1 * u.g
                    wait(e, self.ev["S"], max(v, 0) if isinstance(v, int) else v)
                wait(e, self.ev["ex"], self.G * u.n + f + 1)
                e.scalar_tensor_tensor(out=self.to(u, f), in0=exb[:, b], scalar=-1.0, in1=rrb[:, b],
                                       op0=ALU.add, op1=ALU.add).then_inc(self.ev["eq"], 1)

            def act_sq(self, e, u, f):
                wait(e, self.ev["eq"], self.G * u.n + f + 1)
                wait(e, self.ev["ss"], self.G * u.n + max(f - 1, 0))
                e.activation(sqb[:, (f % 2) * CN:(f % 2) * CN + u.N], self.to(u, f), ACT.Square).then_inc(self.ev["sq"], 1)

            def pe_ss(self, e, u, f):
                wait(e, self.ev["sq"], self.G * u.n + f + 1)
                for t in range(u.N // P):
                    q = (f % 2) * CN + t * P
                    i = e.matmul(bank[1][:, t * FB + 2 * f:t * FB + 2 * f + 2], sqb[:, q:q + P], cst("a1_blk"), start=True, stop=True)
                i.then_inc(self.ev["ss"], 1)

            def act_sse(self, e, u):
                wait(e, self.ev["ss"], self.G * u.n + self.G)
                wait(e, self.ev["ri"], u.n)
                e.activation(ssb[:, 0:u.N // P * FB], bank[1][:, 0:u.N // P * FB], ACT.Copy).then_inc(self.ev["sse"], 1)

            def pool_ri(self, e, u):
                n = u.N // P * FB
                wait(e, self.ev["sse"], u.n + 1)
                wait(e, self.ev["sp"], u.n * 5)
                e.tensor_tensor(rib[:, 0:n], ssb[:, 0:n], mhalf[:, 0:n], ALU.pow).then_inc(self.ev["ri"], 1)

            def dve_split(self, e, u):
                ch = Chain(e, self.ev["sp"], u.n * 5, s_const)
                n = u.N // P
                part = rp3[:, 0:n * PARTS * FB].rearrange("p (t k h) -> p t k h", k=PARTS, h=FB)
                r = rib[:, 0:n * FB].rearrange("p (t h) -> p t h", h=FB)
                wait(e, self.ev["ri"], u.n + 1)
                wait(e, self.ev["rT"], u.n)
                for k in range(PARTS):
                    ch(e.tensor_copy(part[:, :, k, :], r))
                    if k < PARTS - 1:
                        ch(e.tensor_tensor(r, r, part[:, :, k, :], ALU.subtract))

            def pe_rT(self, e, u):
                wait(e, self.ev["sp"], u.n * 5 + 5)
                to = bank[1][:, :].bitcast(BF16)
                for t in range(u.N // P):
                    i = e.transpose(to[0:PARTS * FB, t * P:t * P + P], rp3[:, t * PARTS * FB:(t + 1) * PARTS * FB], cst("identb"))
                i.then_inc(self.ev["rT"], 1)

            def act_rT(self, e, u):
                wait(e, self.ev["rT"], u.n + 1)
                wait(e, self.ev["rb"], self.G * u.n)
                e.activation(rp[:, 0:u.N], bank[1][:, :].bitcast(BF16)[0:PARTS * FB, 0:u.N], ACT.Copy).then_inc(self.ev["rp"], 1)

            def pe_rb(self, e, u, f):
                wait(e, self.ev["rp"], u.n + 1)
                wait(e, self.ev["qn"], self.G * u.n + max(f - 1, 0))
                if f == 0 and u.g == 1 and u.w == "q" and not isinstance(u.c, int):
                    wait(e, self.ev["xT"], u.c + 2)
                e.matmul(bank[f % 2][:, 0:u.N], cst("blkT", f * P, f * P + P, slice(0, PARTS * FB)), rp[:, 0:u.N],
                         start=True, stop=True).then_inc(self.ev["rb"], 1)

            def dve_qn(self, e, u, f):
                wait(e, self.ev["rb"], self.G * u.n + f + 1)
                e.tensor_tensor(self.to(u, f), bank[f % 2][:, 0:u.N], self.to(u, f), ALU.mult).then_inc(self.ev["qn"], 1)

            def pe_V(self, e, t, half):
                n = 2 * t + half
                wait(e, self.ev["Ve"], max(n - 1, 0))
                e.matmul(bank[2 + n % 2][:, :], cst("a1_val", t * P, t * P + P), cst("a1_wv", half * CN, half * CN + CN),
                         start=True, stop=True).then_inc(self.ev["V"], 1)

            def dve_V(self, e, t, half):
                n = 2 * t + half
                wait(e, self.ev["V"], n + 1)
                v = V1[:, :].rearrange("p (t h d) -> p t h d", t=2, h=H1)[:, t, 8 * half:8 * half + 8, 0:DH1]
                e.tensor_tensor(v, bank[2 + n % 2][:, :].rearrange("p (h d) -> p h d", d=DH1),
                                cst("a1_bv", half * CN, half * CN + CN).rearrange("p (h d) -> p h d", d=DH1),
                                ALU.add).then_inc(self.ev["Ve"], 1)

            def pe_S(self, e, c, h):
                r, f = slice(64 * (h % 2), 64 * (h % 2) + 64), h // 2
                if h % 2 == 0:
                    wait(e, self.ev["qn"], FB * (c + 1) + f + 1)
                for t in range(2):
                    wait(e, self.ev["e"], 2 * (c * H1 + h) + t - 1 if h else 2 * c * H1)
                    e.matmul(bank[2 + t][:, :], kn[r, f * S + t * P:f * S + t * P + P], qn[r, f * CN:f * CN + CN],
                             start=True, stop=True).then_inc(self.ev["S"], 1)

            def act_e(self, e, c, h):
                for t in range(2):
                    wait(e, self.ev["S"], 2 * (c * H1 + h) + t + 1)
                    wait(e, self.ev["PV"], c * H1 + max(h - 1, 0))
                    e.activation(AT[:, ((h % 2) * 2 + t) * CN:((h % 2) * 2 + t + 1) * CN], bank[2 + t][:, :], ACT.Exp,
                                 scale=DH1 ** -0.5).then_inc(self.ev["e"], 1)

            def pe_PV(self, e, c, h):
                W = DH1 + 1
                wait(e, self.ev["nrm"], c * H1 + max(h - 1, 0))
                if h == 0:
                    wait(e, self.ev["Ve"], 4)
                wait(e, self.ev["e"], 2 * (c * H1 + h) + 2)
                for q in range(CT):
                    for t in range(2):
                        a = ((h % 2) * 2 + t) * CN + q * P
                        i = e.matmul(bank[4 + h % 2][:, q * W:q * W + W], AT[:, a:a + P], V1[:, (t * H1 + h) * W:(t * H1 + h + 1) * W],
                                     start=t == 0, stop=t == 1)
                i.then_inc(self.ev["PV"], 1)

            def dve_nrm(self, e, c, h):
                o = bank[4 + h % 2][:, 0:CT * (DH1 + 1)].rearrange("p (q d) -> p q d", q=CT)
                wait(e, self.ev["PV"], c * H1 + h + 1)
                e.reciprocal(rden1[:, (h % 2) * CT:(h % 2 + 1) * CT], o[:, :, DH1]).then_inc(self.ev["den"], 1)
                wait(e, self.ev["den"], c * H1 + h + 1)
                wait(e, self.ev["cT"], FB * c + max(h // 2 - 1, 0))
                e.tensor_tensor(ctxb[:, (h // 2 % 2) * CN:(h // 2 % 2 + 1) * CN].rearrange("p (q n d) -> p q n d", q=CT, n=2)[:, :, h % 2, :],
                                o[:, :, 0:DH1], rden1[:, (h % 2) * CT:(h % 2 + 1) * CT].unsqueeze(2).to_broadcast([P, CT, DH1]),
                                ALU.mult).then_inc(self.ev["nrm"], 1)

            def pe_cT(self, e, c, f):
                wait(e, self.ev["nrm"], c * H1 + 2 * f + 2)
                wait(e, self.ev["cTe"], FB * c + f)
                for q in range(CT):
                    i = e.transpose(bank[6][:, q * P:q * P + P], ctxb[:, (f % 2) * CN + q * P:(f % 2) * CN + q * P + P], cst("ident"))
                i.then_inc(self.ev["cT"], 1)

            def act_cT(self, e, c, f):
                wait(e, self.ev["cT"], FB * c + f + 1)
                wait(e, self.ev["O"], FB * c + max(f - 1, 0))
                e.activation(ctxT[:, (f % 2) * CN:(f % 2 + 1) * CN], bank[6][:, :], ACT.Copy).then_inc(self.ev["cTe"], 1)

            def pe_O(self, e, c, f):
                if f == 0:
                    wait(e, self.ev["z"], c)
                    e.matmul(bank[7][:, :], cst("ones", rows=slice(0, 1)), cst("a1_bo", rows=slice(0, 1)), start=True, stop=False)
                wait(e, self.ev["cTe"], FB * c + f + 1)
                for q in range(CT):
                    i = e.matmul(bank[7][:, q * P:q * P + P], ctxT[:, (f % 2) * CN + q * P:(f % 2) * CN + q * P + P],
                                 cst("a1_wo", f * P, f * P + P), start=False, stop=f == FB - 1 and q == CT - 1)
                i.then_inc(self.ev["O"], 1)

            def dve_tail(self, e, c):
                wait(e, self.ev["O"], FB * c + FB)
                zz = z[:, :].rearrange("p (q d) -> p q d", q=CT)

                def row(name):
                    return cst(name).unsqueeze(1).to_broadcast([P, CT, D])
                wait(e, self.ev["keep"], c + 1)
                e.tensor_tensor(z[:, :], bank[7][:, :], tkeep[:, :], ALU.add).then_inc(self.ev["z"], 1)
                alone(e, self.ev["z"], c + 1, s_const)
                for t in range(CT):
                    i = e.bn_stats(stats2[:, 6 * t:6 * t + 6], z[:, t * P:t * P + P])
                i.then_inc(self.ev["st2"], 1)
                alone(e, self.ev["st2"], c + 1, s_const)
                for t in range(CT):
                    i = e.bn_aggr(mv2[:, 2 * t:2 * t + 2], stats2[:, 6 * t:6 * t + 6])
                i.then_inc(self.ev["mv2"], 1)
                ch = Chain(e, self.ev["z2"], c * 4, s_const)
                wait(e, self.ev["rstd2"], c + 1)
                for t in range(CT):
                    i = e.tensor_scalar(z[:, t * P:t * P + P], z[:, t * P:t * P + P], mv2[:, 2 * t:2 * t + 1], rstd2[:, t:t + 1],
                                        ALU.subtract, ALU.mult)
                ch(i)
                ch(e.tensor_tensor(zz, zz, row("a1_g"), ALU.mult))
                ch(e.tensor_tensor(zz, zz, row("a1_b"), ALU.add))
                xc = x[:, bass.ds(c * CN, CN)]
                ch(e.tensor_tensor(xc, xc, z[:, :], ALU.add))
                e.sem_inc(self.ev["x"], 1)

            def pool_keep(self, e, c):
                alone(e, self.ev["xn"], c + 1, s_const)
                alone(e, self.ev["z"], c, s_const)
                e.tensor_copy(tkeep[:, :], xn[:, :]).then_inc(self.ev["keep"], 1)

            def pool_tail(self, e, c):
                alone(e, self.ev["mv2"], c + 1, s_const)
                e.tensor_scalar(rstd2[:, CT:2 * CT], mv2[:, 1:2 * CT:2], LN_EPS2, None, ALU.add).then_inc(self.ev["ve2"], 1)
                wait(e, self.ev["ve2"], c + 1)
                e.tensor_tensor(rstd2[:, 0:CT], rstd2[:, CT:2 * CT], mhalf[:, 0:CT], ALU.pow).then_inc(self.ev["rstd2"], 1)

            UNIT = dict(
                pe=each_block(pe_q, 0) + each_block(pe_ss, 1) + [(5, pe_rT)] + last_step(pe_rb),
                act=each_block(act_relu, 0) + each_block(act_ex, 0) + each_block(act_sq, 0) + [(4, act_sse), (5, act_rT)],
                dve=each_block(dve_min, 0) + each_block(dve_elu, 0) + [(5, dve_split)] + last_step(dve_qn),
                pool=[(4, pool_ri)])
            NORM = dict(pe=[(5, pe_T)], act=[(5, act_xT)], dve=[(0, dve_norm), (1, dve_xn)], pool=[(0, pool_rstd)])

            def unit(self, which, e, u, k):
                for at, task, *f in self.UNIT[which]:
                    if at == k:
                        task(self, e, u, *f)

            def norm(self, which, e, c, k):
                for at, task in self.NORM[which]:
                    if at == k:
                        task(self, e, c)

            def chunk(self, which, e, c, nxt):
                if which == "pool":
                    self.pool_keep(e, c)
                for h in range(H1):
                    if which == "pe":
                        if h == 0:
                            self.pe_S(e, c, 0)
                        if h + 1 < H1:
                            self.pe_S(e, c, h + 1)
                        self.pe_PV(e, c, h)
                        if h % 2 and h > 1:
                            self.pe_O(e, c, h // 2 - 1)
                        if h % 2 == 0 and h > 1:
                            self.pe_cT(e, c, h // 2 - 1)
                    elif which == "act":
                        self.act_e(e, c, h)
                        if h % 2 == 0 and h > 1:
                            self.act_cT(e, c, h // 2 - 1)
                    s_, k = h // 8, h % 8
                    if s_ == 0 and nxt is not None:
                        self.norm(which, e, nxt, k)
                    if s_ == 0 or nxt is not None:
                        self.unit(which, e, Unit(nxt if s_ else c, 1 - s_), k)
                    if which == "dve":
                        self.dve_nrm(e, c, h)
                if which == "pe":
                    self.pe_cT(e, c, FB - 1)
                    self.pe_O(e, c, FB - 1)
                elif which == "act":
                    self.act_cT(e, c, FB - 1)
                elif which == "dve":
                    self.dve_tail(e, c)
                else:
                    self.pool_tail(e, c)

            def run(self, which, e):
                self.x_ready(e, NC - 1)
                for g in range(2):
                    for k in range(8):
                        self.unit(which, e, Unit(None, g), k)
                for t in range(2):
                    for half in range(2):
                        if which == "pe":
                            self.pe_V(e, t, half)
                        elif which == "dve":
                            self.dve_V(e, t, half)
                for k in range(8):
                    self.norm(which, e, 0, k)
                for k in range(8):
                    self.unit(which, e, Unit(0, 0), k)
                with e.Fori(0, NC - 1) as c:
                    self.chunk(which, e, c, c + 1)
                self.chunk(which, e, NC - 1, None)

        kn = sb("kn", FB * S)
        qn = sb("qn", FB * CN)
        exb, rrb, sqb = sg, vb, s2b
        ssb = sb("ssb", CT * FB)
        rib = sb("rib", CT * FB)
        rp3 = sb("rp3", CT * PARTS * FB, BF16)
        rp = sb("rp", CN, BF16, PARTS * FB)
        V1 = sb("V1", 2 * H1 * (DH1 + 1))
        AT = hb
        rden1 = sb("rden1", 2 * CT)
        sS = sb("sS", 4 * 2 * S)
        ctxb, ctxT = sS[:, 0:2 * CN], sS[:, 2 * CN:4 * CN]
        tkeep = sb("tkeep", CN)
        z = yT
        stats2 = sb("stats2", CT * 6)
        mv2 = sb("mv2", CT * 2)
        rstd2 = sb("rstd2", 2 * CT)

        axT = sb("axT", S)
        xsum = sb("xsum", 1)
        qT = [sb(f"qT{n}", 2 * S) for n in range(2)]
        kT = [sb(f"kT{n}", 2 * S) for n in range(2)]
        V0 = [sb(f"V0{n}", 2 * H0 * (DH0 + 1)) for n in range(2)]
        gsm = sb("gsm", 2, F32, 64)
        bgh = sb("bgh", 1, F32, 64)
        gate = [sb(f"gate{n}", 2) for n in range(2)]
        wk, msk = sg[:, 0:2 * S], vb[:, 0:2 * S]
        m8s = sb("m8s", 4 * 8 * ROUNDS)
        negm = sb("negm", 4)
        eS, pS, pT = hb[:, 0:4 * S], hb[:, 4 * S:8 * S], qn[:, 0:4 * S]
        rden = sb("rden", H0)
        attn, aT, mixt, mix = (s2b[:, n * S:n * S + S] for n in range(4))

        SILU_MAX = float(ALPHA * LIMIT / (1.0 + np.exp(-ALPHA * LIMIT)))
        b1s = sb("b1s", 2 * E)
        b1v = sb("b1v", 2 * E)
        b2p = {k: sb("b2p_" + k, PARTS * D, BF16, PARTS * E) for k in ("m0", "m1")}
        b2r = sb("b2r", D)

        def setup_dve(e):
            ch = Chain(e, s_setup, 0, s_const)
            e.memset(mhalf[:, :], -0.5).then_inc(s_const, 1)
            e.wait_ge(s_ld[0], 16)
            e.wait_ge(s_ld[3], 16)
            b1 = cst("m0_b1").rearrange("p (u s) -> p u s", s=2)
            e.tensor_scalar(b1s[:, :], b1[:, :, 0], ALPHA, None, ALU.mult)
            ch(e.tensor_scalar(b1v[:, :], b1[:, :, 1], 1.0, None, ALU.add))
            r = slice(0, PARTS * E)
            for k, f in (("m0", ALPHA), ("m1", 1.0)):
                p = b2p[k]
                ch(e.tensor_scalar(b2r[r, :], cst(k + "_b2", rows=r), f, None, ALU.mult))
                for n in range(PARTS):
                    ch(e.tensor_copy(p[:, n * D:n * D + D], b2r[r, :]))
                    if n < PARTS - 1:
                        ch(e.tensor_tensor(b2r[r, :], b2r[r, :], p[:, n * D:n * D + D], ALU.subtract))
            e.wait_ge(s_ld[2], 16)
            for v in V0:
                e.memset(v[:, DH0::DH0 + 1], 1.0)
            ch(e.tensor_scalar(bgh[:, :], cst("a0_bg", rows=slice(0, 64)), 0.5, None, ALU.mult))
            e.wait_ge(s_ld[4], 16)
            e.memset(V1[:, DH1::DH1 + 1], 1.0)
            e.sem_inc(s_const, 1)

        def after(stage):
            return lambda e, c: wait(e, stage.ev["x"], stage.base + c + 1)

        ms = events("moe", ("st", "mv", "ve", "rstd", "xn", "T", "xnT", "LT", "lgT", "LG", "dif", "th", "c3",
                                           "CT", "cT", "h", "cb", "sg", "s2", "hb", "y", "ye", "yt", "x", "dv"))

        m0a = Moe("swiglu", lambda e, c: e.wait_ge(s_x0[int(not isinstance(c, int) or c > 0)], 16), ms, 0)
        a0 = Sparse("a0", lambda e, b, p: wait(e, m0a.ev["x"], NC))
        m0b = Moe("swiglu", lambda e, c: wait(e, a0.ev["x"], B), ms, 1)
        m1a = Moe("relu", after(m0b), ms, 2)
        a1 = Cross("a1", after(m1a))
        m1b = Moe("relu", after(a1), ms, 3)
        stages = [m0a, a0, m0b, m1a, a1, m1b]
        last = stages[-1]

        block = ctx.enter_context(nc.Block())
        xv = x_in.rearrange("b (t p) d -> p (b t) d", p=P)

        @block.sync
        def _(e):
            e.dma_start(pk[0][:, :], packed[0]).then_inc(s_ld[0], 16)
            for v in counted:
                e.sem_inc(v, 1)
            for n, (a, b) in enumerate(((0, CT), (CT, NT))):
                e.dma_start(x[:, a * D:b * D].rearrange("p (t d) -> p t d", d=D), xv[:, a:b, :]).then_inc(s_x0[n], 16)
            wait(e, last.ev["x"], B if last is a0 else last.base + NC)
            e.dma_start(out.rearrange("b (t p) d -> p (b t) d", p=P), x[:, :].rearrange("p (t d) -> p t d", d=D)).then_inc(s_out, 16)
            e.wait_ge(s_out, 16)

        @block.gpsimd
        def _(e):
            for n in (3, 2, 4):
                e.dma_start(pk[n][:, :], packed[n]).then_inc(s_ld[n], 16)
            e.wait_ge(s_const, 1)
            for s in stages:
                s.run("pool", e)

        @block.scalar
        def _(e):
            e.dma_start(pkb[:, :], packed_b).then_inc(s_ld[5], 16)
            e.dma_start(pk[1][:, :], packed[1]).then_inc(s_ld[1], 16)
            e.wait_ge(s_const, 2)
            for s in stages:
                s.run("act", e)

        @block.vector
        def _(e):
            setup_dve(e)
            for s in stages:
                s.run("dve", e)

        @block.tensor
        def _(e):
            e.wait_ge(s_ld[0], 16)
            e.wait_ge(s_ld[5], 16)
            for n in range(1, 5):
                e.wait_ge(s_ld[n], 16)
            e.wait_ge(s_const, 2)
            for s in stages:
                s.run("pe", e)


def pack(names, n, parts):
    a = np.zeros((P, n), np.float32)
    for k, (lo, hi) in names.items():
        v = parts[k]
        a[:v.shape[0], lo:hi] = v.reshape(v.shape[0], hi - lo)
    return a


def kernel(**inputs):
    import ml_dtypes
    import concourse.bacc as bacc
    from concourse.bass_utils import run_bass_kernel_spmd as run

    i = {k: np.asarray(v) for k, v in inputs.items()}
    a0, f0, a1, f1 = "L0_attn_", "L0_ffn_", "L1_attn_", "L1_ffn_"

    def rows(v):
        return np.broadcast_to(v.reshape(1, -1), (P, v.size))

    def cols(v, n=P):
        return v.reshape(-1, n).T

    def heads(w):
        o = np.zeros((w.shape[1], 8, 32), np.float32)
        o[:, :, :DH0] = w.T.reshape(w.shape[1], 8, DH0)
        return o

    iota = np.broadcast_to(np.arange(E, dtype=np.float32), (P, 2 * CT, E))
    w1 = i[f0 + "dense_1_w"].reshape(E, 2, P, 2, D)
    wd = np.zeros((2, 64, 2, 64), np.float32)
    wd[0, :, 0], wd[1, :, 1] = i[a0 + "Wd"].T, i[a0 + "Wd"].T
    blk = np.zeros((2, 64, 2), np.float32)
    blk[0, :, 0] = blk[1, :, 1] = 1
    parts = {
        "ident": np.eye(P, dtype=np.float32), "iota": iota,
        "m0_gw": i[f0 + "gate_w"], "m0_gb": np.zeros((E, 1), np.float32),
        "m0_b1": i[f0 + "dense_1_b"].reshape(E, 2, P, 2).transpose(2, 0, 1, 3),
        "m0_b2": np.concatenate([i[f0 + "dense_2_b"]] * PARTS),
        "m0_w1": w1.transpose(4, 0, 1, 3, 2),
        "m0_w2": i[f0 + "dense_2_w"].reshape(E, D, 2, P).transpose(3, 0, 2, 1),
        "a0_wq": heads(i[a0 + "Wq"]), "a0_wk": heads(i[a0 + "Wk"]),
        "a0_wv": i[a0 + "Wv"].T, "a0_wd": wd.reshape(P, P), "a0_wo": i[a0 + "Wo"].T,
        "a0_wg": i[a0 + "Wg"].T, "a0_wgp": i[a0 + "Wgp"].T,
        "a0_bq": heads(i[a0 + "bq"].reshape(-1, 1)).reshape(2, P).T, "a0_bk": heads(i[a0 + "bk"].reshape(-1, 1)).reshape(2, P).T,
        "a0_bv": rows(i[a0 + "bv"]), "a0_bd": np.concatenate([i[a0 + "bd"]] * 2).reshape(P, 1),
        "a0_bg": i[a0 + "bg"].reshape(64, 1), "a0_bgp": i[a0 + "bgp"].reshape(P, 1),
        "a0_bo": rows(i[a0 + "bo"]), "ones": np.ones((P, P), np.float32),
        "m1_gw": i[f1 + "Wg"].T, "m1_gb": i[f1 + "bg"].reshape(E, 1),
        "m1_b1": cols(i[f1 + "b1"]), "m1_b2": np.concatenate([i[f1 + "b2"]] * PARTS),
        "m1_w1": i[f1 + "W1"].transpose(2, 0, 1),
        "m1_w2": i[f1 + "W2"].reshape(E, D, 2, P).transpose(3, 0, 2, 1),
        "a1_wq": i[a1 + "Wq"], "a1_wk": i[a1 + "Wk"], "a1_wv": i[a1 + "Wv"],
        "a1_wo": i[a1 + "Wo"].reshape(FB, P, D).transpose(1, 0, 2),
        "a1_bq": cols(i[a1 + "bq"]), "a1_bk": cols(i[a1 + "bk"]),
        "a1_src": i[a1 + "source_embedding"].T, "a1_val": i[a1 + "value_embedding"].T,
        "a1_bv": rows(i[a1 + "bv"]), "a1_g": rows(i[a1 + "ln_g"]), "a1_b": rows(i[a1 + "ln_b"]),
        "a1_bo": rows(np.concatenate([i[a1 + "bo"]] * CT)), "a1_blk": blk.reshape(P, -1),
    }
    sel = np.zeros((PARTS, E, E, P), np.float32)
    for e_ in range(E):
        sel[:, e_, e_] = 1
    blkT = np.zeros((PARTS, FB, FB // 2, 2, 64), np.float32)
    for h in range(FB):
        blkT[:, h, h // 2, h % 2] = 1
    parts |= {"identb": parts["ident"], "sel": sel.reshape(PARTS * E, -1), "blkT": blkT.reshape(PARTS * FB, -1)}

    nc = bacc.Bacc("TRN2", target_bir_lowering=False, num_devices=1)
    arrays = {}

    def arg(name, a):
        arrays[name] = np.ascontiguousarray(a)
        return nc.dram_tensor(name, a.shape, mybir.dt.from_np(a.dtype), kind="ExternalInput").ap()

    packed = [arg(f"packed{n}", pack(names, size, parts))
              for n, (names, size) in enumerate(((PK0, N0), (PK1, N1), (PK2, N2), (PK3, N3), (PK4, N4)))]
    packed_b = arg("packed_b", pack(PKB, NB, parts).astype(ml_dtypes.bfloat16))
    x_in = arg("x_in", i[a0 + "x"])
    out = nc.dram_tensor("out", (B, S, D), F32, kind="ExternalOutput").ap()
    build(nc, packed, packed_b, x_in, out)
    r = run(nc, [arrays], core_ids=[0])
    return r.results[0]["out"]
```

```python
from contextlib import ExitStack

import numpy as np
import concourse.bass as bass
from concourse import mybir

P = 128
F32 = mybir.dt.float32
BF16 = mybir.dt.bfloat16
U32 = mybir.dt.uint32
ALU = mybir.AluOpType
ACT = mybir.ActivationFunctionType

B, S, D = 8, 256, 128
T = B * S
NT = T // P
CT = 4
CN = CT * P
NC = NT // CT
E = 8
PARTS = 3
ALPHA, LIMIT = 1.702, 9.0
LN_EPS, LN_EPS2 = 1e-5, 1e-12
H0, DH0 = 8, 16
TOPK = max(int(S * 0.1), 1)
ROUNDS = -(-TOPK // 8)
H1, DH1 = 16, 64
FB = H1 // 2


def fields(*sizes):
    at, out = 0, {}
    for name, n in sizes:
        out[name] = (at, at + n)
        at += n
    return out, at


PK0, N0 = fields(("ident", P), ("iota", 2 * CT * E), ("m0_gw", E), ("m0_b1", 4 * E), ("m0_gb", 1), ("m0_b2", D))
PK1, N1 = fields(*[(f"m0_w{w}{n}", c) for n in range(4) for w, c in ((1, E * P), (2, E // 2 * D))])
PK2, N2 = fields(("a0_wq", 2 * P), ("a0_wk", 2 * P), ("a0_wv", D), ("a0_wd", D), ("a0_wo", D), ("a0_wg", 64),
                 ("a0_wgp", D), ("a0_bq", 2), ("a0_bk", 2), ("a0_bv", D), ("a0_bd", 1), ("a0_bg", 1),
                 ("a0_bgp", 1), ("a0_bo", D), ("ones", P))
PK3, N3 = fields(("m1_gw", E), ("m1_b1", 2 * E), ("m1_gb", 1), ("m1_b2", D), ("m1_w1", 2 * E * P), ("m1_w2", 2 * E * D))
PK4, N4 = fields(("a1_wq", 1024), ("a1_wk", 1024), ("a1_wv", 1024), ("a1_wo", 1024), ("a1_bq", FB), ("a1_bk", FB),
                 ("a1_src", S), ("a1_val", S), ("a1_bv", 1024), ("a1_g", D), ("a1_b", D), ("a1_bo", CN),
                 ("a1_blk", 2))
PKB, NB = fields(("identb", P), ("sel", E * P), ("blkT", FB // 2 * P))


class Chain:

    def __init__(self, eng, sem, base, met):
        self.eng, self.sem, self.base, self.n, self.met = eng, sem, base, 0, met

    def __call__(self, ins):
        self.n += 1
        ins.then_inc(self.sem, 1)
        alone(self.eng, self.sem, self.base + self.n, self.met)


def wait(eng, ev, n):
    if not isinstance(n, int) or n > 0:
        eng.wait_ge(ev, n + 1)


def alone(eng, ev, n, met):
    if isinstance(n, int):
        wait(eng, ev, n)
    else:
        value = eng.to_reg(n + 1)
        eng.wait_ge(met, 1)
        eng.wait_ge(ev, value)


def build(nc, packed, packed_b, x_in, out):
    ctx = ExitStack()
    with ctx:
        def sb(name, cols, dt=F32, rows=P):
            return ctx.enter_context(nc.sbuf_tensor(name, [rows, cols], dt))

        def sem(name):
            return ctx.enter_context(nc.semaphore(name))

        counted = []

        def events(stage, names):
            made = {n: sem(f"{stage}_{n}") for n in names}
            counted.extend(made.values())
            return made

        bank = [ctx.enter_context(nc.psum_tensor(f"bank{i}", [P, CN], F32)) for i in range(8)]
        pk = [sb(f"pk{i}", n) for i, n in enumerate((N0, N1, N2, N3, N4))]
        pkb = sb("pkb", NB, BF16)
        where = {}
        for t, f in zip(pk, (PK0, PK1, PK2, PK3, PK4)):
            where.update({k: (t, a, b) for k, (a, b) in f.items()})
        where.update({k: (pkb, a, b) for k, (a, b) in PKB.items()})

        def cst(name, a=0, b=None, rows=slice(0, P)):
            t, lo, hi = where[name]
            return t[rows, lo + a:hi if b is None else lo + b]

        x = sb("x", T)
        xnT = sb("xnT", T)
        xn = sb("xn", CN)
        stats = sb("stats", CT * 6)
        mv = sb("mv", CT * 2)
        rstd = sb("rstd", 2 * CT)
        mhalf = sb("mhalf", CN)
        combT = sb("combT", T, BF16, PARTS * E)
        lgT = sb("lgT", CN, F32, E)
        small = {n: sb(n, c) for n, c in dict(lg=CT * E, mx=CT * 8, dif=CT, th=CT, idf=2 * CT, pw=2 * CT,
                                              eq=2 * CT * E, comb=CT * E, rest=CT * E).items()}
        midx = sb("midx", CT * 8, U32)
        comb3 = sb("comb3", CT * PARTS * E, BF16)
        sg = sb("sg", 2 * CN)
        vb = sb("vb", 2 * CN)
        s2b = sb("s2b", 2 * CN)
        hb = sb("hb", 4 * CN)
        yT = sb("yT", CN)

        s_ld = [sem(f"s_ld{i}") for i in range(6)]
        s_w = [sem(f"s_w{i}") for i in range(4)]
        s_x0 = [sem(f"s_x0{i}") for i in range(2)]
        s_const = sem("s_const")
        s_setup = sem("s_setup")
        s_start = sem("s_start")
        counted.append(s_setup)
        s_out = sem("s_out")

        class Moe:

            def __init__(self, kind, x_ready, sems, before, taken_over=lambda which, e: None):
                self.x_ready = x_ready
                self.taken_over = taken_over
                self.base = before * NC
                self.k = "m0" if kind == "swiglu" else "m1"
                self.glu = kind == "swiglu"
                self.hbanks = 2 if self.glu else 3
                self.lag = 2
                self.ev = sems
                self.hbuf = sems["hb"] if self.glu else sems["s2"]

            PREP_LINKS = 12

            def dve_norm(self, e, c):
                g = self.base + c
                if isinstance(c, int) and c == 0:
                    self.taken_over("dve", e)
                self.x_ready(e, c)
                for t in range(CT):
                    i = e.bn_stats(stats[:, 6 * t:6 * t + 6], x[:, bass.ds(c * CN + t * P, P)])
                i.then_inc(self.ev["st"], 1)
                alone(e, self.ev["st"], g + 1, s_const)
                for t in range(CT):
                    i = e.bn_aggr(mv[:, 2 * t:2 * t + 2], stats[:, 6 * t:6 * t + 6])
                i.then_inc(self.ev["mv"], 1)

            def pool_rstd(self, e, c):
                g = self.base + c
                alone(e, self.ev["mv"], g + 1, s_const)
                e.tensor_scalar(rstd[:, CT:2 * CT], mv[:, 1:2 * CT:2], LN_EPS, None, ALU.add).then_inc(self.ev["ve"], 1)
                wait(e, self.ev["ve"], g + 1)
                e.tensor_tensor(rstd[:, 0:CT], rstd[:, CT:2 * CT], mhalf[:, 0:CT], ALU.pow).then_inc(self.ev["rstd"], 1)

            def dve_xn(self, e, c):
                g = self.base + c
                wait(e, self.ev["rstd"], g + 1)
                wait(e, self.ev["T"], g)
                for t in range(CT):
                    i = e.tensor_scalar(xn[:, t * P:t * P + P], x[:, bass.ds(c * CN + t * P, P)],
                                        mv[:, 2 * t:2 * t + 1], rstd[:, t:t + 1], ALU.subtract, ALU.mult)
                i.then_inc(self.ev["xn"], 1)

            def pe_T(self, e, c):
                g = self.base + c
                wait(e, self.ev["xn"], g + 1)
                if isinstance(c, int) and c == 0:
                    self.taken_over("pe", e)
                for t in range(CT):
                    i = e.transpose(bank[0][:, t * P:t * P + P], xn[:, t * P:t * P + P], cst("ident"))
                i.then_inc(self.ev["T"], 1)

            def act_xnT(self, e, c):
                g = self.base + c
                wait(e, self.ev["T"], g + 1)
                e.activation(xnT[:, bass.ds(c * CN, CN)], bank[0][:, :], ACT.Copy).then_inc(self.ev["xnT"], 1)

            def pe_LT(self, e, c):
                g = self.base + c
                wait(e, self.ev["xnT"], g + 1)
                e.matmul(bank[0][0:E, :], cst(self.k + "_gw"), xnT[:, bass.ds(c * CN, CN)],
                         start=True, stop=True).then_inc(self.ev["LT"], 1)

            def act_lgT(self, e, c):
                g = self.base + c
                wait(e, self.ev["LT"], g + 1)
                bias = cst(self.k + "_gb", rows=slice(0, E))
                e.activation(lgT[:, :], bank[0][0:E, :], ACT.Identity, bias=bias).then_inc(self.ev["lgT"], 1)

            def pe_LG(self, e, c):
                g = self.base + c
                alone(e, self.ev["lgT"], g + 1, s_const)
                for t in range(CT):
                    i = e.transpose(bank[0][:, t * E:t * E + E], lgT[:, t * P:t * P + P],
                                    cst("ident", 0, E, slice(0, E)))
                i.then_inc(self.ev["LG"], 1)

            def dve_top2(self, e, c):
                g = self.base + c
                m = small
                ch = self.ch = Chain(e, self.ev["dv"], g * self.PREP_LINKS, s_const)
                wait(e, self.ev["LG"], g + 1)
                ch(e.tensor_copy(m["lg"][:, :], bank[0][:, 0:CT * E]))
                for t in range(CT):
                    i = e.max(m["mx"][:, 8 * t:8 * t + 8], m["lg"][:, E * t:E * t + E])
                ch(i)
                mx = m["mx"][:, :].rearrange("p (t k) -> p t k", k=8)
                e.tensor_tensor(m["dif"][:, :], mx[:, :, 0], mx[:, :, 1], ALU.subtract).then_inc(self.ev["dif"], 1)
                for t in range(CT):
                    i = e.max_index(midx[:, 8 * t:8 * t + 8], m["mx"][:, 8 * t:8 * t + 8], m["lg"][:, E * t:E * t + E])
                ch(i)

            def act_th(self, e, c):
                g = self.base + c
                wait(e, self.ev["dif"], g + 1)
                e.activation(small["th"][:, :], small["dif"][:, :], ACT.Tanh, scale=0.5).then_inc(self.ev["th"], 1)

            def dve_comb(self, e, c):
                g = self.base + c
                m, ch = small, self.ch
                ids = midx[:, :].rearrange("p (t k) -> p t k", k=8)
                for k in range(2):
                    i = e.tensor_copy(m["idf"][:, k * CT:k * CT + CT], ids[:, :, k])
                ch(i)
                wait(e, self.ev["th"], g + 1)
                e.tensor_scalar(m["pw"][:, 0:CT], m["th"][:, :], 0.5, 0.5, ALU.mult, ALU.add)
                e.tensor_scalar(m["pw"][:, CT:2 * CT], m["th"][:, :], -0.5, 0.5, ALU.mult, ALU.add)

                def bc(a):
                    return a.unsqueeze(2).to_broadcast([P, 2 * CT, E])

                def wide(a):
                    return a.rearrange("p (k e) -> p k e", e=E)
                ch(e.tensor_tensor(wide(m["eq"][:, :]), wide(cst("iota")), bc(m["idf"][:, :]), ALU.is_equal))
                ch(e.tensor_tensor(wide(m["eq"][:, :]), wide(m["eq"][:, :]), bc(m["pw"][:, :]), ALU.mult))
                ch(e.tensor_tensor(m["comb"][:, :], m["eq"][:, 0:CT * E], m["eq"][:, CT * E:], ALU.add))
                part = comb3[:, :].rearrange("p (t k e) -> p t k e", k=PARTS, e=E)
                f = m["comb"][:, :].rearrange("p (t e) -> p t e", e=E)
                r = m["rest"][:, :].rearrange("p (t e) -> p t e", e=E)
                wait(e, self.ev["CT"], g)
                ch(e.tensor_copy(part[:, :, 0, :], f))
                ch(e.tensor_tensor(r, f, part[:, :, 0, :], ALU.subtract))
                ch(e.tensor_copy(part[:, :, 1, :], r))
                ch(e.tensor_tensor(r, r, part[:, :, 1, :], ALU.subtract))
                ch(e.tensor_copy(part[:, :, 2, :], r))
                e.sem_inc(self.ev["c3"], 1)
                assert ch.n == self.PREP_LINKS, ch.n

            def pe_CT(self, e, c):
                g = self.base + c
                wait(e, self.ev["c3"], g + 1)
                to = bank[0][:, :].bitcast(BF16)
                for t in range(CT):
                    i = e.transpose(to[0:PARTS * E, t * P:t * P + P], comb3[:, t * PARTS * E:(t + 1) * PARTS * E],
                                    cst("identb"))
                i.then_inc(self.ev["CT"], 1)

            def act_cT(self, e, c):
                g = self.base + c
                wait(e, self.ev["CT"], g + 1)
                e.activation(combT[:, bass.ds(c * CN, CN)], bank[0][:, :].bitcast(BF16)[0:PARTS * E, 0:CN],
                             ACT.Copy).then_inc(self.ev["cT"], 1)

            HOOKS = dict(
                dve={1: dve_norm, 2: dve_xn, 8: dve_top2, 10: dve_comb},
                pool={0: pool_rstd},
                pe={3: pe_T, 5: pe_LT, 7: pe_LG, 12: pe_CT},
                act={3: act_xnT, 5: act_lgT, 9: act_th, 12: act_cT})

            def hooks(self, which, e, u, c, nxt):
                if nxt is None:
                    self.ahead(which, e, u)
                elif u in self.HOOKS[which]:
                    self.HOOKS[which][u](self, e, nxt)

            def first(self, which, e, pos):
                if pos in self.HOOKS[which]:
                    self.HOOKS[which][pos](self, e, 0)

            def units(self):
                return [(u, u // 2, u % 2) for u in range(2 * E)]

            def pe_chunk(self, e, c, nxt):
                g = self.base + c
                U, NB_ = g * 2 * E, self.hbanks
                xc = xnT[:, bass.ds(c * CN, CN)]
                wait(e, self.ev["cT"], g + 1)
                wait(e, self.ev["ye"], g)

                def second(u):
                    wait(e, self.hbuf, U + u + 1)
                    w2 = cst(f"m0_w2{u // 4}", u % 4 * D, u % 4 * D + D) if self.glu else cst("m1_w2", u * D, u * D + D)
                    e.matmul(bank[1][:, :], w2, hb[:, (u % 4) * CN:(u % 4 + 1) * CN],
                             start=False, stop=u == 2 * E - 1).then_inc(self.ev["y"], 1)

                for u, x_, j in self.units():
                    wait(e, self.ev["s2"] if self.glu else self.ev["sg"], U + max(u - NB_ + 1, 0))
                    if self.glu:
                        if u % 4 == 0:
                            e.wait_ge(s_w[u // 4], 16)
                        for s in range(2):
                            w = (u % 4 * 2 + s) * P
                            i = e.matmul(bank[4 + 2 * s + u % 2][:, :], cst(f"m0_w1{u // 4}", w, w + P), xc, start=True, stop=True)
                    else:
                        i = e.matmul(bank[4 + u % 3][:, :], cst("m1_w1", u * P, u * P + P), xc, start=True, stop=True)
                    i.then_inc(self.ev["h"], 1)
                    if j == 0:
                        alone(e, self.ev["s2"], U + max(u - 2, 0), s_const)
                        e.matmul(bank[2 + x_ % 2][:, :], cst("sel", x_ * P, x_ * P + P, slice(0, PARTS * E)),
                                 combT[:, bass.ds(c * CN, CN)], start=True, stop=True).then_inc(self.ev["cb"], 1)
                    if u == 0:
                        for k in range(PARTS):
                            e.matmul(bank[1][:, :], b2p[self.k][:, k * D:k * D + D], combT[:, bass.ds(c * CN, CN)],
                                     start=k == 0, stop=False)
                    if u >= self.lag:
                        second(u - self.lag)
                    self.hooks("pe", e, u, c, nxt)
                for u in range(2 * E - self.lag, 2 * E):
                    second(u)
                wait(e, self.ev["ye"], g + 1)
                if nxt is None:
                    self.bank0_free(e)
                for t in range(CT):
                    i = e.transpose(bank[0][:, t * P:t * P + P], yT[:, t * P:t * P + P], cst("ident"))
                i.then_inc(self.ev["yt"], 1)

            def act_chunk(self, e, c, nxt):
                g = self.base + c
                U = g * 2 * E
                for u, x_, j in self.units():
                    wait(e, self.ev["h"], U + u + 1)
                    wait(e, self.ev["s2"], U + max(u - 1, 0))
                    o = sg[:, (u % 2) * CN:(u % 2 + 1) * CN]
                    if self.glu:
                        e.activation(o, bank[4 + u % 2][:, :], ACT.Silu, bias=b1s[:, u:u + 1], scale=ALPHA).then_inc(self.ev["sg"], 1)
                    else:
                        e.activation(o, bank[4 + u % 3][:, :], ACT.Relu, bias=cst("m1_b1", u, u + 1)).then_inc(self.ev["sg"], 1)
                    self.hooks("act", e, u, c, nxt)
                wait(e, self.ev["y"], U + 2 * E)
                wait(e, self.ev["yt"], g)
                e.activation(yT[:, :], bank[1][:, :], ACT.Copy).then_inc(self.ev["ye"], 1)

            def dve_chunk(self, e, c, nxt):
                g = self.base + c
                U = g * 2 * E

                def last(u):
                    wait(e, self.ev["s2"], U + u + 1)
                    wait(e, self.ev["y"], U + max(u - 3, 0))
                    e.scalar_tensor_tensor(out=hb[:, (u % 4) * CN:(u % 4 + 1) * CN], in0=vb[:, (u % 2) * CN:(u % 2 + 1) * CN],
                                           scalar=1.0 - LIMIT, in1=s2b[:, (u % 2) * CN:(u % 2 + 1) * CN],
                                           op0=ALU.max, op1=ALU.mult).then_inc(self.hbuf, 1)

                for u, x_, j in self.units():
                    self.hooks("dve", e, u, c, nxt)
                    q = slice((u % 2) * CN, (u % 2 + 1) * CN)
                    if self.glu:
                        wait(e, self.hbuf, U + max(u - 1, 0))
                        wait(e, self.ev["h"], U + u + 1)
                        e.tensor_scalar(vb[:, q], bank[6 + u % 2][:, :], b1v[:, u:u + 1], LIMIT + 1.0, ALU.add, ALU.min)
                    wait(e, self.ev["sg"], U + u + 1)
                    if j == 0:
                        wait(e, self.ev["cb"], g * E + x_ + 1)
                    cb = bank[2 + x_ % 2][:, :]
                    if self.glu:
                        e.scalar_tensor_tensor(out=s2b[:, q], in0=sg[:, q], scalar=SILU_MAX, in1=cb,
                                               op0=ALU.min, op1=ALU.mult).then_inc(self.ev["s2"], 1)
                        if u:
                            last(u - 1)
                    else:
                        wait(e, self.ev["y"], U + max(u - 3, 0))
                        e.tensor_tensor(hb[:, (u % 4) * CN:(u % 4 + 1) * CN], sg[:, q], cb, ALU.mult).then_inc(self.ev["s2"], 1)
                if self.glu:
                    last(2 * E - 1)
                wait(e, self.ev["yt"], g + 1)
                e.scalar_tensor_tensor(out=x[:, bass.ds(c * CN, CN)], in0=bank[0][:, :],
                                       scalar=0.5 / ALPHA if self.glu else 0.5, in1=x[:, bass.ds(c * CN, CN)],
                                       op0=ALU.mult, op1=ALU.add).then_inc(self.ev["x"], 1)

            def pool_chunk(self, e, c, nxt):
                for u, _, _ in self.units():
                    self.hooks("pool", e, u, c, nxt)

            def run(self, which, e, start, ahead, bank0_free):
                self.ahead, self.bank0_free = ahead, bank0_free
                start(which, e)
                chunk = dict(pe=self.pe_chunk, act=self.act_chunk, dve=self.dve_chunk, pool=self.pool_chunk)[which]
                with e.Fori(0, NC - 1) as c:
                    chunk(e, c, c + 1)
                chunk(e, NC - 1, None)

        class Sparse:
            PAIRS = H0 // 2
            STEPS = 2 * PAIRS
            TK = 2 * (2 * ROUNDS - 1)
            SCALE = DH0 ** -0.5

            def __init__(self, name, x_ready):
                self.x_ready = x_ready
                self.ev = events(name, ("st", "mv", "ve", "rstd", "xn", "T", "xT", "q", "qe", "k", "ke", "V", "Ve", "th", "gs", "gp",
                          "gate", "S", "c", "tk", "nm", "e", "mk", "p", "PT", "pT", "PV", "den", "nrm", "aT", "aTe",
                          "ds", "mi", "mx", "o", "x"))

            def dve_norm(self, e, b, p):
                self.x_ready(e, b, p)
                for t in range(2):
                    i = e.bn_stats(stats[:, 6 * t:6 * t + 6], x[:, bass.ds(b * S + t * P, P)])
                i.then_inc(self.ev["st"], 1)
                alone(e, self.ev["st"], b + 1, s_const)
                for t in range(2):
                    i = e.bn_aggr(mv[:, 2 * t:2 * t + 2], stats[:, 6 * t:6 * t + 6])
                i.then_inc(self.ev["mv"], 1)

            def pool_rstd(self, e, b, p):
                alone(e, self.ev["mv"], b + 1, s_const)
                e.tensor_scalar(rstd[:, CT:CT + 2], mv[:, 1:4:2], LN_EPS, None, ALU.add).then_inc(self.ev["ve"], 1)
                wait(e, self.ev["ve"], b + 1)
                e.tensor_tensor(rstd[:, 0:2], rstd[:, CT:CT + 2], mhalf[:, 0:2], ALU.pow).then_inc(self.ev["rstd"], 1)

            def dve_xn(self, e, b, p):
                wait(e, self.ev["rstd"], b + 1)
                wait(e, self.ev["T"], b)
                for t in range(2):
                    i = e.tensor_scalar(xn[:, t * P:t * P + P], x[:, bass.ds(b * S + t * P, P)],
                                        mv[:, 2 * t:2 * t + 1], rstd[:, t:t + 1], ALU.subtract, ALU.mult)
                i.then_inc(self.ev["xn"], 1)

            def pe_T(self, e, b, p):
                wait(e, self.ev["xn"], b + 1)
                wait(e, self.ev["gate"], b)
                for t in range(2):
                    i = e.transpose(bank[0][:, t * P:t * P + P], xn[:, t * P:t * P + P], cst("ident"))
                i.then_inc(self.ev["T"], 1)

            def act_xT(self, e, b, p):
                wait(e, self.ev["T"], b + 1)
                e.activation(axT[:, :], bank[0][:, 0:S], ACT.Copy, accum_out=xsum[:, :]).then_inc(self.ev["xT"], 1)

            def pe_q(self, e, b, p):
                wait(e, self.ev["xT"], b + 1)
                for n in range(2):
                    i = e.matmul(bank[0][:, n * S:n * S + S], cst("a0_wq", n * P, n * P + P), axT[:, :], start=True, stop=True)
                i.then_inc(self.ev["q"], 1)

            def act_qe(self, e, b, p):
                wait(e, self.ev["q"], b + 1)
                for n in range(2):
                    i = e.activation(qT[p][:, n * S:n * S + S], bank[0][:, n * S:n * S + S], ACT.Identity,
                                     bias=cst("a0_bq", n, n + 1))
                i.then_inc(self.ev["qe"], 1)

            def pe_k(self, e, b, p):
                wait(e, self.ev["qe"], b + 1)
                for n in range(2):
                    i = e.matmul(bank[0][:, n * S:n * S + S], cst("a0_wk", n * P, n * P + P), axT[:, :], start=True, stop=True)
                i.then_inc(self.ev["k"], 1)

            def act_ke(self, e, b, p):
                wait(e, self.ev["k"], b + 1)
                for n in range(2):
                    i = e.activation(kT[p][:, n * S:n * S + S], bank[0][:, n * S:n * S + S], ACT.Identity,
                                     bias=cst("a0_bk", n, n + 1))
                i.then_inc(self.ev["ke"], 1)

            def pe_V(self, e, b, p):
                alone(e, self.ev["ke"], b + 1, s_const)
                for t in range(2):
                    e.matmul(bank[0][:, t * P:t * P + P], axT[:, t * P:t * P + P], cst("a0_wv"), start=True, stop=True)
                e.matmul(bank[0][0:64, S:S + 1], cst("a0_wg"), xsum[:, :], start=True, stop=True).then_inc(self.ev["V"], 1)

            def act_th(self, e, b, p):
                wait(e, self.ev["V"], b + 1)
                e.activation(gsm[:, 0:1], bank[0][0:64, S:S + 1], ACT.Tanh, bias=bgh[:, :], scale=0.5 / S).then_inc(self.ev["th"], 1)

            def dve_Ve(self, e, b, p):
                wait(e, self.ev["th"], b + 1)
                wait(e, self.ev["PV"], b * self.STEPS - self.STEPS if not isinstance(b, int) else max(b - 1, 0) * self.STEPS)
                for t in range(2):
                    e.tensor_tensor(V0[p][:, :].rearrange("p (t h d) -> p t h d", t=2, h=H0)[:, t, :, 0:DH0],
                                    bank[0][:, t * P:t * P + P].rearrange("p (h d) -> p h d", h=H0),
                                    cst("a0_bv").rearrange("p (h d) -> p h d", h=H0), ALU.add)
                e.tensor_scalar(gsm[:, 1:2], gsm[:, 0:1], 0.5, 0.5, ALU.mult, ALU.add).then_inc(self.ev["Ve"], 1)

            def pe_gp(self, e, b, p):
                alone(e, self.ev["Ve"], b + 1, s_const)
                e.matmul(bank[0][:, 0:1], cst("a0_wgp", rows=slice(0, 64)), gsm[:, 1:2], start=True, stop=True).then_inc(self.ev["gp"], 1)

            def dve_gate(self, e, b, p):
                wait(e, self.ev["gp"], b + 1)
                g = gate[p]
                e.tensor_scalar(g[:, 0:1], bank[0][:, 0:1], cst("a0_bgp"), None, ALU.add).then_inc(self.ev["gs"], 1)
                wait(e, self.ev["gs"], b + 1)
                e.tensor_scalar(g[:, 1:2], g[:, 0:1], -1.0, 1.0, ALU.mult, ALU.add).then_inc(self.ev["gate"], 1)

            def pe_S(self, e, A, a):
                p, m = a // self.STEPS % 2, a % self.PAIRS
                if a % self.STEPS == 0:
                    wait(e, self.ev["ke"], self.batch(A, a) + 1)
                if not (isinstance(A, int) and A < 2):
                    wait(e, self.ev["c"], A - 1)
                qt = a // self.PAIRS % 2
                for n in range(2):
                    r = slice(32 * m, 32 * m + DH0)
                    i = e.matmul(bank[4 + a % 2][:, n * S:n * S + S], qT[p][r, n * S + qt * P:n * S + qt * P + P],
                                 kT[p][r, n * S:n * S + S], start=True, stop=True)
                i.then_inc(self.ev["S"], 1)

            def act_c(self, e, A, a):
                wait(e, self.ev["S"], A + 1)
                if not (isinstance(A, int) and A < 4):
                    wait(e, self.ev["p"], A - 3)
                e.activation(sS[:, (a % 4) * 2 * S:(a % 4 + 1) * 2 * S], bank[4 + a % 2][:, :], ACT.Copy).then_inc(self.ev["c"], 1)

            def dve_topk(self, e, A, a):
                wait(e, self.ev["c"], A + 1)
                if not (isinstance(A, int) and A < 2):
                    wait(e, self.ev["p"], A - 1)
                ops = []
                for r in range(ROUNDS):
                    for n in range(2):
                        src = sS[:, (a % 4) * 2 * S + n * S:(a % 4) * 2 * S + n * S + S]
                        w = wk[:, n * S:n * S + S]
                        m8 = m8s[:, ((a % 2) * 2 + n) * 8 * ROUNDS + 8 * r:((a % 2) * 2 + n) * 8 * ROUNDS + 8 * r + 8]
                        ops.append(lambda m8=m8, s_=w if r else src: e.max(m8, s_))
                    if r < ROUNDS - 1:
                        for n in range(2):
                            src = sS[:, (a % 4) * 2 * S + n * S:(a % 4) * 2 * S + n * S + S]
                            w = wk[:, n * S:n * S + S]
                            m8 = m8s[:, ((a % 2) * 2 + n) * 8 * ROUNDS + 8 * r:((a % 2) * 2 + n) * 8 * ROUNDS + 8 * r + 8]
                            ops.append(lambda m8=m8, w=w, s_=w if r else src: e.match_replace(w, m8, s_, -3.0e38))
                for n, op in enumerate(ops):
                    if n >= 2:
                        alone(e, self.ev["tk"], A * self.TK + n - 1, s_const)
                    elif not (isinstance(A, int) and A == 0):
                        alone(e, self.ev["tk"], A * self.TK, s_const)
                    op().then_inc(self.ev["tk"], 1)

            def pool_sel(self, e, A, a):
                m = m8s[:, (a % 2) * 16 * ROUNDS:(a % 2 + 1) * 16 * ROUNDS].rearrange("p (n k) -> p n k", n=2)
                alone(e, self.ev["tk"], A * self.TK + 2, s_const)
                if not (isinstance(A, int) and A < 2):
                    alone(e, self.ev["e"], A - 1, s_const)
                e.tensor_scalar(negm[:, (a % 2) * 2:(a % 2) * 2 + 2], m[:, :, 0], -self.SCALE, None, ALU.mult).then_inc(self.ev["nm"], 1)
                alone(e, self.ev["tk"], A * self.TK + self.TK, s_const)
                alone(e, self.ev["p"], A, s_const)
                for n in range(2):
                    i = e.tensor_scalar(msk[:, n * S:n * S + S], sS[:, (a % 4) * 2 * S + n * S:(a % 4) * 2 * S + n * S + S],
                                        m[:, n, TOPK - 1:TOPK], None, ALU.is_ge)
                i.then_inc(self.ev["mk"], 1)
                wait(e, self.ev["mk"], A + 1)
                wait(e, self.ev["e"], A + 1)
                if not (isinstance(A, int) and A < 2):
                    wait(e, self.ev["PT"], A - 1)
                q = slice((a % 2) * 2 * S, (a % 2 + 1) * 2 * S)
                e.tensor_tensor(pS[:, q], msk[:, :], eS[:, q], ALU.mult).then_inc(self.ev["p"], 1)

            def act_e(self, e, A, a):
                wait(e, self.ev["nm"], A + 1)
                if not (isinstance(A, int) and A < 2):
                    wait(e, self.ev["p"], A - 1)
                for n in range(2):
                    i = e.activation(eS[:, ((a % 2) * 2 + n) * S:((a % 2) * 2 + n + 1) * S],
                                     sS[:, (a % 4) * 2 * S + n * S:(a % 4) * 2 * S + n * S + S], ACT.Exp,
                                     bias=negm[:, (a % 2) * 2 + n:(a % 2) * 2 + n + 1], scale=self.SCALE)
                i.then_inc(self.ev["e"], 1)

            def pe_PT(self, e, A, a):
                wait(e, self.ev["p"], A + 1)
                if not (isinstance(A, int) and A < 2):
                    wait(e, self.ev["pT"], A - 1)
                for n in range(4):
                    i = e.transpose(bank[6 + a % 2][:, n * P:n * P + P], pS[:, (a % 2) * 2 * S + n * P:(a % 2) * 2 * S + n * P + P],
                                    cst("ident"))
                i.then_inc(self.ev["PT"], 1)

            def act_pT(self, e, A, a):
                wait(e, self.ev["PT"], A + 1)
                if not (isinstance(A, int) and A < 2):
                    wait(e, self.ev["PV"], A - 1)
                e.activation(pT[:, (a % 2) * 2 * S:(a % 2 + 1) * 2 * S], bank[6 + a % 2][:, :], ACT.Copy).then_inc(self.ev["pT"], 1)

            def pe_PV(self, e, A, a):
                p, g, m = a // self.STEPS % 2, a // self.PAIRS % 2, a % self.PAIRS
                W = DH0 + 1
                if m == 0:
                    if a % self.STEPS == 0:
                        wait(e, self.ev["Ve"], self.batch(A, a) + 1)
                    if not (isinstance(A, int) and A < 2 * self.PAIRS):
                        wait(e, self.ev["nrm"], self.batch(A, a) * 2 + g - 1)
                wait(e, self.ev["pT"], A + 1)
                for n in range(2):
                    h = m + self.PAIRS * n
                    for t in range(2):
                        i = e.matmul(bank[2 + g][:, h * W:h * W + W], pT[:, ((a % 2) * 4 + n * 2 + t) * P:((a % 2) * 4 + n * 2 + t + 1) * P],
                                     V0[p][:, (t * H0 + h) * W:(t * H0 + h + 1) * W], start=t == 0, stop=t == 1)
                i.then_inc(self.ev["PV"], 1)

            def dve_nrm(self, e, b, g):
                W = DH0 + 1
                o = bank[2 + g][:, 0:H0 * W].rearrange("p (h d) -> p h d", h=H0)
                wait(e, self.ev["PV"], b * self.STEPS + (g + 1) * self.PAIRS)
                if not (isinstance(b, int) and b == 0):
                    wait(e, self.ev["aT"], b)
                e.reciprocal(rden[:, :], o[:, :, DH0]).then_inc(self.ev["den"], 1)
                wait(e, self.ev["den"], 2 * b + g + 1)
                e.tensor_tensor(attn[:, g * P:g * P + P].rearrange("p (h d) -> p h d", h=H0), o[:, :, 0:DH0],
                                rden[:, :].unsqueeze(2).to_broadcast([P, H0, DH0]), ALU.mult).then_inc(self.ev["nrm"], 1)

            def pe_aT(self, e, b, p):
                wait(e, self.ev["nrm"], 2 * b + 2)
                wait(e, self.ev["x"], b)
                for t in range(2):
                    i = e.transpose(bank[1][:, t * P:t * P + P], attn[:, t * P:t * P + P], cst("ident"))
                i.then_inc(self.ev["aT"], 1)

            def act_aT(self, e, b, p):
                wait(e, self.ev["aT"], b + 1)
                e.activation(aT[:, :], bank[1][:, 0:S], ACT.Copy).then_inc(self.ev["aTe"], 1)

            def pe_ds(self, e, b, p):
                wait(e, self.ev["aTe"], b + 1)
                e.matmul(bank[1][:, 0:S], cst("a0_wd"), aT[:, :], start=True, stop=True).then_inc(self.ev["ds"], 1)

            def dve_mix(self, e, b, p):
                wait(e, self.ev["ds"], b + 1)
                wait(e, self.ev["o"], b)
                e.tensor_scalar(mixt[:, :], bank[1][:, 0:S], cst("a0_bd"), gate[p][:, 0:1], ALU.add, ALU.mult).then_inc(self.ev["mi"], 1)
                wait(e, self.ev["mi"], b + 1)
                e.scalar_tensor_tensor(out=mix[:, :], in0=aT[:, :], scalar=gate[p][:, 1:2], in1=mixt[:, :],
                                       op0=ALU.mult, op1=ALU.add).then_inc(self.ev["mx"], 1)

            def pe_o(self, e, b, p):
                wait(e, self.ev["mx"], b + 1)
                for t in range(2):
                    e.matmul(bank[1][:, t * P:t * P + P], mix[:, t * P:t * P + P], cst("a0_wo"), start=True, stop=False)
                    i = e.matmul(bank[1][:, t * P:t * P + P], cst("ones", rows=slice(0, 1)), cst("a0_bo", rows=slice(0, 1)),
                                 start=False, stop=True)
                i.then_inc(self.ev["o"], 1)

            def dve_x(self, e, b, p):
                wait(e, self.ev["o"], b + 1)
                xb = x[:, bass.ds(b * S, S)]
                e.tensor_tensor(xb, bank[1][:, 0:S], xb, ALU.add).then_inc(self.ev["x"], 1)

            def batch(self, A, a):
                return A // self.STEPS if isinstance(A, int) else self.b_of(A, a)

            TASKS = dict(
                dve=((0, dve_norm, 1), (1, dve_xn, 1), (5, dve_Ve, 1), (6, dve_gate, 1), (4, dve_mix, -1), (5, dve_x, -1)),
                pool=((0, pool_rstd, 1),),
                pe=((1, pe_T, 1), (2, pe_q, 1), (3, pe_k, 1), (4, pe_V, 1), (5, pe_gp, 1),
                    (2, pe_aT, -1), (3, pe_ds, -1), (4, pe_o, -1)),
                act=((1, act_xT, 1), (2, act_qe, 1), (3, act_ke, 1), (4, act_th, 1), (2, act_aT, -1)))

            def tasks(self, which, e, b, a, first, final):
                r, p = a % self.STEPS, a // self.STEPS % 2
                for at, task, to in self.TASKS[which]:
                    if at == r and not (to > 0 and final) and not (to < 0 and first):
                        task(self, e, b + to, (p + 1) % 2)

            def step(self, which, e, b, a, first=False, final=False):
                r = a % self.STEPS
                A = b * self.STEPS + r
                self.b_of = lambda A_, a_: b + (a_ // self.STEPS - a // self.STEPS)

                def at(n):
                    if first and r + n < 0 or final and r + n >= self.STEPS:
                        return None
                    return A + n, a + n
                def call(f, n):
                    if at(n) is not None:
                        f(e, *at(n))
                if which == "pe":
                    call(self.pe_S, 2)
                    call(self.pe_PT, -1)
                    call(self.pe_PV, -2)
                elif which == "act":
                    call(self.act_e, 0)
                    call(self.act_c, 2)
                    call(self.act_pT, -1)
                elif which == "pool":
                    self.tasks(which, e, b, a, first, final)
                    call(self.pool_sel, 0)
                else:
                    if r == 2 and not first:
                        self.dve_nrm(e, b - 1, 1)
                    if r == 6:
                        self.dve_nrm(e, b, 0)
                    self.tasks(which, e, b, a, first, final)
                    call(self.dve_topk, 0)
                if which in ("pe", "act"):
                    self.tasks(which, e, b, a, first, final)
                if final:
                    self.ahead(which, e, 2 * r)
                    self.ahead(which, e, 2 * r + 1)

            def first(self, which, e, pos):
                if pos == 2:
                    e.wait_ge(s_const, 3)
                for r, task, to in self.TASKS[which]:
                    if to > 0 and pos == 2 * r + 2:
                        task(self, e, 0, 0)

            def run(self, which, e, start, ahead, bank0_free):
                start(which, e)
                self.ahead = ahead
                for A in range(2):
                    if which == "pe":
                        self.pe_S(e, A, A)
                    if which == "act":
                        self.act_c(e, A, A)
                N_ = self.STEPS
                for r in range(N_):
                    self.step(which, e, 0, r, first=True)
                with e.Fori(0, (B - 2) // 2) as i:
                    for a in range(N_, 3 * N_):
                        self.step(which, e, 2 * i + a // N_, a)
                for r in range(N_):
                    self.step(which, e, B - 1, N_ + r, final=True)
                if which == "pe":
                    A = B * N_
                    self.pe_PT(e, A - 1, 2 * N_ - 1)
                    for n in (2, 1):
                        self.pe_PV(e, A - n, 2 * N_ - n)
                    self.pe_aT(e, B - 1, 1), self.pe_ds(e, B - 1, 1), self.pe_o(e, B - 1, 1)
                elif which == "act":
                    self.act_pT(e, B * N_ - 1, 2 * N_ - 1)
                    self.act_aT(e, B - 1, 1)
                elif which == "dve":
                    self.dve_nrm(e, B - 1, 1), self.dve_mix(e, B - 1, 1), self.dve_x(e, B - 1, 1)

        class Unit:
            def __init__(self, c, g):
                self.c, self.g = c, g
                if c is None:
                    self.n, self.w, self.N, self.src, self.to = g, "k", S, cst("a1_src"), kn
                else:
                    self.n, self.w, self.N = 2 * c + 2 + g, "q", CN
                    self.src, self.to = xnT[:, bass.ds(c * CN, CN)], qn

        def each_block(task, first, apart=1):
            return [(first + apart * f, task, f) for f in range(FB // 2)]

        class Cross:
            G = FB // 2
            base = 0

            def __init__(self, name, x_ready):
                self.x_ready = x_ready
                self.ev = events(name, ("st", "mv", "ve", "rstd", "xn", "T", "xT", "q", "rr", "mn", "ex", "eq", "sq", "ss", "sse", "ri", "sp", "rT",
                          "rp", "rb", "qn", "S", "e", "PV", "de", "den", "nrm", "O", "z", "z2", "st2", "mv2", "ve2",
                          "rstd2", "x", "V", "Ve", "keep"))

            def dve_norm(self, e, c):
                self.x_ready(e, c)
                for t in range(CT):
                    i = e.bn_stats(stats[:, 6 * t:6 * t + 6], x[:, bass.ds(c * CN + t * P, P)])
                i.then_inc(self.ev["st"], 1)
                alone(e, self.ev["st"], c + 1, s_const)
                for t in range(CT):
                    i = e.bn_aggr(mv[:, 2 * t:2 * t + 2], stats[:, 6 * t:6 * t + 6])
                i.then_inc(self.ev["mv"], 1)

            def pool_rstd(self, e, c):
                alone(e, self.ev["mv"], c + 1, s_const)
                e.tensor_scalar(rstd[:, CT:2 * CT], mv[:, 1:2 * CT:2], LN_EPS, None, ALU.add).then_inc(self.ev["ve"], 1)
                wait(e, self.ev["ve"], c + 1)
                e.tensor_tensor(rstd[:, 0:CT], rstd[:, CT:2 * CT], mhalf[:, 0:CT], ALU.pow).then_inc(self.ev["rstd"], 1)

            def dve_xn(self, e, c):
                wait(e, self.ev["rstd"], c + 1)
                wait(e, self.ev["T"], c)
                wait(e, self.ev["keep"], c)
                for t in range(CT):
                    i = e.tensor_scalar(xn[:, t * P:t * P + P], x[:, bass.ds(c * CN + t * P, P)],
                                        mv[:, 2 * t:2 * t + 1], rstd[:, t:t + 1], ALU.subtract, ALU.mult)
                i.then_inc(self.ev["xn"], 1)

            def pe_T(self, e, c):
                wait(e, self.ev["xn"], c + 1)
                wait(e, self.ev["mn"], self.G * 2 * (c + 1))
                for t in range(CT):
                    i = e.transpose(bank[0][:, t * P:t * P + P], xn[:, t * P:t * P + P], cst("ident"))
                i.then_inc(self.ev["T"], 1)

            def act_xT(self, e, c):
                wait(e, self.ev["T"], c + 1)
                e.activation(xnT[:, bass.ds(c * CN, CN)], bank[0][:, :], ACT.Copy).then_inc(self.ev["xT"], 1)

            def to(self, u, f):
                f += self.G * u.g
                return u.to[:, f * u.N:f * u.N + u.N]

            def pe_q(self, e, u, f):
                if u.w == "q" and u.g == 0 and f == 0:
                    wait(e, self.ev["xT"], u.c + 1)
                wait(e, self.ev["mn"], self.G * u.n + f)
                if f == 0:
                    wait(e, self.ev["qn"], self.G * u.n)
                f += self.G * u.g
                e.matmul(bank[0][:, 0:u.N], cst("a1_w" + u.w, f * P, f * P + P), u.src, start=True, stop=True).then_inc(self.ev["q"], 1)

            def act_relu(self, e, u, f):
                F = f + self.G * u.g
                wait(e, self.ev["q"], self.G * u.n + f + 1)
                wait(e, self.ev["eq"], self.G * u.n + max(f - 1, 0))
                e.activation(rrb[:, (f % 2) * CN:(f % 2) * CN + u.N], bank[0][:, 0:u.N], ACT.Relu,
                             bias=cst("a1_b" + u.w, F, F + 1)).then_inc(self.ev["rr"], 1)

            def dve_min(self, e, u, f):
                F = f + self.G * u.g
                wait(e, self.ev["rr"], self.G * u.n + f + 1)
                wait(e, self.ev["eq"], self.G * u.n + max(f - 1, 0))
                e.tensor_scalar(exb[:, (f % 2) * CN:(f % 2) * CN + u.N], bank[0][:, 0:u.N], cst("a1_b" + u.w, F, F + 1),
                                0.0, ALU.add, ALU.min).then_inc(self.ev["mn"], 1)

            def act_ex(self, e, u, f):
                wait(e, self.ev["mn"], self.G * u.n + f + 1)
                b = slice((f % 2) * CN, (f % 2) * CN + u.N)
                e.activation(exb[:, b], exb[:, b], ACT.Exp).then_inc(self.ev["ex"], 1)

            def dve_elu(self, e, u, f):
                b = slice((f % 2) * CN, (f % 2) * CN + u.N)
                if u.w == "q" and f == 0:
                    v = 2 * H1 * u.c - H1 + H1 * u.g
                    wait(e, self.ev["S"], max(v, 0) if isinstance(v, int) else v)
                wait(e, self.ev["ex"], self.G * u.n + f + 1)
                e.scalar_tensor_tensor(out=self.to(u, f), in0=exb[:, b], scalar=-1.0, in1=rrb[:, b],
                                       op0=ALU.add, op1=ALU.add).then_inc(self.ev["eq"], 1)

            def act_sq(self, e, u, f):
                wait(e, self.ev["eq"], self.G * u.n + f + 1)
                wait(e, self.ev["ss"], self.G * u.n + max(f - 1, 0))
                e.activation(sqb[:, (f % 2) * CN:(f % 2) * CN + u.N], self.to(u, f), ACT.Square).then_inc(self.ev["sq"], 1)

            def pe_ss(self, e, u, f):
                wait(e, self.ev["sq"], self.G * u.n + f + 1)
                for t in range(u.N // P):
                    q = (f % 2) * CN + t * P
                    i = e.matmul(bank[7][:, t * FB + 2 * f:t * FB + 2 * f + 2], sqb[:, q:q + P], cst("a1_blk"), start=True, stop=True)
                i.then_inc(self.ev["ss"], 1)

            def act_sse(self, e, u):
                wait(e, self.ev["ss"], self.G * u.n + self.G)
                wait(e, self.ev["ri"], u.n)
                e.activation(ssb[:, 0:u.N // P * FB], bank[7][:, 0:u.N // P * FB], ACT.Copy).then_inc(self.ev["sse"], 1)

            def pool_ri(self, e, u):
                n = u.N // P * FB
                wait(e, self.ev["sse"], u.n + 1)
                wait(e, self.ev["sp"], u.n * 5)
                e.tensor_tensor(rib[:, 0:n], ssb[:, 0:n], mhalf[:, 0:n], ALU.pow).then_inc(self.ev["ri"], 1)

            def dve_split(self, e, u):
                ch = Chain(e, self.ev["sp"], u.n * 5, s_const)
                n = u.N // P
                part = rp3[:, 0:n * PARTS * FB].rearrange("p (t k h) -> p t k h", k=PARTS, h=FB)
                r = rib[:, 0:n * FB].rearrange("p (t h) -> p t h", h=FB)
                wait(e, self.ev["ri"], u.n + 1)
                wait(e, self.ev["rT"], u.n)
                for k in range(PARTS):
                    ch(e.tensor_copy(part[:, :, k, :], r))
                    if k < PARTS - 1:
                        ch(e.tensor_tensor(r, r, part[:, :, k, :], ALU.subtract))

            def pe_rT(self, e, u):
                wait(e, self.ev["sp"], u.n * 5 + 5)
                to = bank[7][:, :].bitcast(BF16)
                for t in range(u.N // P):
                    i = e.transpose(to[0:PARTS * FB, t * P:t * P + P], rp3[:, t * PARTS * FB:(t + 1) * PARTS * FB], cst("identb"))
                i.then_inc(self.ev["rT"], 1)

            def act_rT(self, e, u):
                wait(e, self.ev["rT"], u.n + 1)
                wait(e, self.ev["rb"], self.G * u.n)
                e.activation(rp[:, 0:u.N], bank[7][:, :].bitcast(BF16)[0:PARTS * FB, 0:u.N], ACT.Copy).then_inc(self.ev["rp"], 1)

            def pe_rb(self, e, u, f):
                wait(e, self.ev["rp"], u.n + 1)
                wait(e, self.ev["qn"], self.G * u.n + max(f - 1, 0))
                if f == 0 and u.g == 1 and u.w == "q" and not isinstance(u.c, int):
                    wait(e, self.ev["xT"], u.c + 2)
                e.matmul(bank[7 * (f % 2)][:, 0:u.N], cst("blkT", f * P, f * P + P, slice(0, PARTS * FB)), rp[:, 0:u.N],
                         start=True, stop=True).then_inc(self.ev["rb"], 1)

            def dve_qn(self, e, u, f):
                wait(e, self.ev["rb"], self.G * u.n + f + 1)
                e.tensor_tensor(self.to(u, f), bank[7 * (f % 2)][:, 0:u.N], self.to(u, f), ALU.mult).then_inc(self.ev["qn"], 1)

            def pe_V(self, e, n):
                t, half = n // 2, n % 2
                wait(e, self.ev["Ve"], max(n - 1, 0))
                e.matmul(bank[7 * half][:, :], cst("a1_val", t * P, t * P + P), cst("a1_wv", half * CN, half * CN + CN),
                         start=True, stop=True).then_inc(self.ev["V"], 1)

            def dve_V(self, e, n):
                t, half = n // 2, n % 2
                wait(e, self.ev["V"], n + 1)
                v = VO[:, :].rearrange("p (t f s d) -> p t f s d", t=2, f=FB, s=3)[:, t, 4 * half:4 * half + 4, 0:3:2, :]
                e.tensor_tensor(v, bank[7 * half][:, :].rearrange("p (f s d) -> p f s d", s=2, d=DH1),
                                cst("a1_bv", half * CN, half * CN + CN).rearrange("p (f s d) -> p f s d", s=2, d=DH1),
                                ALU.add).then_inc(self.ev["Ve"], 1)

            def pe_S(self, e, c, h):
                r, f = slice(64 * (h % 2), 64 * (h % 2) + 64), h // 2
                if h % 2 == 0:
                    wait(e, self.ev["qn"], FB * (c + 1) + f + 1)
                for t in range(2):
                    wait(e, self.ev["e"], 2 * (c * H1 + h) + t - 1 if h else 2 * c * H1)
                    e.matmul(bank[2 + t][:, :], kn[r, f * S + t * P:f * S + t * P + P], qn[r, f * CN:f * CN + CN],
                             start=True, stop=True).then_inc(self.ev["S"], 1)

            def act_e(self, e, c, h):
                for t in range(2):
                    wait(e, self.ev["S"], 2 * (c * H1 + h) + t + 1)
                    wait(e, self.ev["PV"], c * H1 + max(h - 1, 0))
                    e.activation(AT[:, ((h % 2) * 2 + t) * CN:((h % 2) * 2 + t + 1) * CN], bank[2 + t][:, :], ACT.Exp,
                                 scale=DH1 ** -0.5).then_inc(self.ev["e"], 1)

            def pe_PV(self, e, c, h):
                wait(e, self.ev["de"], c * H1 + max(h - 1, 0))
                if h == 0:
                    wait(e, self.ev["Ve"], 4)
                wait(e, self.ev["e"], 2 * (c * H1 + h) + 2)
                for t in range(2):
                    v = (t * FB + h // 2) * 3 * DH1 + (h % 2) * DH1
                    i = e.matmul(bank[4 + h % 2][:, :], VO[:, v:v + P], AT[:, ((h % 2) * 2 + t) * CN:((h % 2) * 2 + t + 1) * CN],
                                 start=t == 0, stop=t == 1)
                i.then_inc(self.ev["PV"], 1)

            def act_cp(self, e, c, h):
                f = h // 2
                own, other = (slice(0, 64), slice(64, P)) if h % 2 == 0 else (slice(64, P), slice(0, 64))
                q = slice((f % 2) * CN, (f % 2 + 1) * CN)
                wait(e, self.ev["PV"], c * H1 + h + 1)
                wait(e, self.ev["O"], FB * c + max(f - 1, 0))
                e.activation(denb[own, q], bank[4 + h % 2][other, :], ACT.Copy)
                e.activation(ctxb[own, q], bank[4 + h % 2][own, :], ACT.Copy).then_inc(self.ev["de"], 1)

            def dve_nrm(self, e, c, f):
                q = slice((f % 2) * CN, (f % 2 + 1) * CN)
                wait(e, self.ev["de"], c * H1 + 2 * f + 2)
                e.reciprocal(denb[:, q], denb[:, q]).then_inc(self.ev["den"], 1)
                wait(e, self.ev["den"], FB * c + f + 1)
                e.tensor_tensor(ctxb[:, q], ctxb[:, q], denb[:, q], ALU.mult).then_inc(self.ev["nrm"], 1)

            def pe_O(self, e, c, f):
                if f == 0:
                    wait(e, self.ev["z"], c)
                    e.matmul(bank[1][:, :], cst("ones", rows=slice(0, 1)), cst("a1_bo", rows=slice(0, 1)), start=True, stop=False)
                wait(e, self.ev["nrm"], FB * c + f + 1)
                for q in range(CT):
                    i = e.matmul(bank[1][:, q * P:q * P + P], ctxb[:, (f % 2) * CN + q * P:(f % 2) * CN + q * P + P],
                                 cst("a1_wo", f * P, f * P + P), start=False, stop=f == FB - 1 and q == CT - 1)
                i.then_inc(self.ev["O"], 1)

            def dve_tail(self, e, c):
                wait(e, self.ev["O"], FB * c + FB)
                zz = z[:, :].rearrange("p (q d) -> p q d", q=CT)

                def row(name):
                    return cst(name).unsqueeze(1).to_broadcast([P, CT, D])
                wait(e, self.ev["keep"], c + 1)
                e.tensor_tensor(z[:, :], bank[1][:, :], tkeep[:, :], ALU.add).then_inc(self.ev["z"], 1)
                alone(e, self.ev["z"], c + 1, s_const)
                for t in range(CT):
                    i = e.bn_stats(stats2[:, 6 * t:6 * t + 6], z[:, t * P:t * P + P])
                i.then_inc(self.ev["st2"], 1)
                alone(e, self.ev["st2"], c + 1, s_const)
                for t in range(CT):
                    i = e.bn_aggr(mv2[:, 2 * t:2 * t + 2], stats2[:, 6 * t:6 * t + 6])
                i.then_inc(self.ev["mv2"], 1)
                ch = Chain(e, self.ev["z2"], c * 4, s_const)
                wait(e, self.ev["rstd2"], c + 1)
                for t in range(CT):
                    i = e.tensor_scalar(z[:, t * P:t * P + P], z[:, t * P:t * P + P], mv2[:, 2 * t:2 * t + 1], rstd2[:, t:t + 1],
                                        ALU.subtract, ALU.mult)
                ch(i)
                ch(e.tensor_tensor(zz, zz, row("a1_g"), ALU.mult))
                ch(e.tensor_tensor(zz, zz, row("a1_b"), ALU.add))
                xc = x[:, bass.ds(c * CN, CN)]
                ch(e.tensor_tensor(xc, xc, z[:, :], ALU.add))
                e.sem_inc(self.ev["x"], 1)

            def pool_keep(self, e, c):
                alone(e, self.ev["xn"], c + 1, s_const)
                alone(e, self.ev["z"], c, s_const)
                e.tensor_copy(tkeep[:, :], xn[:, :]).then_inc(self.ev["keep"], 1)

            def pool_tail(self, e, c):
                alone(e, self.ev["mv2"], c + 1, s_const)
                e.tensor_scalar(rstd2[:, CT:2 * CT], mv2[:, 1:2 * CT:2], LN_EPS2, None, ALU.add).then_inc(self.ev["ve2"], 1)
                wait(e, self.ev["ve2"], c + 1)
                e.tensor_tensor(rstd2[:, 0:CT], rstd2[:, CT:2 * CT], mhalf[:, 0:CT], ALU.pow).then_inc(self.ev["rstd2"], 1)

            UNIT = dict(
                pe=each_block(pe_q, 0) + each_block(pe_ss, 1) + [(6, pe_rT)] + each_block(pe_rb, 7, 0),
                act=[(7, act_rT), (5, act_sse)] + each_block(act_ex, 1) + each_block(act_relu, 0) + each_block(act_sq, 1),
                dve=[(6, dve_split)] + each_block(dve_elu, 1) + each_block(dve_min, 0) + each_block(dve_qn, 7, 0),
                pool=[(5, pool_ri)])
            NORM = dict(pe=[(5, pe_T)], act=[(5, act_xT)], dve=[(0, dve_norm), (1, dve_xn)], pool=[(0, pool_rstd)])

            def unit(self, which, e, u, k, of=slice(None)):
                for at, task, *f in [t for t in self.UNIT[which] if t[0] == k][of]:
                    task(self, e, u, *f)

            def norm(self, which, e, c, k):
                for at, task in self.NORM[which]:
                    if at == k:
                        task(self, e, c)

            def chunk(self, which, e, c, nxt):
                if which == "pool":
                    self.pool_keep(e, c)
                for h in range(H1):
                    half, k = h // 8, h % 8
                    u = Unit(nxt if half else c, 1 - half) if half == 0 or nxt is not None else None

                    def beside(of=slice(None)):
                        if u is not None:
                            self.unit(which, e, u, k, of)
                    if which == "pe":
                        if k < 7:
                            self.pe_S(e, c, h + 1)
                            if k < 4:
                                beside(slice(0, 1))
                            self.pe_PV(e, c, h)
                            beside(slice(1 if k < 4 else 0, None))
                        else:
                            beside(slice(0, 1))
                            self.pe_PV(e, c, h)
                            if half == 0:
                                self.pe_S(e, c, h + 1)
                            elif nxt is not None:
                                self.pe_S(e, nxt, 0)
                            beside(slice(1, None))
                        if h % 2 and h > 1:
                            self.pe_O(e, c, h // 2 - 1)
                    elif which == "act":
                        self.act_e(e, c, h)
                        if h > 0:
                            self.act_cp(e, c, h - 1)
                        beside()
                    elif which == "dve":
                        beside()
                        if h % 2 == 0 and h > 0:
                            self.dve_nrm(e, c, h // 2 - 1)
                    else:
                        beside()
                    if half == 0 and nxt is not None:
                        self.norm(which, e, nxt, k)
                    if half == 1 and nxt is None:
                        self.ahead(which, e, 2 * k)
                        self.ahead(which, e, 2 * k + 1)
                if which == "pe":
                    self.pe_O(e, c, FB - 1)
                elif which == "act":
                    self.act_cp(e, c, H1 - 1)
                elif which == "dve":
                    self.dve_nrm(e, c, FB - 1)
                    self.dve_tail(e, c)
                else:
                    self.pool_tail(e, c)

            def first(self, which, e, pos):
                if pos == 1 and which == "pe":
                    wait(e, ms["x"], m1a.base + NC - 1)
                for n in range(2 * pos - 2, 2 * pos) if pos in (1, 2) else ():
                    if which == "pe":
                        self.pe_V(e, n)
                    elif which == "dve":
                        self.dve_V(e, n)
                if pos == 0 and which == "dve":
                    wait(e, ms["T"], m1a.base + NC)
                if pos == 4 and which in ("pe", "act"):
                    wait(e, self.ev["Ve"], 4)
                for k in range(8):
                    if pos == 6 + k:
                        self.norm(which, e, 0, k)
                todo = [(Unit(*u), k) for u in ((None, 0), (None, 1), (0, 0)) for k in range(8)]
                for u, k in todo[2 * (pos - 4):2 * (pos - 3)] if pos >= 4 else ():
                    self.unit(which, e, u, k)

            def run(self, which, e, start, ahead, bank0_free):
                start(which, e)
                self.ahead = ahead
                if which == "pe":
                    self.pe_S(e, 0, 0)
                with e.Fori(0, NC - 1) as c:
                    self.chunk(which, e, c, c + 1)
                self.chunk(which, e, NC - 1, None)

        kn = sb("kn", FB * S)
        qn = sb("qn", FB * CN)
        exb = sb("exb", 2 * CN)
        rrb, sqb = vb, s2b
        ssb = sb("ssb", CT * FB)
        rib = sb("rib", CT * FB)
        rp3 = sb("rp3", CT * PARTS * FB, BF16)
        rp = sb("rp", CN, BF16, PARTS * FB)
        VO = sb("VO", 2 * FB * 3 * DH1)
        AT = hb
        sS = sb("sS", 4 * 2 * S)
        ctxb, denb = sS[:, 0:2 * CN], sS[:, 2 * CN:4 * CN]
        tkeep = sb("tkeep", CN)
        z = yT
        stats2 = sb("stats2", CT * 6)
        mv2 = sb("mv2", CT * 2)
        rstd2 = sb("rstd2", 2 * CT)

        axT = sb("axT", S)
        xsum = sb("xsum", 1)
        qT = [sb(f"qT{n}", 2 * S) for n in range(2)]
        kT = [sb(f"kT{n}", 2 * S) for n in range(2)]
        V0 = [sb(f"V0{n}", 2 * H0 * (DH0 + 1)) for n in range(2)]
        gsm = sb("gsm", 2, F32, 64)
        bgh = sb("bgh", 1, F32, 64)
        gate = [sb(f"gate{n}", 2) for n in range(2)]
        wk, msk = sg[:, 0:2 * S], vb[:, 0:2 * S]
        m8s = sb("m8s", 4 * 8 * ROUNDS)
        negm = sb("negm", 4)
        eS, pS, pT = hb[:, 0:4 * S], hb[:, 4 * S:8 * S], qn[:, 0:4 * S]
        rden = sb("rden", H0)
        attn, aT, mixt, mix = (s2b[:, n * S:n * S + S] for n in range(4))

        SILU_MAX = float(ALPHA * LIMIT / (1.0 + np.exp(-ALPHA * LIMIT)))
        b1s = sb("b1s", 2 * E)
        b1v = sb("b1v", 2 * E)
        b2p = {k: sb("b2p_" + k, PARTS * D, BF16, PARTS * E) for k in ("m0", "m1")}
        b2r = sb("b2r", D)

        def setup_dve(e):
            ch = Chain(e, s_setup, 0, s_const)
            e.memset(mhalf[:, :], -0.5).then_inc(s_const, 1)
            e.wait_ge(s_ld[0], 16)
            b1 = cst("m0_b1").rearrange("p (u s) -> p u s", s=2)
            e.tensor_scalar(b1s[:, :], b1[:, :, 0], ALPHA, None, ALU.mult)
            ch(e.tensor_scalar(b1v[:, :], b1[:, :, 1], 1.0, None, ALU.add))
            exact_b2(ch, e, "m0", ALPHA)
            e.sem_inc(s_const, 1)

        def exact_b2(ch, e, k, f):
            r = slice(0, PARTS * E)
            p = b2p[k]
            ch(e.tensor_scalar(b2r[r, :], cst(k + "_b2", rows=r), f, None, ALU.mult))
            for n in range(PARTS):
                ch(e.tensor_copy(p[:, n * D:n * D + D], b2r[r, :]))
                if n < PARTS - 1:
                    ch(e.tensor_tensor(b2r[r, :], b2r[r, :], p[:, n * D:n * D + D], ALU.subtract))

        def setup_late(e):
            ch = Chain(e, s_setup, 7, s_const)
            for n in (2, 3, 4):
                e.wait_ge(s_ld[n], 16)
            exact_b2(ch, e, "m1", 1.0)
            for v in V0:
                e.memset(v[:, DH0::DH0 + 1], 1.0)
            e.memset(VO[:, :].rearrange("p (f s d) -> p f s d", s=3, d=DH1)[:, :, 1, :], 1.0)
            ch(e.tensor_scalar(bgh[:, :], cst("a0_bg", rows=slice(0, 64)), 0.5, None, ALU.mult))
            e.sem_inc(s_const, 1)

        def after(stage):
            return lambda e, c: wait(e, stage.ev["x"], stage.base + c + 1)

        ms = events("moe", ("st", "mv", "ve", "rstd", "xn", "T", "xnT", "LT", "lgT", "LG", "dif", "th", "c3",
                                           "CT", "cT", "h", "cb", "sg", "s2", "hb", "y", "ye", "yt", "x", "dv"))

        def a0_done(which, e):
            wait(e, a0.ev["gate"] if which == "pe" else a0.ev["T"], B)

        def a1_done(which, e):
            if which == "pe":
                wait(e, a1.ev["qn"], FB // 2 * (2 + 2 * NC))
            else:
                wait(e, a1.ev["keep"], NC)
                wait(e, a1.ev["T"], NC)

        def a0_x_ready(e, b, p):
            if isinstance(b, int) and b == 0:
                wait(e, m0a.ev["x"], m0a.base + 1)
                wait(e, ms["T"], m0a.base + NC)
            else:
                wait(e, m0a.ev["x"], m0a.base + NC)

        m0a = Moe("swiglu", lambda e, c: e.wait_ge(s_x0[int(not isinstance(c, int) or c > 0)], 16), ms, 0)
        a0 = Sparse("a0", a0_x_ready)
        m0b = Moe("swiglu", lambda e, c: wait(e, a0.ev["x"], 2 if isinstance(c, int) and c == 0 else B), ms, 1, a0_done)
        m1a = Moe("relu", after(m0b), ms, 2)
        a1 = Cross("a1", after(m1a))
        m1b = Moe("relu", after(a1), ms, 3, a1_done)
        stages = [m0a, a0, m0b, m1a, a1, m1b]
        last = stages[-1]

        def run_all(which, e):
            for n, stage in enumerate(stages):
                def start(which, e, n=n):
                    if n == 0:
                        for pos in range(16):
                            stages[0].first(which, e, pos)
                    elif stages[n - 1] is a0:
                        wait(e, a0.ev["x"], B)
                    elif which != "pool":
                        wait(e, stages[n - 1].ev["x"], stages[n - 1].base + NC)

                def ahead(which, e, pos, n=n):
                    if n == 0 and which == "dve" and pos == 0:
                        setup_late(e)
                    if n + 1 < len(stages):
                        stages[n + 1].first(which, e, pos)

                def bank0_free(e, n=n):
                    if n + 1 < len(stages) and stages[n + 1] is a0:
                        wait(e, a0.ev["gate"], 1)
                    elif n + 1 < len(stages) and stages[n + 1] is a1:
                        wait(e, a1.ev["qn"], 3 * FB // 2)
                stage.run(which, e, start, ahead, bank0_free)

        block = ctx.enter_context(nc.Block())
        xv = x_in.rearrange("b (t p) d -> p (b t) d", p=P)

        @block.sync
        def _(e):
            e.dma_start(pk[0][:, :], packed[0]).then_inc(s_ld[0], 16)

            def load_x(n, a, b):
                e.dma_start(x[:, a * D:b * D].rearrange("p (t d) -> p t d", d=D), xv[:, a:b, :]).then_inc(s_x0[n], 16)
            load_x(0, 0, CT)
            e.dma_start(pkb[:, :], packed_b).then_inc(s_ld[5], 16)
            for n in range(4):
                e.dma_start(pk[1][:, n * (N1 // 4):(n + 1) * (N1 // 4)], packed[1][:, n * (N1 // 4):(n + 1) * (N1 // 4)]).then_inc(s_w[n], 16)
                if n == 0:
                    load_x(1, CT, NT)
            for n in (2, 3, 4):
                e.dma_start(pk[n][:, :], packed[n]).then_inc(s_ld[n], 16)
            e.wait_ge(s_start, 1)
            wait(e, last.ev["x"], B if last is a0 else last.base + NC)
            e.dma_start(out.rearrange("b (t p) d -> p (b t) d", p=P), x[:, :].rearrange("p (t d) -> p t d", d=D)).then_inc(s_out, 16)
            e.wait_ge(s_out, 16)

        @block.gpsimd
        def _(e):
            for v in counted:
                e.sem_inc(v, 1)
            e.sem_inc(s_start, 1)
            e.wait_ge(s_const, 1)
            run_all("pool", e)

        @block.scalar
        def _(e):
            e.wait_ge(s_start, 1)
            e.wait_ge(s_const, 2)
            run_all("act", e)

        @block.vector
        def _(e):
            e.wait_ge(s_start, 1)
            setup_dve(e)
            run_all("dve", e)

        @block.tensor
        def _(e):
            e.wait_ge(s_start, 1)
            e.wait_ge(s_ld[0], 16)
            e.wait_ge(s_ld[5], 16)
            e.wait_ge(s_const, 2)
            run_all("pe", e)


def pack(names, n, parts):
    a = np.zeros((P, n), np.float32)
    for k, (lo, hi) in names.items():
        v = parts[k]
        a[:v.shape[0], lo:hi] = v.reshape(v.shape[0], hi - lo)
    return a


def kernel(**inputs):
    import ml_dtypes
    import concourse.bacc as bacc
    from concourse.bass_utils import run_bass_kernel_spmd as run

    i = {k: np.asarray(v) for k, v in inputs.items()}
    a0, f0, a1, f1 = "L0_attn_", "L0_ffn_", "L1_attn_", "L1_ffn_"

    def rows(v):
        return np.broadcast_to(v.reshape(1, -1), (P, v.size))

    def cols(v, n=P):
        return v.reshape(-1, n).T

    def heads(w):
        o = np.zeros((w.shape[1], 8, 32), np.float32)
        o[:, :, :DH0] = w.T.reshape(w.shape[1], 8, DH0)
        return o

    iota = np.broadcast_to(np.arange(E, dtype=np.float32), (P, 2 * CT, E))
    w1 = i[f0 + "dense_1_w"].reshape(E, 2, P, 2, D)
    wd = np.zeros((2, 64, 2, 64), np.float32)
    wd[0, :, 0], wd[1, :, 1] = i[a0 + "Wd"].T, i[a0 + "Wd"].T
    blk = np.zeros((2, 64, 2), np.float32)
    blk[0, :, 0] = blk[1, :, 1] = 1
    parts = {
        "ident": np.eye(P, dtype=np.float32), "iota": iota,
        "m0_gw": i[f0 + "gate_w"], "m0_gb": np.zeros((E, 1), np.float32),
        "m0_b1": i[f0 + "dense_1_b"].reshape(E, 2, P, 2).transpose(2, 0, 1, 3),
        "m0_b2": np.concatenate([i[f0 + "dense_2_b"]] * PARTS),
        "a0_wq": heads(i[a0 + "Wq"]), "a0_wk": heads(i[a0 + "Wk"]),
        "a0_wv": i[a0 + "Wv"].T, "a0_wd": wd.reshape(P, P), "a0_wo": i[a0 + "Wo"].T,
        "a0_wg": i[a0 + "Wg"].T, "a0_wgp": i[a0 + "Wgp"].T,
        "a0_bq": heads(i[a0 + "bq"].reshape(-1, 1)).reshape(2, P).T, "a0_bk": heads(i[a0 + "bk"].reshape(-1, 1)).reshape(2, P).T,
        "a0_bv": rows(i[a0 + "bv"]), "a0_bd": np.concatenate([i[a0 + "bd"]] * 2).reshape(P, 1),
        "a0_bg": i[a0 + "bg"].reshape(64, 1), "a0_bgp": i[a0 + "bgp"].reshape(P, 1),
        "a0_bo": rows(i[a0 + "bo"]), "ones": np.ones((P, P), np.float32),
        "m1_gw": i[f1 + "Wg"].T, "m1_gb": i[f1 + "bg"].reshape(E, 1),
        "m1_b1": cols(i[f1 + "b1"]), "m1_b2": np.concatenate([i[f1 + "b2"]] * PARTS),
        "m1_w1": i[f1 + "W1"].transpose(2, 0, 1),
        "m1_w2": i[f1 + "W2"].reshape(E, D, 2, P).transpose(3, 0, 2, 1),
        "a1_wq": i[a1 + "Wq"], "a1_wk": i[a1 + "Wk"], "a1_wv": i[a1 + "Wv"],
        "a1_wo": i[a1 + "Wo"].reshape(FB, P, D).transpose(1, 0, 2),
        "a1_bq": cols(i[a1 + "bq"]), "a1_bk": cols(i[a1 + "bk"]),
        "a1_src": i[a1 + "source_embedding"].T, "a1_val": i[a1 + "value_embedding"].T,
        "a1_bv": rows(i[a1 + "bv"]), "a1_g": rows(i[a1 + "ln_g"]), "a1_b": rows(i[a1 + "ln_b"]),
        "a1_bo": rows(np.concatenate([i[a1 + "bo"]] * CT)), "a1_blk": blk.reshape(P, -1),
    }
    w1 = w1.transpose(4, 0, 1, 3, 2)
    w2 = i[f0 + "dense_2_w"].reshape(E, D, 2, P).transpose(3, 0, 2, 1)
    for n in range(4):
        parts |= {f"m0_w1{n}": w1[:, 2 * n:2 * n + 2], f"m0_w2{n}": w2[:, 2 * n:2 * n + 2]}
    sel = np.zeros((PARTS, E, E, P), np.float32)
    for e_ in range(E):
        sel[:, e_, e_] = 1
    blkT = np.zeros((PARTS, FB, FB // 2, 2, 64), np.float32)
    for h in range(FB):
        blkT[:, h, h // 2, h % 2] = 1
    parts |= {"identb": parts["ident"], "sel": sel.reshape(PARTS * E, -1), "blkT": blkT.reshape(PARTS * FB, -1)}

    nc = bacc.Bacc("TRN2", target_bir_lowering=False, num_devices=1)
    arrays = {}

    def arg(name, a):
        arrays[name] = np.ascontiguousarray(a)
        return nc.dram_tensor(name, a.shape, mybir.dt.from_np(a.dtype), kind="ExternalInput").ap()

    packed = [arg(f"packed{n}", pack(names, size, parts))
              for n, (names, size) in enumerate(((PK0, N0), (PK1, N1), (PK2, N2), (PK3, N3), (PK4, N4)))]
    packed_b = arg("packed_b", pack(PKB, NB, parts).astype(ml_dtypes.bfloat16))
    x_in = arg("x_in", i[a0 + "x"])
    out = nc.dram_tensor("out", (B, S, D), F32, kind="ExternalOutput").ap()
    build(nc, packed, packed_b, x_in, out)
    r = run(nc, [arrays], core_ids=[0])
    return r.results[0]["out"]
```

```python
from contextlib import ExitStack

import numpy as np
import concourse.bass as bass
from concourse import mybir

P = 128
F32 = mybir.dt.float32
BF16 = mybir.dt.bfloat16
U32 = mybir.dt.uint32
ALU = mybir.AluOpType
ACT = mybir.ActivationFunctionType

B, S, D = 8, 256, 128
T = B * S
NT = T // P
CT = 4
CN = CT * P
NC = NT // CT
E = 8
PARTS = 3
AHEAD = 3
ALPHA, LIMIT = 1.702, 9.0
LN_EPS, LN_EPS2 = 1e-5, 1e-12
H0, DH0 = 8, 16
TOPK = max(int(S * 0.1), 1)
ROUNDS = -(-TOPK // 8)
H1, DH1 = 16, 64
FB = H1 // 2


def fields(*sizes):
    at, out = 0, {}
    for name, n in sizes:
        out[name] = (at, at + n)
        at += n
    return out, at


PK0, N0 = fields(("ident", P), ("iota", 2 * CT * E), ("m0_gw", E), ("m0_b1", 4 * E), ("m0_gb", 1), ("m0_b2", D))
PK1, N1 = fields(*[(f"m0_w{w}{n}", c) for n in range(4) for w, c in ((1, E * P), (2, E // 2 * D))])
PK2, N2 = fields(("a0_wq", 2 * P), ("a0_wk", 2 * P), ("a0_wv", D), ("a0_wd", D), ("a0_wo", D), ("a0_wg", 64),
                 ("a0_wgp", D), ("a0_bq", 2), ("a0_bk", 2), ("a0_bv", D), ("a0_bd", 1), ("a0_bg", 1),
                 ("a0_bgp", 1), ("a0_bo", D), ("ones", P))
PK3, N3 = fields(("m1_gw", E), ("m1_b1", 2 * E), ("m1_gb", 1), ("m1_b2", D), ("m1_w1", 2 * E * P), ("m1_w2", 2 * E * D))
PK4, N4 = fields(("a1_wq", 1024), ("a1_wk", 1024), ("a1_wv", 1024), ("a1_wo", 1024), ("a1_bq", FB), ("a1_bk", FB),
                 ("a1_src", S), ("a1_val", S), ("a1_bv", 1024), ("a1_g", D), ("a1_b", D), ("a1_bo", CN),
                 ("a1_blk", 2))
PKB, NB = fields(("identb", P), ("sel", E * P), ("blkT", FB // 2 * P))


class Chain:

    def __init__(self, eng, sem, base, met):
        self.eng, self.sem, self.base, self.n, self.met = eng, sem, base, 0, met

    def __call__(self, ins):
        self.n += 1
        ins.then_inc(self.sem, 1)
        alone(self.eng, self.sem, self.base + self.n, self.met)


def wait(eng, ev, n):
    if not isinstance(n, int) or n > 0:
        eng.wait_ge(ev, n + 1)


def alone(eng, ev, n, met):
    if isinstance(n, int):
        wait(eng, ev, n)
    else:
        value = eng.to_reg(n + 1)
        eng.wait_ge(met, 1)
        eng.wait_ge(ev, value)


def build(nc, packed, packed_b, x_in, out):
    ctx = ExitStack()
    with ctx:
        def sb(name, cols, dt=F32, rows=P):
            return ctx.enter_context(nc.sbuf_tensor(name, [rows, cols], dt))

        def sem(name):
            return ctx.enter_context(nc.semaphore(name))

        counted = []

        def events(stage, names):
            made = {n: sem(f"{stage}_{n}") for n in names}
            counted.extend(made.values())
            return made

        bank = [ctx.enter_context(nc.psum_tensor(f"bank{i}", [P, CN], F32)) for i in range(8)]
        pk = [sb(f"pk{i}", n) for i, n in enumerate((N0, N1, N2, N3, N4))]
        pkb = sb("pkb", NB, BF16)
        where = {}
        for t, f in zip(pk, (PK0, PK1, PK2, PK3, PK4)):
            where.update({k: (t, a, b) for k, (a, b) in f.items()})
        where.update({k: (pkb, a, b) for k, (a, b) in PKB.items()})

        def cst(name, a=0, b=None, rows=slice(0, P)):
            t, lo, hi = where[name]
            return t[rows, lo + a:hi if b is None else lo + b]

        x = sb("x", T)
        xnT = sb("xnT", T)
        xn = sb("xn", CN)
        stats = sb("stats", CT * 6)
        mv = sb("mv", CT * 2)
        rstd = sb("rstd", 2 * CT)
        mhalf = sb("mhalf", CN)
        combT = sb("combT", T, BF16, PARTS * E)
        lgT = sb("lgT", CN, F32, E)
        small = {n: sb(n, c) for n, c in dict(lg=CT * E, mx=CT * 8, dif=CT, th=CT, idf=2 * CT, pw=2 * CT,
                                              eq=2 * CT * E, comb=CT * E, rest=CT * E).items()}
        midx = sb("midx", CT * 8, U32)
        comb3 = sb("comb3", CT * PARTS * E, BF16)
        sg = sb("sg", 2 * CN)
        vb = sb("vb", 2 * CN)
        s2b = sb("s2b", 2 * CN)
        hb = sb("hb", 4 * CN)
        yT = sb("yT", CN)

        s_ld = [sem(f"s_ld{i}") for i in range(6)]
        s_w = [sem(f"s_w{i}") for i in range(4)]
        s_x0 = [sem(f"s_x0{i}") for i in range(2)]
        s_const = sem("s_const")
        s_setup = sem("s_setup")
        s_start = sem("s_start")
        counted.append(s_setup)
        s_out = sem("s_out")

        class Moe:

            def __init__(self, kind, x_ready, sems, before, taken_over=lambda which, e: None):
                self.x_ready, self.early = x_ready, 0
                self.taken_over = taken_over
                self.base = before * NC
                self.k = "m0" if kind == "swiglu" else "m1"
                self.glu = kind == "swiglu"
                self.ev = sems
                self.hbuf = sems["hb"] if self.glu else sems["s2"]

            PREP_LINKS = 12

            def dve_norm(self, e, c):
                g = self.base + c
                if isinstance(c, int) and c == 0:
                    self.taken_over("dve", e)
                self.x_ready(e, c)
                for t in range(CT):
                    i = e.bn_stats(stats[:, 6 * t:6 * t + 6], x[:, bass.ds(c * CN + t * P, P)])
                i.then_inc(self.ev["st"], 1)
                alone(e, self.ev["st"], g + 1, s_const)
                for t in range(CT):
                    i = e.bn_aggr(mv[:, 2 * t:2 * t + 2], stats[:, 6 * t:6 * t + 6])
                i.then_inc(self.ev["mv"], 1)

            def pool_rstd(self, e, c):
                g = self.base + c
                alone(e, self.ev["mv"], g + 1, s_const)
                e.tensor_scalar(rstd[:, CT:2 * CT], mv[:, 1:2 * CT:2], LN_EPS, None, ALU.add).then_inc(self.ev["ve"], 1)
                wait(e, self.ev["ve"], g + 1)
                e.tensor_tensor(rstd[:, 0:CT], rstd[:, CT:2 * CT], mhalf[:, 0:CT], ALU.pow).then_inc(self.ev["rstd"], 1)

            def dve_xn(self, e, c):
                g = self.base + c
                wait(e, self.ev["rstd"], g + 1)
                wait(e, self.ev["T"], g)
                for t in range(CT):
                    i = e.tensor_scalar(xn[:, t * P:t * P + P], x[:, bass.ds(c * CN + t * P, P)],
                                        mv[:, 2 * t:2 * t + 1], rstd[:, t:t + 1], ALU.subtract, ALU.mult)
                i.then_inc(self.ev["xn"], 1)

            def pe_T(self, e, c):
                g = self.base + c
                wait(e, self.ev["xn"], g + 1)
                if isinstance(c, int) and c == 0:
                    self.taken_over("pe", e)
                for t in range(CT):
                    i = e.transpose(bank[0][:, t * P:t * P + P], xn[:, t * P:t * P + P], cst("ident"))
                i.then_inc(self.ev["T"], 1)

            def act_xnT(self, e, c):
                g = self.base + c
                wait(e, self.ev["T"], g + 1)
                e.activation(xnT[:, bass.ds(c * CN, CN)], bank[0][:, :], ACT.Copy).then_inc(self.ev["xnT"], 1)

            def pe_LT(self, e, c):
                g = self.base + c
                wait(e, self.ev["xnT"], g + 1)
                e.matmul(bank[0][0:E, :], cst(self.k + "_gw"), xnT[:, bass.ds(c * CN, CN)],
                         start=True, stop=True).then_inc(self.ev["LT"], 1)

            def act_lgT(self, e, c):
                g = self.base + c
                wait(e, self.ev["LT"], g + 1)
                bias = cst(self.k + "_gb", rows=slice(0, E))
                e.activation(lgT[:, :], bank[0][0:E, :], ACT.Identity, bias=bias).then_inc(self.ev["lgT"], 1)

            def pe_LG(self, e, c):
                g = self.base + c
                alone(e, self.ev["lgT"], g + 1, s_const)
                for t in range(CT):
                    i = e.transpose(bank[0][:, t * E:t * E + E], lgT[:, t * P:t * P + P],
                                    cst("ident", 0, E, slice(0, E)))
                i.then_inc(self.ev["LG"], 1)

            def dve_top2(self, e, c):
                g = self.base + c
                m = small
                ch = self.ch = Chain(e, self.ev["dv"], g * self.PREP_LINKS, s_const)
                wait(e, self.ev["LG"], g + 1)
                ch(e.tensor_copy(m["lg"][:, :], bank[0][:, 0:CT * E]))
                for t in range(CT):
                    i = e.max(m["mx"][:, 8 * t:8 * t + 8], m["lg"][:, E * t:E * t + E])
                ch(i)
                mx = m["mx"][:, :].rearrange("p (t k) -> p t k", k=8)
                e.tensor_tensor(m["dif"][:, :], mx[:, :, 0], mx[:, :, 1], ALU.subtract).then_inc(self.ev["dif"], 1)
                for t in range(CT):
                    i = e.max_index(midx[:, 8 * t:8 * t + 8], m["mx"][:, 8 * t:8 * t + 8], m["lg"][:, E * t:E * t + E])
                ch(i)

            def act_th(self, e, c):
                g = self.base + c
                wait(e, self.ev["dif"], g + 1)
                e.activation(small["th"][:, :], small["dif"][:, :], ACT.Tanh, scale=0.5).then_inc(self.ev["th"], 1)

            def dve_comb(self, e, c):
                g = self.base + c
                m, ch = small, self.ch
                ids = midx[:, :].rearrange("p (t k) -> p t k", k=8)
                for k in range(2):
                    i = e.tensor_copy(m["idf"][:, k * CT:k * CT + CT], ids[:, :, k])
                ch(i)
                wait(e, self.ev["th"], g + 1)
                e.tensor_scalar(m["pw"][:, 0:CT], m["th"][:, :], 0.5, 0.5, ALU.mult, ALU.add)
                e.tensor_scalar(m["pw"][:, CT:2 * CT], m["th"][:, :], -0.5, 0.5, ALU.mult, ALU.add)

                def bc(a):
                    return a.unsqueeze(2).to_broadcast([P, 2 * CT, E])

                def wide(a):
                    return a.rearrange("p (k e) -> p k e", e=E)
                ch(e.tensor_tensor(wide(m["eq"][:, :]), wide(cst("iota")), bc(m["idf"][:, :]), ALU.is_equal))
                ch(e.tensor_tensor(wide(m["eq"][:, :]), wide(m["eq"][:, :]), bc(m["pw"][:, :]), ALU.mult))
                ch(e.tensor_tensor(m["comb"][:, :], m["eq"][:, 0:CT * E], m["eq"][:, CT * E:], ALU.add))

            def dve_parts(self, e, c):
                g = self.base + c
                m, ch = small, self.ch
                part = comb3[:, :].rearrange("p (t k e) -> p t k e", k=PARTS, e=E)
                f = m["comb"][:, :].rearrange("p (t e) -> p t e", e=E)
                r = m["rest"][:, :].rearrange("p (t e) -> p t e", e=E)
                wait(e, self.ev["CT"], g)
                ch(e.tensor_copy(part[:, :, 0, :], f))
                ch(e.tensor_tensor(r, f, part[:, :, 0, :], ALU.subtract))
                ch(e.tensor_copy(part[:, :, 1, :], r))
                ch(e.tensor_tensor(r, r, part[:, :, 1, :], ALU.subtract))
                ch(e.tensor_copy(part[:, :, 2, :], r))
                e.sem_inc(self.ev["c3"], 1)
                assert ch.n == self.PREP_LINKS, ch.n

            def pe_CT(self, e, c):
                g = self.base + c
                wait(e, self.ev["c3"], g + 1)
                to = bank[0][:, :].bitcast(BF16)
                for t in range(CT):
                    i = e.transpose(to[0:PARTS * E, t * P:t * P + P], comb3[:, t * PARTS * E:(t + 1) * PARTS * E],
                                    cst("identb"))
                i.then_inc(self.ev["CT"], 1)

            def act_cT(self, e, c):
                g = self.base + c
                wait(e, self.ev["CT"], g + 1)
                e.activation(combT[:, bass.ds(c * CN, CN)], bank[0][:, :].bitcast(BF16)[0:PARTS * E, 0:CN],
                             ACT.Copy).then_inc(self.ev["cT"], 1)

            HOOKS = dict(
                dve={0: dve_norm, 1: dve_xn, 6: dve_top2, 8: dve_comb, 9: dve_parts},
                pool={0: pool_rstd},
                pe={2: pe_T, 4: pe_LT, 5: pe_LG, 11: pe_CT},
                act={2: act_xnT, 4: act_lgT, 7: act_th, 11: act_cT})

            def hooks(self, which, e, u, c, nxt):
                if self.beside:
                    self.beside(which, e, u)
                if nxt is not None and u in self.HOOKS[which]:
                    self.HOOKS[which][u](self, e, nxt)

            def first(self, which, e, pos):
                if pos in self.HOOKS[which]:
                    self.HOOKS[which][pos](self, e, 0)

            def before(self, c, u, k):
                return (self.base + c) * 2 * E + (u - k if u < AHEAD else max(u - k, 0))

            def pe_first(self, e, c, u):
                g = self.base + c
                if u == 0:
                    wait(e, self.ev["xnT"], g + 1)
                wait(e, self.ev["s2"] if self.glu else self.ev["sg"], self.before(c, u, 1))
                xc = xnT[:, bass.ds(c * CN, CN)]
                if self.glu:
                    if u % 4 == 0:
                        e.wait_ge(s_w[u // 4], 16)
                    for s in range(2):
                        w = (u % 4 * 2 + s) * P
                        i = e.matmul(bank[4 + 2 * s + u % 2][:, :], cst(f"m0_w1{u // 4}", w, w + P), xc, start=True, stop=True)
                else:
                    i = e.matmul(bank[4 + u % 2][:, :], cst("m1_w1", u * P, u * P + P), xc, start=True, stop=True)
                i.then_inc(self.ev["h"], 1)

            def pe_comb(self, e, c, x_):
                if x_ == 0:
                    alone(e, self.ev["cT"], self.base + c + 1, s_const)
                alone(e, self.ev["s2"], self.before(c, 2 * x_, 2), s_const)
                e.matmul(bank[2 + x_ % 2][:, :], cst("sel", x_ * P, x_ * P + P, slice(0, PARTS * E)),
                         combT[:, bass.ds(c * CN, CN)], start=True, stop=True).then_inc(self.ev["cb"], 1)

            def pe_second(self, e, c, u):
                g = self.base + c
                if u == 0:
                    alone(e, self.ev["ye"], g, s_const)
                    for k in range(PARTS):
                        e.matmul(bank[1][:, :], b2p[self.k][:, k * D:k * D + D], combT[:, bass.ds(c * CN, CN)],
                                 start=k == 0, stop=False)
                wait(e, self.hbuf, g * 2 * E + u + 1)
                w2 = cst(f"m0_w2{u // 4}", u % 4 * D, u % 4 * D + D) if self.glu else cst("m1_w2", u * D, u * D + D)
                e.matmul(bank[1][:, :], w2, hb[:, (u % 4) * CN:(u % 4 + 1) * CN],
                         start=False, stop=u == 2 * E - 1).then_inc(self.ev["y"], 1)

            def act_unit(self, e, c, u):
                wait(e, self.ev["h"], (self.base + c) * 2 * E + u + 1)
                wait(e, self.ev["s2"], self.before(c, u, 1))
                o = sg[:, (u % 2) * CN:(u % 2 + 1) * CN]
                if self.glu:
                    i = e.activation(o, bank[4 + u % 2][:, :], ACT.Silu, bias=b1s[:, u:u + 1], scale=ALPHA)
                else:
                    i = e.activation(o, bank[4 + u % 2][:, :], ACT.Relu, bias=cst("m1_b1", u, u + 1))
                i.then_inc(self.ev["sg"], 1)

            def dve_h(self, e, c, u, ahead=True):
                wait(e, self.ev["s2"], (self.base + c) * 2 * E + u + 1)
                wait(e, self.ev["y"], self.before(c, u, 3) if ahead else (self.base + c) * 2 * E)
                e.scalar_tensor_tensor(out=hb[:, (u % 4) * CN:(u % 4 + 1) * CN], in0=vb[:, (u % 2) * CN:(u % 2 + 1) * CN],
                                       scalar=1.0 - LIMIT, in1=s2b[:, (u % 2) * CN:(u % 2 + 1) * CN],
                                       op0=ALU.max, op1=ALU.mult).then_inc(self.hbuf, 1)

            def dve_unit(self, e, c, u, last):
                U, q = (self.base + c) * 2 * E, slice((u % 2) * CN, (u % 2 + 1) * CN)
                cb = bank[2 + u // 2 % 2][:, :]
                if self.glu:
                    wait(e, self.hbuf, self.before(c, u, 1))
                    wait(e, self.ev["h"], U + u + 1)
                    e.tensor_scalar(vb[:, q], bank[6 + u % 2][:, :], b1v[:, u:u + 1], LIMIT + 1.0, ALU.add, ALU.min)
                wait(e, self.ev["sg"], U + u + 1)
                if u % 2 == 0:
                    wait(e, self.ev["cb"], (self.base + c) * E + u // 2 + 1)
                if self.glu:
                    e.scalar_tensor_tensor(out=s2b[:, q], in0=sg[:, q], scalar=SILU_MAX, in1=cb,
                                           op0=ALU.min, op1=ALU.mult).then_inc(self.ev["s2"], 1)
                    if last is not None:
                        self.dve_h(e, *last)
                else:
                    wait(e, self.ev["y"], self.before(c, u, 3))
                    e.tensor_tensor(hb[:, (u % 4) * CN:(u % 4 + 1) * CN], sg[:, q], cb, ALU.mult).then_inc(self.ev["s2"], 1)

            def rotated(self, c, nxt):
                own = [(c, u) for u in range(AHEAD, 2 * E)]
                return own + ([(nxt, u) for u in range(AHEAD)] if nxt is not None else [None] * AHEAD)

            def start(self, which, e):
                if which == "pe":
                    for u in range(AHEAD):
                        if u >= self.early:
                            self.pe_first(e, 0, u)
                        if u % 2 == 0:
                            self.pe_comb(e, 0, u // 2)
                    self.pe_second(e, 0, 0)
                for u in range(AHEAD):
                    if which == "act":
                        self.act_unit(e, 0, u)
                    elif which == "dve":
                        self.dve_unit(e, 0, u, (0, u - 1, False) if u else None)

            def prologue(self, which, e):
                self.early = 2
                for pos in range(16):
                    self.first(which, e, pos)
                    if which == "pe" and pos in (4, 5):
                        self.pe_first(e, 0, pos - 4)

            def pe_both(self, e, c, u):
                self.pe_first(e, c, u)
                if u % 2 == 0:
                    self.pe_comb(e, c, u // 2)

            def pe_chunk(self, e, c, nxt):
                g = self.base + c
                second = [(c, u) for u in range(1, 2 * E)] + [(nxt, 0)]
                for n, at in enumerate(self.rotated(c, nxt)):
                    if at is not None:
                        self.pe_both(e, *at)
                    if self.beside:
                        self.beside("pe", e, n - 0.5)
                    if second[n][0] is not None:
                        self.pe_second(e, *second[n])
                    self.hooks("pe", e, n, c, nxt)
                wait(e, self.ev["ye"], g + 1)
                if nxt is None:
                    self.bank0_free(e)
                for t in range(CT):
                    i = e.transpose(bank[0][:, t * P:t * P + P], yT[:, t * P:t * P + P], cst("ident"))
                i.then_inc(self.ev["yt"], 1)

            def act_chunk(self, e, c, nxt):
                g = self.base + c
                for n, at in enumerate(self.rotated(c, nxt)):
                    if n == 2 * E - 1:
                        wait(e, self.ev["y"], (g + 1) * 2 * E)
                        wait(e, self.ev["yt"], g)
                        e.activation(yT[:, :], bank[1][:, :], ACT.Copy).then_inc(self.ev["ye"], 1)
                    if self.beside:
                        self.beside("act", e, n - 0.5)
                    if at is not None:
                        self.act_unit(e, *at)
                    self.hooks("act", e, n, c, nxt)

            def dve_chunk(self, e, c, nxt):
                g = self.base + c
                last = (c, AHEAD - 1, False)
                for n, at in enumerate(self.rotated(c, nxt)):
                    self.hooks("dve", e, n, c, nxt)
                    if at is not None:
                        self.dve_unit(e, *at, last)
                        last = at
                    if self.beside:
                        self.beside("dve", e, n + 0.5)
                if self.glu and nxt is None:
                    self.dve_h(e, *last)
                wait(e, self.ev["yt"], g + 1)
                e.scalar_tensor_tensor(out=x[:, bass.ds(c * CN, CN)], in0=bank[0][:, :],
                                       scalar=0.5 / ALPHA if self.glu else 0.5, in1=x[:, bass.ds(c * CN, CN)],
                                       op0=ALU.mult, op1=ALU.add).then_inc(self.ev["x"], 1)

            def pool_chunk(self, e, c, nxt):
                for u in range(2 * E):
                    self.hooks("pool", e, u, c, nxt)
                    if self.beside:
                        self.beside("pool", e, u + 0.5)

            def run(self, which, e, start, ahead, bank0_free):
                self.beside, self.bank0_free = None, bank0_free
                start(which, e)
                self.start(which, e)
                chunk = dict(pe=self.pe_chunk, act=self.act_chunk, dve=self.dve_chunk, pool=self.pool_chunk)[which]
                if self is m1a:
                    self.beside = a1.keys
                    chunk(e, 0, 1)
                    self.beside = None
                with e.Fori(1 if self is m1a else 0, NC - 1) as c:
                    chunk(e, c, c + 1)
                self.beside = ahead
                chunk(e, NC - 1, None)

        class Sparse:
            PAIRS = H0 // 2
            STEPS = 2 * PAIRS
            TK = 2 * (2 * ROUNDS - 1)
            SCALE = DH0 ** -0.5

            def __init__(self, name, x_ready):
                self.x_ready = x_ready
                self.ev = events(name, ("st", "mv", "ve", "rstd", "xn", "T", "xT", "q", "qe", "k", "ke", "V", "Ve", "th", "gs", "gp",
                          "gate", "S", "c", "tk", "nm", "e", "mk", "p", "PT", "pT", "PV", "den", "nrm", "aT", "aTe",
                          "ds", "mi", "mx", "o", "x"))

            def dve_norm(self, e, b, p):
                self.x_ready(e, b, p)
                for t in range(2):
                    i = e.bn_stats(stats[:, 6 * t:6 * t + 6], x[:, bass.ds(b * S + t * P, P)])
                i.then_inc(self.ev["st"], 1)
                alone(e, self.ev["st"], b + 1, s_const)
                for t in range(2):
                    i = e.bn_aggr(mv[:, 2 * t:2 * t + 2], stats[:, 6 * t:6 * t + 6])
                i.then_inc(self.ev["mv"], 1)

            def pool_rstd(self, e, b, p):
                alone(e, self.ev["mv"], b + 1, s_const)
                e.tensor_scalar(rstd[:, CT:CT + 2], mv[:, 1:4:2], LN_EPS, None, ALU.add).then_inc(self.ev["ve"], 1)
                wait(e, self.ev["ve"], b + 1)
                e.tensor_tensor(rstd[:, 0:2], rstd[:, CT:CT + 2], mhalf[:, 0:2], ALU.pow).then_inc(self.ev["rstd"], 1)

            def dve_xn(self, e, b, p):
                wait(e, self.ev["rstd"], b + 1)
                wait(e, self.ev["T"], b)
                for t in range(2):
                    i = e.tensor_scalar(xn[:, t * P:t * P + P], x[:, bass.ds(b * S + t * P, P)],
                                        mv[:, 2 * t:2 * t + 1], rstd[:, t:t + 1], ALU.subtract, ALU.mult)
                i.then_inc(self.ev["xn"], 1)

            def pe_T(self, e, b, p):
                wait(e, self.ev["xn"], b + 1)
                wait(e, self.ev["gate"], b)
                for t in range(2):
                    i = e.transpose(bank[0][:, t * P:t * P + P], xn[:, t * P:t * P + P], cst("ident"))
                i.then_inc(self.ev["T"], 1)

            def act_xT(self, e, b, p):
                wait(e, self.ev["T"], b + 1)
                e.activation(axT[:, :], bank[0][:, 0:S], ACT.Copy, accum_out=xsum[:, :]).then_inc(self.ev["xT"], 1)

            def pe_q(self, e, b, p):
                wait(e, self.ev["xT"], b + 1)
                for n in range(2):
                    i = e.matmul(bank[0][:, n * S:n * S + S], cst("a0_wq", n * P, n * P + P), axT[:, :], start=True, stop=True)
                i.then_inc(self.ev["q"], 1)

            def act_qe(self, e, b, p):
                wait(e, self.ev["q"], b + 1)
                for n in range(2):
                    i = e.activation(qT[p][:, n * S:n * S + S], bank[0][:, n * S:n * S + S], ACT.Identity,
                                     bias=cst("a0_bq", n, n + 1))
                i.then_inc(self.ev["qe"], 1)

            def pe_k(self, e, b, p):
                wait(e, self.ev["qe"], b + 1)
                for n in range(2):
                    i = e.matmul(bank[0][:, n * S:n * S + S], cst("a0_wk", n * P, n * P + P), axT[:, :], start=True, stop=True)
                i.then_inc(self.ev["k"], 1)

            def act_ke(self, e, b, p):
                wait(e, self.ev["k"], b + 1)
                for n in range(2):
                    i = e.activation(kT[p][:, n * S:n * S + S], bank[0][:, n * S:n * S + S], ACT.Identity,
                                     bias=cst("a0_bk", n, n + 1))
                i.then_inc(self.ev["ke"], 1)

            def pe_V(self, e, b, p):
                alone(e, self.ev["ke"], b + 1, s_const)
                for t in range(2):
                    e.matmul(bank[0][:, t * P:t * P + P], axT[:, t * P:t * P + P], cst("a0_wv"), start=True, stop=True)
                e.matmul(bank[0][0:64, S:S + 1], cst("a0_wg"), xsum[:, :], start=True, stop=True).then_inc(self.ev["V"], 1)

            def act_th(self, e, b, p):
                wait(e, self.ev["V"], b + 1)
                e.activation(gsm[:, 0:1], bank[0][0:64, S:S + 1], ACT.Tanh, bias=bgh[:, :], scale=0.5 / S).then_inc(self.ev["th"], 1)

            def dve_Ve(self, e, b, p):
                wait(e, self.ev["th"], b + 1)
                wait(e, self.ev["PV"], b * self.STEPS - self.STEPS if not isinstance(b, int) else max(b - 1, 0) * self.STEPS)
                for t in range(2):
                    e.tensor_tensor(V0[p][:, :].rearrange("p (t h d) -> p t h d", t=2, h=H0)[:, t, :, 0:DH0],
                                    bank[0][:, t * P:t * P + P].rearrange("p (h d) -> p h d", h=H0),
                                    cst("a0_bv").rearrange("p (h d) -> p h d", h=H0), ALU.add)
                e.tensor_scalar(gsm[:, 1:2], gsm[:, 0:1], 0.5, 0.5, ALU.mult, ALU.add).then_inc(self.ev["Ve"], 1)

            def pe_gp(self, e, b, p):
                alone(e, self.ev["Ve"], b + 1, s_const)
                e.matmul(bank[0][:, 0:1], cst("a0_wgp", rows=slice(0, 64)), gsm[:, 1:2], start=True, stop=True).then_inc(self.ev["gp"], 1)

            def dve_gate(self, e, b, p):
                wait(e, self.ev["gp"], b + 1)
                g = gate[p]
                e.tensor_scalar(g[:, 0:1], bank[0][:, 0:1], cst("a0_bgp"), None, ALU.add).then_inc(self.ev["gs"], 1)
                wait(e, self.ev["gs"], b + 1)
                e.tensor_scalar(g[:, 1:2], g[:, 0:1], -1.0, 1.0, ALU.mult, ALU.add).then_inc(self.ev["gate"], 1)

            def pe_S(self, e, A, a):
                p, m = a // self.STEPS % 2, a % self.PAIRS
                if a % self.STEPS == 0:
                    wait(e, self.ev["ke"], self.batch(A, a) + 1)
                if not (isinstance(A, int) and A < 2):
                    wait(e, self.ev["c"], A - 1)
                qt = a // self.PAIRS % 2
                for n in range(2):
                    r = slice(32 * m, 32 * m + DH0)
                    i = e.matmul(bank[4 + a % 2][:, n * S:n * S + S], qT[p][r, n * S + qt * P:n * S + qt * P + P],
                                 kT[p][r, n * S:n * S + S], start=True, stop=True)
                i.then_inc(self.ev["S"], 1)

            def act_c(self, e, A, a):
                wait(e, self.ev["S"], A + 1)
                if not (isinstance(A, int) and A < 4):
                    wait(e, self.ev["p"], A - 3)
                e.activation(sS[:, (a % 4) * 2 * S:(a % 4 + 1) * 2 * S], bank[4 + a % 2][:, :], ACT.Copy).then_inc(self.ev["c"], 1)

            def dve_topk(self, e, A, a):
                wait(e, self.ev["c"], A + 1)
                if not (isinstance(A, int) and A < 2):
                    wait(e, self.ev["p"], A - 1)
                ops = []
                for r in range(ROUNDS):
                    for n in range(2):
                        src = sS[:, (a % 4) * 2 * S + n * S:(a % 4) * 2 * S + n * S + S]
                        w = wk[:, n * S:n * S + S]
                        m8 = m8s[:, ((a % 2) * 2 + n) * 8 * ROUNDS + 8 * r:((a % 2) * 2 + n) * 8 * ROUNDS + 8 * r + 8]
                        ops.append(lambda m8=m8, s_=w if r else src: e.max(m8, s_))
                    if r < ROUNDS - 1:
                        for n in range(2):
                            src = sS[:, (a % 4) * 2 * S + n * S:(a % 4) * 2 * S + n * S + S]
                            w = wk[:, n * S:n * S + S]
                            m8 = m8s[:, ((a % 2) * 2 + n) * 8 * ROUNDS + 8 * r:((a % 2) * 2 + n) * 8 * ROUNDS + 8 * r + 8]
                            ops.append(lambda m8=m8, w=w, s_=w if r else src: e.match_replace(w, m8, s_, -3.0e38))
                for n, op in enumerate(ops):
                    if n >= 2:
                        alone(e, self.ev["tk"], A * self.TK + n - 1, s_const)
                    elif not (isinstance(A, int) and A == 0):
                        alone(e, self.ev["tk"], A * self.TK, s_const)
                    op().then_inc(self.ev["tk"], 1)

            def pool_sel(self, e, A, a):
                m = m8s[:, (a % 2) * 16 * ROUNDS:(a % 2 + 1) * 16 * ROUNDS].rearrange("p (n k) -> p n k", n=2)
                alone(e, self.ev["tk"], A * self.TK + 2, s_const)
                if not (isinstance(A, int) and A < 2):
                    alone(e, self.ev["e"], A - 1, s_const)
                e.tensor_scalar(negm[:, (a % 2) * 2:(a % 2) * 2 + 2], m[:, :, 0], -self.SCALE, None, ALU.mult).then_inc(self.ev["nm"], 1)
                if isinstance(A, int) and A == B * self.STEPS - 1:
                    return
                self.select(e, A, a)

            def select(self, e, A, a):
                m = m8s[:, (a % 2) * 16 * ROUNDS:(a % 2 + 1) * 16 * ROUNDS].rearrange("p (n k) -> p n k", n=2)
                alone(e, self.ev["tk"], A * self.TK + self.TK, s_const)
                alone(e, self.ev["p"], A, s_const)
                for n in range(2):
                    i = e.tensor_scalar(msk[:, n * S:n * S + S], sS[:, (a % 4) * 2 * S + n * S:(a % 4) * 2 * S + n * S + S],
                                        m[:, n, TOPK - 1:TOPK], None, ALU.is_ge)
                i.then_inc(self.ev["mk"], 1)
                wait(e, self.ev["mk"], A + 1)
                wait(e, self.ev["e"], A + 1)
                if not (isinstance(A, int) and A < 2):
                    wait(e, self.ev["PT"], A - 1)
                q = slice((a % 2) * 2 * S, (a % 2 + 1) * 2 * S)
                e.tensor_tensor(pS[:, q], msk[:, :], eS[:, q], ALU.mult).then_inc(self.ev["p"], 1)

            def act_e(self, e, A, a):
                wait(e, self.ev["nm"], A + 1)
                if not (isinstance(A, int) and A < 2):
                    wait(e, self.ev["p"], A - 1)
                for n in range(2):
                    i = e.activation(eS[:, ((a % 2) * 2 + n) * S:((a % 2) * 2 + n + 1) * S],
                                     sS[:, (a % 4) * 2 * S + n * S:(a % 4) * 2 * S + n * S + S], ACT.Exp,
                                     bias=negm[:, (a % 2) * 2 + n:(a % 2) * 2 + n + 1], scale=self.SCALE)
                i.then_inc(self.ev["e"], 1)

            def pe_PT(self, e, A, a):
                wait(e, self.ev["p"], A + 1)
                if not (isinstance(A, int) and A < 2):
                    wait(e, self.ev["pT"], A - 1)
                for n in range(4):
                    i = e.transpose(bank[6 + a % 2][:, n * P:n * P + P], pS[:, (a % 2) * 2 * S + n * P:(a % 2) * 2 * S + n * P + P],
                                    cst("ident"))
                i.then_inc(self.ev["PT"], 1)

            def act_pT(self, e, A, a):
                wait(e, self.ev["PT"], A + 1)
                if not (isinstance(A, int) and A < 2):
                    wait(e, self.ev["PV"], A - 1)
                e.activation(pT[:, (a % 2) * 2 * S:(a % 2 + 1) * 2 * S], bank[6 + a % 2][:, :], ACT.Copy).then_inc(self.ev["pT"], 1)

            def pe_PV(self, e, A, a):
                p, g, m = a // self.STEPS % 2, a // self.PAIRS % 2, a % self.PAIRS
                W = DH0 + 1
                if m == 0:
                    if a % self.STEPS == 0:
                        wait(e, self.ev["Ve"], self.batch(A, a) + 1)
                    if not (isinstance(A, int) and A < 2 * self.PAIRS):
                        wait(e, self.ev["nrm"], self.batch(A, a) * 2 + g - 1)
                wait(e, self.ev["pT"], A + 1)
                for n in range(2):
                    h = m + self.PAIRS * n
                    for t in range(2):
                        i = e.matmul(bank[2 + g][:, h * W:h * W + W], pT[:, ((a % 2) * 4 + n * 2 + t) * P:((a % 2) * 4 + n * 2 + t + 1) * P],
                                     V0[p][:, (t * H0 + h) * W:(t * H0 + h + 1) * W], start=t == 0, stop=t == 1)
                i.then_inc(self.ev["PV"], 1)

            def dve_nrm(self, e, b, g):
                W = DH0 + 1
                o = bank[2 + g][:, 0:H0 * W].rearrange("p (h d) -> p h d", h=H0)
                wait(e, self.ev["PV"], b * self.STEPS + (g + 1) * self.PAIRS)
                if not (isinstance(b, int) and b == 0):
                    wait(e, self.ev["aT"], b)
                e.reciprocal(rden[:, :], o[:, :, DH0]).then_inc(self.ev["den"], 1)
                wait(e, self.ev["den"], 2 * b + g + 1)
                e.tensor_tensor(attn[:, g * P:g * P + P].rearrange("p (h d) -> p h d", h=H0), o[:, :, 0:DH0],
                                rden[:, :].unsqueeze(2).to_broadcast([P, H0, DH0]), ALU.mult).then_inc(self.ev["nrm"], 1)

            def pe_aT(self, e, b, p):
                wait(e, self.ev["nrm"], 2 * b + 2)
                wait(e, self.ev["x"], b)
                for t in range(2):
                    i = e.transpose(bank[1][:, t * P:t * P + P], attn[:, t * P:t * P + P], cst("ident"))
                i.then_inc(self.ev["aT"], 1)

            def act_aT(self, e, b, p):
                wait(e, self.ev["aT"], b + 1)
                e.activation(aT[:, :], bank[1][:, 0:S], ACT.Copy).then_inc(self.ev["aTe"], 1)

            def pe_ds(self, e, b, p):
                wait(e, self.ev["aTe"], b + 1)
                e.matmul(bank[1][:, 0:S], cst("a0_wd"), aT[:, :], start=True, stop=True).then_inc(self.ev["ds"], 1)

            def dve_mix(self, e, b, p):
                wait(e, self.ev["ds"], b + 1)
                wait(e, self.ev["o"], b)
                e.tensor_scalar(mixt[:, :], bank[1][:, 0:S], cst("a0_bd"), gate[p][:, 0:1], ALU.add, ALU.mult).then_inc(self.ev["mi"], 1)
                wait(e, self.ev["mi"], b + 1)
                e.scalar_tensor_tensor(out=mix[:, :], in0=aT[:, :], scalar=gate[p][:, 1:2], in1=mixt[:, :],
                                       op0=ALU.mult, op1=ALU.add).then_inc(self.ev["mx"], 1)

            def pe_o(self, e, b, p):
                wait(e, self.ev["mx"], b + 1)
                for t in range(2):
                    e.matmul(bank[1][:, t * P:t * P + P], mix[:, t * P:t * P + P], cst("a0_wo"), start=True, stop=False)
                    i = e.matmul(bank[1][:, t * P:t * P + P], cst("ones", rows=slice(0, 1)), cst("a0_bo", rows=slice(0, 1)),
                                 start=False, stop=True)
                i.then_inc(self.ev["o"], 1)

            def dve_x(self, e, b, p):
                wait(e, self.ev["o"], b + 1)
                xb = x[:, bass.ds(b * S, S)]
                e.tensor_tensor(xb, bank[1][:, 0:S], xb, ALU.add).then_inc(self.ev["x"], 1)

            def batch(self, A, a):
                return A // self.STEPS if isinstance(A, int) else self.b_of(A, a)

            TASKS = dict(
                dve=((0, dve_norm, 1), (1, dve_xn, 1), (6, dve_Ve, 1), (6, dve_mix, -1), (7, dve_x, -1)),
                pool=((0, pool_rstd, 1),),
                pe=((1, pe_T, 1), (2, pe_q, 1), (3, pe_k, 1), (4, pe_V, 1), (6, pe_gp, 1),
                    (3, pe_aT, -1), (4, pe_ds, -1)),
                act=((1, act_xT, 1), (2, act_qe, 1), (3, act_ke, 1), (4, act_th, 1), (3, act_aT, -1)))

            def tasks(self, which, e, b, a, first, final):
                r, p = a % self.STEPS, a // self.STEPS % 2
                for at, task, to in self.TASKS[which]:
                    if at == r and not (to > 0 and final) and not (to < 0 and first):
                        task(self, e, b + to, (p + 1) % 2)

            def step(self, which, e, b, a, first=False, final=False):
                r = a % self.STEPS
                A = b * self.STEPS + r
                self.b_of = lambda A_, a_: b + (a_ // self.STEPS - a // self.STEPS)

                def at(n):
                    if first and r + n < 0 or final and r + n >= self.STEPS:
                        return None
                    return A + n, a + n
                def call(f, n):
                    if at(n) is not None:
                        f(e, *at(n))
                if which == "pe":
                    call(self.pe_S, 2)
                    if r == 6 and not first:
                        self.pe_o(e, b - 1, 0)
                    call(self.pe_PT, -1)
                    call(self.pe_PV, -2)
                elif which == "act":
                    call(self.act_e, 0)
                    call(self.act_c, 2)
                    call(self.act_pT, -1)
                elif which == "pool":
                    self.tasks(which, e, b, a, first, final)
                    call(self.pool_sel, 0)
                else:
                    if r == 0 and not first:
                        self.dve_gate(e, b, a // self.STEPS % 2)
                    if r == 3 and not first:
                        self.dve_nrm(e, b - 1, 1)
                    if r == 7:
                        self.dve_nrm(e, b, 0)
                    self.tasks(which, e, b, a, first, final)
                    call(self.dve_topk, 0)
                if which in ("pe", "act"):
                    self.tasks(which, e, b, a, first, final)
                if final:
                    self.ahead(which, e, 2 * r)
                    self.ahead(which, e, 2 * r + 1)

            def first(self, which, e, pos):
                if pos == 2:
                    e.wait_ge(s_const, 3)
                for r, task, to in self.TASKS[which]:
                    if to > 0 and pos == 2 * r + 1:
                        task(self, e, 0, 0)
                if which == "dve" and pos == 15:
                    self.dve_gate(e, 0, 0)

            def run(self, which, e, start, ahead, bank0_free):
                start(which, e)
                self.ahead = ahead
                for A in range(2):
                    if which == "pe":
                        self.pe_S(e, A, A)
                    if which == "act":
                        self.act_c(e, A, A)
                N_ = self.STEPS
                for r in range(N_):
                    self.step(which, e, 0, r, first=True)
                with e.Fori(0, (B - 2) // 2) as i:
                    for a in range(N_, 3 * N_):
                        self.step(which, e, 2 * i + a // N_, a)
                for r in range(N_):
                    self.step(which, e, B - 1, N_ + r, final=True)
                if which == "pe":
                    A = B * N_
                    self.pe_PT(e, A - 1, 2 * N_ - 1)
                    for n in (2, 1):
                        self.pe_PV(e, A - n, 2 * N_ - n)
                    self.pe_aT(e, B - 1, 1), self.pe_ds(e, B - 1, 1), self.pe_o(e, B - 1, 1)
                elif which == "act":
                    self.act_pT(e, B * N_ - 1, 2 * N_ - 1)
                    self.act_aT(e, B - 1, 1)
                elif which == "dve":
                    self.select(e, B * N_ - 1, 2 * N_ - 1)
                    self.dve_nrm(e, B - 1, 1), self.dve_mix(e, B - 1, 1), self.dve_x(e, B - 1, 1)

        class Unit:
            def __init__(self, c, g):
                self.c, self.g = c, g
                if c is None:
                    self.n, self.w, self.N, self.src, self.to = g, "k", S, cst("a1_src"), kn
                else:
                    self.n, self.w, self.N = 2 * c + 2 + g, "q", CN
                    self.src, self.to = xnT[:, bass.ds(c * CN, CN)], qn

        def each_block(task, first, apart=1):
            return [(first + apart * f, task, f) for f in range(FB // 2)]

        class Cross:
            G = FB // 2
            base = 0

            def __init__(self, name, x_ready):
                self.x_ready = x_ready
                self.ev = events(name, ("st", "mv", "ve", "rstd", "xn", "T", "xT", "q", "rr", "mn", "ex", "eq", "sq", "ss", "sse", "ri", "sp", "rT",
                          "rp", "rb", "qn", "S", "e", "PV", "de", "den", "nrm", "O", "z", "z2", "st2", "mv2", "ve2",
                          "rstd2", "x", "V", "Ve", "keep"))

            def dve_norm(self, e, c):
                self.x_ready(e, c)
                for t in range(CT):
                    i = e.bn_stats(stats[:, 6 * t:6 * t + 6], x[:, bass.ds(c * CN + t * P, P)])
                i.then_inc(self.ev["st"], 1)
                alone(e, self.ev["st"], c + 1, s_const)
                for t in range(CT):
                    i = e.bn_aggr(mv[:, 2 * t:2 * t + 2], stats[:, 6 * t:6 * t + 6])
                i.then_inc(self.ev["mv"], 1)

            def pool_rstd(self, e, c):
                alone(e, self.ev["mv"], c + 1, s_const)
                e.tensor_scalar(rstd[:, CT:2 * CT], mv[:, 1:2 * CT:2], LN_EPS, None, ALU.add).then_inc(self.ev["ve"], 1)
                wait(e, self.ev["ve"], c + 1)
                e.tensor_tensor(rstd[:, 0:CT], rstd[:, CT:2 * CT], mhalf[:, 0:CT], ALU.pow).then_inc(self.ev["rstd"], 1)

            def dve_xn(self, e, c):
                wait(e, self.ev["rstd"], c + 1)
                wait(e, self.ev["T"], c)
                wait(e, self.ev["keep"], c)
                for t in range(CT):
                    i = e.tensor_scalar(xn[:, t * P:t * P + P], x[:, bass.ds(c * CN + t * P, P)],
                                        mv[:, 2 * t:2 * t + 1], rstd[:, t:t + 1], ALU.subtract, ALU.mult)
                i.then_inc(self.ev["xn"], 1)

            def pe_T(self, e, c):
                wait(e, self.ev["xn"], c + 1)
                wait(e, self.ev["xT"], c)
                for t in range(CT):
                    i = e.transpose(bank[0][:, t * P:t * P + P], xn[:, t * P:t * P + P], cst("ident"))
                i.then_inc(self.ev["T"], 1)

            def act_xT(self, e, c):
                wait(e, self.ev["T"], c + 1)
                e.activation(xnT[:, bass.ds(c * CN, CN)], bank[0][:, :], ACT.Copy).then_inc(self.ev["xT"], 1)

            def to(self, u, f):
                f += self.G * u.g
                return u.to[:, f * u.N:f * u.N + u.N]

            def pe_q(self, e, u, f):
                if u.w == "q" and u.g == 0 and f == 0:
                    wait(e, self.ev["xT"], u.c + 1)
                wait(e, self.ev["mn"], self.G * u.n + f)
                if f == 0:
                    wait(e, self.ev["qn"], self.G * u.n)
                f += self.G * u.g
                e.matmul(bank[6][:, 0:u.N], cst("a1_w" + u.w, f * P, f * P + P), u.src, start=True, stop=True).then_inc(self.ev["q"], 1)

            def act_relu(self, e, u, f):
                F = f + self.G * u.g
                wait(e, self.ev["q"], self.G * u.n + f + 1)
                wait(e, self.ev["eq"], self.G * u.n + max(f - 1, 0))
                e.activation(rrb[:, (f % 2) * CN:(f % 2) * CN + u.N], bank[6][:, 0:u.N], ACT.Relu,
                             bias=cst("a1_b" + u.w, F, F + 1)).then_inc(self.ev["rr"], 1)

            def dve_min(self, e, u, f):
                F = f + self.G * u.g
                wait(e, self.ev["rr"], self.G * u.n + f + 1)
                wait(e, self.ev["eq"], self.G * u.n + max(f - 1, 0))
                e.tensor_scalar(exb[:, (f % 2) * CN:(f % 2) * CN + u.N], bank[6][:, 0:u.N], cst("a1_b" + u.w, F, F + 1),
                                0.0, ALU.add, ALU.min).then_inc(self.ev["mn"], 1)

            def act_ex(self, e, u, f):
                wait(e, self.ev["mn"], self.G * u.n + f + 1)
                b = slice((f % 2) * CN, (f % 2) * CN + u.N)
                e.activation(exb[:, b], exb[:, b], ACT.Exp).then_inc(self.ev["ex"], 1)

            def dve_elu(self, e, u, f):
                b = slice((f % 2) * CN, (f % 2) * CN + u.N)
                if u.w == "q" and f == 0:
                    v = 2 * H1 * u.c - H1 + H1 * u.g
                    wait(e, self.ev["S"], max(v, 0) if isinstance(v, int) else v)
                wait(e, self.ev["ex"], self.G * u.n + f + 1)
                e.scalar_tensor_tensor(out=self.to(u, f), in0=exb[:, b], scalar=-1.0, in1=rrb[:, b],
                                       op0=ALU.add, op1=ALU.add).then_inc(self.ev["eq"], 1)

            def act_sq(self, e, u, f):
                wait(e, self.ev["eq"], self.G * u.n + f + 1)
                wait(e, self.ev["ss"], self.G * u.n + max(f - 1, 0))
                e.activation(sqb[:, (f % 2) * CN:(f % 2) * CN + u.N], self.to(u, f), ACT.Square).then_inc(self.ev["sq"], 1)

            def pe_ss(self, e, u, f):
                wait(e, self.ev["sq"], self.G * u.n + f + 1)
                for t in range(u.N // P):
                    q = (f % 2) * CN + t * P
                    i = e.matmul(bank[7][:, t * FB + 2 * f:t * FB + 2 * f + 2], sqb[:, q:q + P], cst("a1_blk"), start=True, stop=True)
                i.then_inc(self.ev["ss"], 1)

            def act_sse(self, e, u):
                wait(e, self.ev["ss"], self.G * u.n + self.G)
                wait(e, self.ev["ri"], u.n)
                e.activation(ssb[:, 0:u.N // P * FB], bank[7][:, 0:u.N // P * FB], ACT.Copy).then_inc(self.ev["sse"], 1)

            def pool_ri(self, e, u):
                n = u.N // P * FB
                wait(e, self.ev["sse"], u.n + 1)
                wait(e, self.ev["sp"], u.n * 5)
                e.tensor_tensor(rib[:, 0:n], ssb[:, 0:n], mhalf[:, 0:n], ALU.pow).then_inc(self.ev["ri"], 1)

            def dve_split(self, e, u):
                ch = Chain(e, self.ev["sp"], u.n * 5, s_const)
                n = u.N // P
                part = rp3[:, 0:n * PARTS * FB].rearrange("p (t k h) -> p t k h", k=PARTS, h=FB)
                r = rib[:, 0:n * FB].rearrange("p (t h) -> p t h", h=FB)
                wait(e, self.ev["ri"], u.n + 1)
                wait(e, self.ev["rT"], u.n)
                for k in range(PARTS):
                    ch(e.tensor_copy(part[:, :, k, :], r))
                    if k < PARTS - 1:
                        ch(e.tensor_tensor(r, r, part[:, :, k, :], ALU.subtract))

            def pe_rT(self, e, u):
                wait(e, self.ev["sp"], u.n * 5 + 5)
                to = bank[7][:, :].bitcast(BF16)
                for t in range(u.N // P):
                    i = e.transpose(to[0:PARTS * FB, t * P:t * P + P], rp3[:, t * PARTS * FB:(t + 1) * PARTS * FB], cst("identb"))
                i.then_inc(self.ev["rT"], 1)

            def act_rT(self, e, u):
                wait(e, self.ev["rT"], u.n + 1)
                wait(e, self.ev["rb"], self.G * u.n)
                e.activation(rp[:, 0:u.N], bank[7][:, :].bitcast(BF16)[0:PARTS * FB, 0:u.N], ACT.Copy).then_inc(self.ev["rp"], 1)

            def pe_rb(self, e, u, f):
                wait(e, self.ev["rp"], u.n + 1)
                wait(e, self.ev["qn"], self.G * u.n + max(f - 1, 0))
                e.matmul(bank[6 + f % 2][:, 0:u.N], cst("blkT", f * P, f * P + P, slice(0, PARTS * FB)), rp[:, 0:u.N],
                         start=True, stop=True).then_inc(self.ev["rb"], 1)

            def dve_qn(self, e, u, f):
                wait(e, self.ev["rb"], self.G * u.n + f + 1)
                e.tensor_tensor(self.to(u, f), bank[6 + f % 2][:, 0:u.N], self.to(u, f), ALU.mult).then_inc(self.ev["qn"], 1)

            def pe_V(self, e, n):
                t, half = n // 2, n % 2
                wait(e, self.ev["Ve"], max(n - 1, 0))
                e.matmul(bank[6 + half][:, :], cst("a1_val", t * P, t * P + P), cst("a1_wv", half * CN, half * CN + CN),
                         start=True, stop=True).then_inc(self.ev["V"], 1)

            def dve_V(self, e, n):
                t, half = n // 2, n % 2
                wait(e, self.ev["V"], n + 1)
                v = VO[:, :].rearrange("p (t f s d) -> p t f s d", t=2, f=FB, s=3)[:, t, 4 * half:4 * half + 4, 0:3:2, :]
                e.tensor_tensor(v, bank[6 + half][:, :].rearrange("p (f s d) -> p f s d", s=2, d=DH1),
                                cst("a1_bv", half * CN, half * CN + CN).rearrange("p (f s d) -> p f s d", s=2, d=DH1),
                                ALU.add).then_inc(self.ev["Ve"], 1)

            def pe_S(self, e, c, h):
                r, f = slice(64 * (h % 2), 64 * (h % 2) + 64), h // 2
                if h % 2 == 0:
                    wait(e, self.ev["qn"], FB * (c + 1) + f + 1)
                for t in range(2):
                    wait(e, self.ev["e"], 2 * (c * H1 + h) + t - 1 if h else 2 * c * H1)
                    e.matmul(bank[2 + t][:, :], kn[r, f * S + t * P:f * S + t * P + P], qn[r, f * CN:f * CN + CN],
                             start=True, stop=True).then_inc(self.ev["S"], 1)

            def act_e(self, e, c, h):
                for t in range(2):
                    wait(e, self.ev["S"], 2 * (c * H1 + h) + t + 1)
                    wait(e, self.ev["PV"], c * H1 + h - 1)
                    e.activation(AT[:, ((h % 2) * 2 + t) * CN:((h % 2) * 2 + t + 1) * CN], bank[2 + t][:, :], ACT.Exp,
                                 scale=DH1 ** -0.5).then_inc(self.ev["e"], 1)

            def pe_PV(self, e, c, h):
                wait(e, self.ev["de"], c * H1 + h - 1)
                if h == 0:
                    wait(e, self.ev["Ve"], 4)
                wait(e, self.ev["e"], 2 * (c * H1 + h) + 2)
                for t in range(2):
                    v = (t * FB + h // 2) * 3 * DH1 + (h % 2) * DH1
                    i = e.matmul(bank[4 + h % 2][:, :], VO[:, v:v + P], AT[:, ((h % 2) * 2 + t) * CN:((h % 2) * 2 + t + 1) * CN],
                                 start=t == 0, stop=t == 1)
                i.then_inc(self.ev["PV"], 1)

            def act_cp(self, e, c, h):
                f = h // 2
                own, other = (slice(0, 64), slice(64, P)) if h % 2 == 0 else (slice(64, P), slice(0, 64))
                q = slice((f % 2) * CN, (f % 2 + 1) * CN)
                wait(e, self.ev["PV"], c * H1 + h + 1)
                wait(e, self.ev["O"], FB * c + f - 1)
                e.activation(denb[own, q], bank[4 + h % 2][other, :], ACT.Copy)
                e.activation(ctxb[own, q], bank[4 + h % 2][own, :], ACT.Copy).then_inc(self.ev["de"], 1)

            def dve_rec(self, e, c, f):
                q = slice((f % 2) * CN, (f % 2 + 1) * CN)
                wait(e, self.ev["de"], c * H1 + 2 * f + 2)
                e.reciprocal(denb[:, q], denb[:, q]).then_inc(self.ev["den"], 1)

            def dve_nrm(self, e, c, f):
                q = slice((f % 2) * CN, (f % 2 + 1) * CN)
                wait(e, self.ev["den"], FB * c + f + 1)
                e.tensor_tensor(ctxb[:, q], ctxb[:, q], denb[:, q], ALU.mult).then_inc(self.ev["nrm"], 1)

            def pe_O(self, e, c, f):
                if f == 0:
                    wait(e, self.ev["z"], c)
                    e.matmul(bank[1][:, :], cst("ones", rows=slice(0, 1)), cst("a1_bo", rows=slice(0, 1)), start=True, stop=False)
                wait(e, self.ev["nrm"], FB * c + f + 1)
                for q in range(CT):
                    i = e.matmul(bank[1][:, q * P:q * P + P], ctxb[:, (f % 2) * CN + q * P:(f % 2) * CN + q * P + P],
                                 cst("a1_wo", f * P, f * P + P), start=False, stop=f == FB - 1 and q == CT - 1)
                i.then_inc(self.ev["O"], 1)

            def dve_tail(self, e, c):
                wait(e, self.ev["O"], FB * c + FB)
                wait(e, self.ev["keep"], c + 1)
                wait(e, self.ev["x"], c)
                e.tensor_tensor(z[:, :], bank[1][:, :], tkeep[:, :], ALU.add).then_inc(self.ev["z"], 1)
                alone(e, self.ev["z"], c + 1, s_const)
                for t in range(CT):
                    i = e.bn_stats(stats2[:, 6 * t:6 * t + 6], z[:, t * P:t * P + P])
                i.then_inc(self.ev["st2"], 1)
                alone(e, self.ev["st2"], c + 1, s_const)
                for t in range(CT):
                    i = e.bn_aggr(mv2[:, 2 * t:2 * t + 2], stats2[:, 6 * t:6 * t + 6])
                i.then_inc(self.ev["mv2"], 1)

            def pool_end(self, e, c):
                zz = z[:, :].rearrange("p (q d) -> p q d", q=CT)

                def row(name):
                    return cst(name).unsqueeze(1).to_broadcast([P, CT, D])
                ch = Chain(e, self.ev["z2"], c * 4, s_const)
                alone(e, self.ev["rstd2"], c + 1, s_const)
                for t in range(CT):
                    i = e.tensor_scalar(z[:, t * P:t * P + P], z[:, t * P:t * P + P], mv2[:, 2 * t:2 * t + 1], rstd2[:, t:t + 1],
                                        ALU.subtract, ALU.mult)
                ch(i)
                ch(e.tensor_tensor(zz, zz, row("a1_g"), ALU.mult))
                ch(e.tensor_tensor(zz, zz, row("a1_b"), ALU.add))
                xc = x[:, bass.ds(c * CN, CN)]
                ch(e.tensor_tensor(xc, xc, z[:, :], ALU.add))
                e.sem_inc(self.ev["x"], 1)

            def pool_keep(self, e, c):
                alone(e, self.ev["xn"], c + 1, s_const)
                alone(e, self.ev["z"], c, s_const)
                e.tensor_copy(tkeep[:, :], xn[:, :]).then_inc(self.ev["keep"], 1)

            def pool_tail(self, e, c):
                alone(e, self.ev["mv2"], c + 1, s_const)
                e.tensor_scalar(rstd2[:, CT:2 * CT], mv2[:, 1:2 * CT:2], LN_EPS2, None, ALU.add).then_inc(self.ev["ve2"], 1)
                wait(e, self.ev["ve2"], c + 1)
                e.tensor_tensor(rstd2[:, 0:CT], rstd2[:, CT:2 * CT], mhalf[:, 0:CT], ALU.pow).then_inc(self.ev["rstd2"], 1)

            UNIT = dict(
                pe=each_block(pe_q, 0) + [(2, pe_ss, 0), (2, pe_ss, 1), (3, pe_ss, 2), (4, pe_ss, 3), (6, pe_rT)] + each_block(pe_rb, 7, 0),
                act=[(7, act_rT), (5, act_sse)] + each_block(act_ex, 1) + each_block(act_relu, 0) + each_block(act_sq, 1),
                dve=[(6, dve_split)] + each_block(dve_elu, 1) + each_block(dve_min, 0) + each_block(dve_qn, 7, 0),
                pool=[(5, pool_ri)])
            NORM = dict(pe=[(5, pe_T)], act=[(6, act_xT)], dve=[(3, dve_norm), (4, dve_xn)], pool=[(3, pool_rstd)])

            def unit(self, which, e, u, k, of=slice(None)):
                for at, task, *f in [t for t in self.UNIT[which] if t[0] == k][of]:
                    task(self, e, u, *f)

            def norm(self, which, e, c, k):
                for at, task in self.NORM[which]:
                    if at == k:
                        task(self, e, c)

            def step(self, which, e, c, h, nxt, last=None):
                half, k = h // 8, h % 8
                u = Unit(nxt if half else c, 1 - half) if half == 0 or nxt is not None else None

                def beside(of=slice(None)):
                    if u is not None:
                        self.unit(which, e, u, k, of)
                if which == "pe":
                    if k < 7:
                        self.pe_S(e, c, h + 1)
                        if k < 4:
                            beside(slice(0, 1))
                        self.pe_PV(e, c, h)
                        if h == 1 and last is not None:
                            self.pe_O(e, last, FB - 1)
                        beside(slice(1 if k < 4 else 0, None))
                    else:
                        self.pe_PV(e, c, h)
                        beside(slice(0, 2))
                        if half == 0:
                            self.pe_S(e, c, h + 1)
                        elif nxt is not None:
                            self.pe_S(e, nxt, 0)
                        beside(slice(2, None))
                    if h % 2 == 0 and h > 2:
                        self.pe_O(e, c, h // 2 - 2)
                    elif h == 0 and last is not None:
                        self.pe_O(e, last, FB - 2)
                elif which == "act":
                    self.act_e(e, c, h)
                    if k == 5:
                        beside()
                    if h > 0:
                        self.act_cp(e, c, h - 1)
                    elif last is not None:
                        self.act_cp(e, last, H1 - 1)
                    if k != 5:
                        beside()
                elif which == "dve":
                    n = 1 if 0 < k < 7 else 0
                    pair = (c, h // 2 - 1) if h > 0 else (last, FB - 1)
                    beside(slice(0, n))
                    if h % 2 == 0 and pair[0] is not None:
                        self.dve_rec(e, *pair)
                    beside(slice(n, None))
                    if h % 2 == 0 and pair[0] is not None:
                        self.dve_nrm(e, *pair)
                    if h == 2 and last is not None:
                        self.dve_tail(e, last)
                else:
                    beside()
                if half == 0 and nxt is not None:
                    self.norm(which, e, nxt, k)
                if half == 1 and nxt is None:
                    self.ahead(which, e, 2 * k)
                    self.ahead(which, e, 2 * k + 1)

            def chunk(self, which, e, c, nxt):
                if which == "pool":
                    self.pool_keep(e, c)
                for h in range(3, H1):
                    self.step(which, e, c, h, nxt)
                if nxt is not None:
                    for h in range(3):
                        self.step(which, e, nxt, h, None, last=c)
                elif which == "pe":
                    self.pe_O(e, c, FB - 2)
                    self.pe_O(e, c, FB - 1)
                elif which == "act":
                    self.act_cp(e, c, H1 - 1)
                elif which == "dve":
                    self.dve_rec(e, c, FB - 1)
                    self.dve_nrm(e, c, FB - 1)
                    self.dve_tail(e, c)
                if which == "pool":
                    self.pool_tail(e, c)
                    self.pool_end(e, c)

            def keys(self, which, e, pos):
                for n in (0, 1) if pos == 0 else (2, 3) if pos == 1 else ():
                    if which == "pe":
                        self.pe_V(e, n)
                    elif which == "dve":
                        self.dve_V(e, n)
                if pos == 1 and which in ("pe", "act"):
                    wait(e, self.ev["Ve"], 4)
                for g in range(2):
                    for k in range(8):
                        if pos == 1.5 + 7 * g + min(k, 6.5):
                            self.unit(which, e, Unit(None, g), k)

            def first(self, which, e, pos):
                if pos == 0 and which == "dve":
                    wait(e, ms["T"], m1a.base + NC)
                for k in range(8):
                    if pos == k - 3:
                        self.norm(which, e, 0, k)
                for k in range(8):
                    if pos == 3 + 1.5 * k:
                        self.unit(which, e, Unit(0, 0), k)

            def run(self, which, e, start, ahead, bank0_free):
                start(which, e)
                self.ahead = ahead
                if which == "pe":
                    self.pe_S(e, 0, 0)
                for h in range(3):
                    self.step(which, e, 0, h, None)
                with e.Fori(0, NC - 1) as c:
                    self.chunk(which, e, c, c + 1)
                self.chunk(which, e, NC - 1, None)

        kn = sb("kn", FB * S)
        qn = sb("qn", FB * CN)
        exb = sb("exb", 2 * CN)
        rrb, sqb = vb, s2b
        ssb = sb("ssb", CT * FB)
        rib = sb("rib", CT * FB)
        rp3 = sb("rp3", CT * PARTS * FB, BF16)
        rp = sb("rp", CN, BF16, PARTS * FB)
        VO = sb("VO", 2 * FB * 3 * DH1)
        AT = hb
        sS = sb("sS", 4 * 2 * S)
        ctxb, denb = sS[:, 0:2 * CN], sS[:, 2 * CN:4 * CN]
        tkeep = sb("tkeep", CN)
        z = yT
        stats2 = sb("stats2", CT * 6)
        mv2 = sb("mv2", CT * 2)
        rstd2 = sb("rstd2", 2 * CT)

        axT = sb("axT", S)
        xsum = sb("xsum", 1)
        qT = [sb(f"qT{n}", 2 * S) for n in range(2)]
        kT = [sb(f"kT{n}", 2 * S) for n in range(2)]
        V0 = [sb(f"V0{n}", 2 * H0 * (DH0 + 1)) for n in range(2)]
        gsm = sb("gsm", 2, F32, 64)
        bgh = sb("bgh", 1, F32, 64)
        gate = [sb(f"gate{n}", 2) for n in range(2)]
        wk, msk = sg[:, 0:2 * S], vb[:, 0:2 * S]
        m8s = sb("m8s", 4 * 8 * ROUNDS)
        negm = sb("negm", 4)
        eS, pS, pT = hb[:, 0:4 * S], hb[:, 4 * S:8 * S], qn[:, 0:4 * S]
        rden = sb("rden", H0)
        attn, aT, mixt, mix = (s2b[:, n * S:n * S + S] for n in range(4))

        SILU_MAX = float(ALPHA * LIMIT / (1.0 + np.exp(-ALPHA * LIMIT)))
        b1s = sb("b1s", 2 * E)
        b1v = sb("b1v", 2 * E)
        b2p = {k: sb("b2p_" + k, PARTS * D, BF16, PARTS * E) for k in ("m0", "m1")}
        b2r = sb("b2r", D)

        def setup_dve(e):
            ch = Chain(e, s_setup, 0, s_const)
            e.memset(mhalf[:, :], -0.5).then_inc(s_const, 1)
            e.wait_ge(s_ld[0], 16)
            b1 = cst("m0_b1").rearrange("p (u s) -> p u s", s=2)
            e.tensor_scalar(b1s[:, :], b1[:, :, 0], ALPHA, None, ALU.mult)
            ch(e.tensor_scalar(b1v[:, :], b1[:, :, 1], 1.0, None, ALU.add))
            exact_b2(ch, e, "m0", ALPHA)
            e.sem_inc(s_const, 1)

        def exact_b2(ch, e, k, f):
            r = slice(0, PARTS * E)
            p = b2p[k]
            ch(e.tensor_scalar(b2r[r, :], cst(k + "_b2", rows=r), f, None, ALU.mult))
            for n in range(PARTS):
                ch(e.tensor_copy(p[:, n * D:n * D + D], b2r[r, :]))
                if n < PARTS - 1:
                    ch(e.tensor_tensor(b2r[r, :], b2r[r, :], p[:, n * D:n * D + D], ALU.subtract))

        def setup_late(e):
            ch = Chain(e, s_setup, 7, s_const)
            for n in (2, 3, 4):
                e.wait_ge(s_ld[n], 16)
            exact_b2(ch, e, "m1", 1.0)
            for v in V0:
                e.memset(v[:, DH0::DH0 + 1], 1.0)
            e.memset(VO[:, :].rearrange("p (f s d) -> p f s d", s=3, d=DH1)[:, :, 1, :], 1.0)
            ch(e.tensor_scalar(bgh[:, :], cst("a0_bg", rows=slice(0, 64)), 0.5, None, ALU.mult))
            e.sem_inc(s_const, 1)

        def after(stage):
            return lambda e, c: wait(e, stage.ev["x"], stage.base + c + 1)

        ms = events("moe", ("st", "mv", "ve", "rstd", "xn", "T", "xnT", "LT", "lgT", "LG", "dif", "th", "c3",
                                           "CT", "cT", "h", "cb", "sg", "s2", "hb", "y", "ye", "yt", "x", "dv"))

        def a0_done(which, e):
            wait(e, a0.ev["gate"] if which == "pe" else a0.ev["T"], B)

        def a1_done(which, e):
            if which == "pe":
                wait(e, a1.ev["xT"], NC)
            else:
                wait(e, a1.ev["keep"], NC)
                wait(e, a1.ev["T"], NC)

        def a0_x_ready(e, b, p):
            if isinstance(b, int) and b == 0:
                wait(e, m0a.ev["x"], m0a.base + 1)
                wait(e, ms["T"], m0a.base + NC)
            else:
                wait(e, m0a.ev["x"], m0a.base + NC)

        m0a = Moe("swiglu", lambda e, c: e.wait_ge(s_x0[int(not isinstance(c, int) or c > 0)], 16), ms, 0)
        a0 = Sparse("a0", a0_x_ready)
        m0b = Moe("swiglu", lambda e, c: wait(e, a0.ev["x"], 2 if isinstance(c, int) and c == 0 else B), ms, 1, a0_done)
        m1a = Moe("relu", after(m0b), ms, 2)
        a1 = Cross("a1", after(m1a))
        m1b = Moe("relu", after(a1), ms, 3, a1_done)
        stages = [m0a, a0, m0b, m1a, a1, m1b]
        last = stages[-1]

        def run_all(which, e):
            for n, stage in enumerate(stages):
                def start(which, e, n=n):
                    if n == 0:
                        stage.prologue(which, e)
                    elif stages[n - 1] is a0:
                        wait(e, a0.ev["x"], B)
                    elif stages[n - 1] is a1:
                        wait(e, a1.ev["z"], NC)
                    elif stage is m1a:
                        wait(e, ms["hb"], stage.base * 2 * E)
                    elif which != "pool":
                        wait(e, stages[n - 1].ev["x"], stages[n - 1].base + NC)

                def ahead(which, e, pos, n=n):
                    if n == 0 and which == "dve" and pos == 0:
                        setup_late(e)
                    if n + 1 < len(stages):
                        stages[n + 1].first(which, e, pos)

                def bank0_free(e, n=n):
                    if n + 1 < len(stages) and stages[n + 1] is a0:
                        wait(e, a0.ev["gate"], 1)
                    elif n + 1 < len(stages) and stages[n + 1] is a1:
                        wait(e, a1.ev["xT"], 1)
                stage.run(which, e, start, ahead, bank0_free)

        block = ctx.enter_context(nc.Block())
        xv = x_in.rearrange("b (t p) d -> p (b t) d", p=P)

        @block.sync
        def _(e):
            e.dma_start(pk[0][:, :], packed[0]).then_inc(s_ld[0], 16)

            def load_x(n, a, b):
                e.dma_start(x[:, a * D:b * D].rearrange("p (t d) -> p t d", d=D), xv[:, a:b, :]).then_inc(s_x0[n], 16)
            load_x(0, 0, CT)
            e.dma_start(pkb[:, :], packed_b).then_inc(s_ld[5], 16)
            for n in range(4):
                e.dma_start(pk[1][:, n * (N1 // 4):(n + 1) * (N1 // 4)], packed[1][:, n * (N1 // 4):(n + 1) * (N1 // 4)]).then_inc(s_w[n], 16)
                if n == 0:
                    load_x(1, CT, NT)
            for n in (2, 3, 4):
                e.dma_start(pk[n][:, :], packed[n]).then_inc(s_ld[n], 16)
            e.wait_ge(s_start, 1)
            outv = out.rearrange("b (t p) d -> p (b t) d", p=P)
            for c in range(NC):
                wait(e, last.ev["x"], last.base + c + 1)
                e.dma_start(outv[:, c * CT:(c + 1) * CT, :],
                            x[:, c * CN:(c + 1) * CN].rearrange("p (t d) -> p t d", d=D)).then_inc(s_out, 16)
            e.wait_ge(s_out, 16 * NC)

        @block.gpsimd
        def _(e):
            for v in counted:
                e.sem_inc(v, 1)
            e.sem_inc(s_start, 1)
            e.wait_ge(s_const, 1)
            run_all("pool", e)

        @block.scalar
        def _(e):
            e.wait_ge(s_start, 1)
            e.wait_ge(s_const, 2)
            run_all("act", e)

        @block.vector
        def _(e):
            e.wait_ge(s_start, 1)
            setup_dve(e)
            run_all("dve", e)

        @block.tensor
        def _(e):
            e.wait_ge(s_start, 1)
            e.wait_ge(s_ld[0], 16)
            e.wait_ge(s_ld[5], 16)
            e.wait_ge(s_const, 2)
            run_all("pe", e)


def pack(names, n, parts):
    a = np.zeros((P, n), np.float32)
    for k, (lo, hi) in names.items():
        v = parts[k]
        a[:v.shape[0], lo:hi] = v.reshape(v.shape[0], hi - lo)
    return a


def kernel(**inputs):
    import ml_dtypes
    import concourse.bacc as bacc
    from concourse.bass_utils import run_bass_kernel_spmd as run

    i = {k: np.asarray(v) for k, v in inputs.items()}
    a0, f0, a1, f1 = "L0_attn_", "L0_ffn_", "L1_attn_", "L1_ffn_"

    def rows(v):
        return np.broadcast_to(v.reshape(1, -1), (P, v.size))

    def cols(v, n=P):
        return v.reshape(-1, n).T

    def heads(w):
        o = np.zeros((w.shape[1], 8, 32), np.float32)
        o[:, :, :DH0] = w.T.reshape(w.shape[1], 8, DH0)
        return o

    iota = np.broadcast_to(np.arange(E, dtype=np.float32), (P, 2 * CT, E))
    w1 = i[f0 + "dense_1_w"].reshape(E, 2, P, 2, D)
    wd = np.zeros((2, 64, 2, 64), np.float32)
    wd[0, :, 0], wd[1, :, 1] = i[a0 + "Wd"].T, i[a0 + "Wd"].T
    blk = np.zeros((2, 64, 2), np.float32)
    blk[0, :, 0] = blk[1, :, 1] = 1
    parts = {
        "ident": np.eye(P, dtype=np.float32), "iota": iota,
        "m0_gw": i[f0 + "gate_w"], "m0_gb": np.zeros((E, 1), np.float32),
        "m0_b1": i[f0 + "dense_1_b"].reshape(E, 2, P, 2).transpose(2, 0, 1, 3),
        "m0_b2": np.concatenate([i[f0 + "dense_2_b"]] * PARTS),
        "a0_wq": heads(i[a0 + "Wq"]), "a0_wk": heads(i[a0 + "Wk"]),
        "a0_wv": i[a0 + "Wv"].T, "a0_wd": wd.reshape(P, P), "a0_wo": i[a0 + "Wo"].T,
        "a0_wg": i[a0 + "Wg"].T, "a0_wgp": i[a0 + "Wgp"].T,
        "a0_bq": heads(i[a0 + "bq"].reshape(-1, 1)).reshape(2, P).T, "a0_bk": heads(i[a0 + "bk"].reshape(-1, 1)).reshape(2, P).T,
        "a0_bv": rows(i[a0 + "bv"]), "a0_bd": np.concatenate([i[a0 + "bd"]] * 2).reshape(P, 1),
        "a0_bg": i[a0 + "bg"].reshape(64, 1), "a0_bgp": i[a0 + "bgp"].reshape(P, 1),
        "a0_bo": rows(i[a0 + "bo"]), "ones": np.ones((P, P), np.float32),
        "m1_gw": i[f1 + "Wg"].T, "m1_gb": i[f1 + "bg"].reshape(E, 1),
        "m1_b1": cols(i[f1 + "b1"]), "m1_b2": np.concatenate([i[f1 + "b2"]] * PARTS),
        "m1_w1": i[f1 + "W1"].transpose(2, 0, 1),
        "m1_w2": i[f1 + "W2"].reshape(E, D, 2, P).transpose(3, 0, 2, 1),
        "a1_wq": i[a1 + "Wq"], "a1_wk": i[a1 + "Wk"], "a1_wv": i[a1 + "Wv"],
        "a1_wo": i[a1 + "Wo"].reshape(FB, P, D).transpose(1, 0, 2),
        "a1_bq": cols(i[a1 + "bq"]), "a1_bk": cols(i[a1 + "bk"]),
        "a1_src": i[a1 + "source_embedding"].T, "a1_val": i[a1 + "value_embedding"].T,
        "a1_bv": rows(i[a1 + "bv"]), "a1_g": rows(i[a1 + "ln_g"]), "a1_b": rows(i[a1 + "ln_b"]),
        "a1_bo": rows(np.concatenate([i[a1 + "bo"]] * CT)), "a1_blk": blk.reshape(P, -1),
    }
    w1 = w1.transpose(4, 0, 1, 3, 2)
    w2 = i[f0 + "dense_2_w"].reshape(E, D, 2, P).transpose(3, 0, 2, 1)
    for n in range(4):
        parts |= {f"m0_w1{n}": w1[:, 2 * n:2 * n + 2], f"m0_w2{n}": w2[:, 2 * n:2 * n + 2]}
    sel = np.zeros((PARTS, E, E, P), np.float32)
    for e_ in range(E):
        sel[:, e_, e_] = 1
    blkT = np.zeros((PARTS, FB, FB // 2, 2, 64), np.float32)
    for h in range(FB):
        blkT[:, h, h // 2, h % 2] = 1
    parts |= {"identb": parts["ident"], "sel": sel.reshape(PARTS * E, -1), "blkT": blkT.reshape(PARTS * FB, -1)}

    nc = bacc.Bacc("TRN2", target_bir_lowering=False, num_devices=1)
    arrays = {}

    def arg(name, a):
        arrays[name] = np.ascontiguousarray(a)
        return nc.dram_tensor(name, a.shape, mybir.dt.from_np(a.dtype), kind="ExternalInput").ap()

    packed = [arg(f"packed{n}", pack(names, size, parts))
              for n, (names, size) in enumerate(((PK0, N0), (PK1, N1), (PK2, N2), (PK3, N3), (PK4, N4)))]
    packed_b = arg("packed_b", pack(PKB, NB, parts).astype(ml_dtypes.bfloat16))
    x_in = arg("x_in", i[a0 + "x"])
    out = nc.dram_tensor("out", (B, S, D), F32, kind="ExternalOutput").ap()
    build(nc, packed, packed_b, x_in, out)
    r = run(nc, [arrays], core_ids=[0])
    return r.results[0]["out"]
```
